# Optimizing a Trainium2 kernel written in Bass

```python
import numpy as np
import jax
import jax.numpy as jnp

def _softmax(x, axis=-1):
    return jax.nn.softmax(x, axis=axis)

def _gelu(x):
    return jax.nn.gelu(x, approximate=True)

def _silu(x):
    return jax.nn.silu(x)

def _sigmoid(x):
    return jax.nn.sigmoid(x)

def _layernorm(x, axis=-1, eps=1e-05):
    m = jnp.mean(x, axis=axis, keepdims=True)
    v = jnp.var(x, axis=axis, keepdims=True)
    return (x - m) / jnp.sqrt(v + eps)

def _scatter_add(tgt, idx, src, axis=0):
    return tgt.at[idx].add(src)

def _segment_sum(src, seg, n):
    return jax.ops.segment_sum(src, seg, n)
kernel_name = 'mk_early_fusion_d2_tok_img256_r4_a708ea'

def setup_inputs(seed: int=0):
    np.random.seed(seed)
    _w = jnp.asarray

    def _rec_inputs():
        import jax
        import jax.numpy as jnp
        _rk = jax.random.key(seed)
        x = -0.0003702 + 0.999946 * jax.random.normal(jax.random.fold_in(_rk, 1), (128, 1, 128, 128), jnp.float32)
        txt = 0.281643 + 0.58738 * jax.random.normal(jax.random.fold_in(_rk, 2), (128, 128, 64), jnp.float32)
        return (x, txt)
    x, txt = _rec_inputs()

    def _L0_tok_setup():
        import jax, jax.numpy as jnp
        import numpy as np
        PH, PW = (64, 25)
        SH, SW = (64, 12)

        def _unfold(x, ph, pw, sh, sw):
            B, C, H, W = x.shape
            nh = (H - ph) // sh + 1
            nw = (W - pw) // sw + 1
            rows = jnp.arange(nh)[:, None] * sh + jnp.arange(ph)[None, :]
            cols = jnp.arange(nw)[:, None] * sw + jnp.arange(pw)[None, :]
            p = x[:, :, rows, :]
            p = p[:, :, :, :, cols]
            p = jnp.transpose(p, (0, 2, 4, 1, 3, 5))
            return p.reshape(B, nh * nw, C * ph * pw)
        key = jax.random.key(seed)
        kx, kw = jax.random.split(key, 2)
        x = jax.random.normal(kx, (64, 1, 64, 1000), dtype=jnp.float32)
        in_dim = 1 * PH * PW
        weight = jax.random.normal(kw, (in_dim, 64), dtype=jnp.float32) / np.sqrt(in_dim).astype(np.float32)
        bias = jnp.zeros((64,), dtype=jnp.float32)
        return {'x': x, 'weight': weight, 'bias': bias}
    _L0_tok_all = _L0_tok_setup()
    _L0_tok_in = {k: v for k, v in _L0_tok_all.items() if k in ('weight', 'bias')}
    del _L0_tok_all

    def _L0_attn_setup():
        import jax, jax.numpy as jnp
        import numpy as np
        EPS = 1e-09

        def _glorot(key, shape):
            fan_in, fan_out = (shape[-2], shape[-1])
            std = (2.0 / (fan_in + fan_out)) ** 0.5
            return jax.random.normal(key, shape, dtype=jnp.float32) * std

        def _reference_tuple_inner(x, Wks, Wqs, Wvs, Wo):
            keys = jnp.einsum('bsd,hdk->hbsk', x, Wks)
            queries = jnp.einsum('bsd,hdk->hbsk', x, Wqs)
            values = jnp.einsum('bsd,hde->hbse', x, Wvs)
            keys = jax.nn.elu(keys) + 1.0
            queries = jax.nn.elu(queries) + 1.0
            att = jnp.einsum('hbsk,hbtk->hbst', queries, keys)
            S = att.shape[-1]
            causal = jnp.tril(jnp.ones((S, S), dtype=att.dtype))
            att = att * causal
            att = att / (jnp.sum(att, axis=-1, keepdims=True) + EPS)
            kv = jnp.einsum('hbsk,hbsd->hbsdk', keys, values)
            kv_cum = jnp.cumsum(kv, axis=2)
            numerator = jnp.einsum('hbsdk,hbsk->hbsd', kv_cum, queries)
            denominator = jnp.einsum('hbsk,hbsk->hbs', jnp.cumsum(keys, axis=2), queries)
            node = numerator / (denominator[..., None] + EPS)
            out = jnp.einsum('hbsd,hde->bse', node, Wo)
            return (out, att)
        key = jax.random.key(seed)
        kx, k1, k2, k3, k4 = jax.random.split(key, 5)
        B, S, D = (2, 256, 64)
        H, K = (8, 32)
        return {'x': jax.random.normal(kx, (B, S, D), dtype=jnp.float32), 'Wks': _glorot(k1, (H, D, K)), 'Wqs': _glorot(k2, (H, D, K)), 'Wvs': _glorot(k3, (H, D, D)), 'Wo': _glorot(k4, (H, D, D))}
    _L0_attn_all = _L0_attn_setup()
    _L0_attn_in = {k: v for k, v in _L0_attn_all.items() if k in ('Wks', 'Wqs', 'Wvs', 'Wo')}
    del _L0_attn_all

    def _L0_ffn_setup():
        import jax, jax.numpy as jnp
        import numpy as np
        E, D, H, TOP_K = (6, 64, 64, 2)
        ROUTER_H = D // 2
        key = jax.random.key(seed)
        ks = jax.random.split(key, 12)
        s = 1.0 / np.sqrt(D)
        sh = 1.0 / np.sqrt(H)
        sr = 1.0 / np.sqrt(ROUTER_H)
        return {'features': jax.random.normal(ks[0], (8, 1024, D), dtype=jnp.float32), 'router_w1': jax.random.uniform(ks[1], (D, ROUTER_H), jnp.float32, -s, s), 'router_b1': jnp.zeros((ROUTER_H,), jnp.float32), 'router_w2': jax.random.uniform(ks[2], (ROUTER_H, E), jnp.float32, -sr, sr), 'router_b2': jnp.zeros((E,), jnp.float32), 'expert_w1': jax.random.uniform(ks[3], (E, D, H), jnp.float32, -s, s), 'expert_b1': jnp.zeros((E, H), jnp.float32), 'expert_w2': jax.random.uniform(ks[4], (E, H, H), jnp.float32, -sh, sh), 'expert_b2': jnp.zeros((E, H), jnp.float32), 'expert_w3': jax.random.uniform(ks[5], (E, H, D), jnp.float32, -sh, sh), 'expert_b3': jnp.zeros((E, D), jnp.float32)}
    _L0_ffn_all = _L0_ffn_setup()
    _L0_ffn_in = {k: v for k, v in _L0_ffn_all.items() if k in ('router_w1', 'router_b1', 'router_w2', 'router_b2', 'expert_w1', 'expert_b1', 'expert_w2', 'expert_b2', 'expert_w3', 'expert_b3')}
    del _L0_ffn_all

    def _L1_attn_setup():
        import jax, jax.numpy as jnp
        import numpy as np
        B, T, C = (16, 512, 64)
        TT = T
        LAYER_ID, N_LAYER = (3, 6)
        key = jax.random.key(seed)
        ks = jax.random.split(key, 6)
        ratio_0_to_1 = LAYER_ID / (N_LAYER - 1)
        ratio_1_to_almost0 = 1.0 - LAYER_ID / N_LAYER
        h = np.arange(TT, dtype=np.float32)
        decay_speed = -5.0 + 8.0 * (h / (TT - 1)) ** (0.7 + 1.3 * ratio_0_to_1)
        curve = -(TT - 1 - h)
        time_w = jnp.asarray(np.exp(np.clip(curve * decay_speed, -30.0, 0.0)), dtype=jnp.float32)
        i = np.arange(C, dtype=np.float32) / C
        time_mix_k = jnp.asarray((i ** ratio_1_to_almost0).reshape(1, 1, C), dtype=jnp.float32)
        time_mix_v = jnp.asarray((i ** ratio_1_to_almost0 + 0.3 * ratio_0_to_1).reshape(1, 1, C), dtype=jnp.float32)
        time_mix_r = jnp.asarray((i ** (0.5 * ratio_1_to_almost0)).reshape(1, 1, C), dtype=jnp.float32)
        x = jax.random.normal(ks[0], (B, T, C), dtype=jnp.float32)
        scale = 0.02
        Wk = scale * jax.random.normal(ks[1], (C, C), dtype=jnp.float32)
        Wv = scale * jax.random.normal(ks[2], (C, C), dtype=jnp.float32)
        Wr = scale * jax.random.normal(ks[3], (C, C), dtype=jnp.float32)
        Wo = scale * jax.random.normal(ks[4], (C, C), dtype=jnp.float32)
        return {'x': x, 'time_w': time_w, 'time_mix_k': time_mix_k, 'time_mix_v': time_mix_v, 'time_mix_r': time_mix_r, 'Wk': Wk, 'Wv': Wv, 'Wr': Wr, 'Wo': Wo}
    _L1_attn_all = _L1_attn_setup()
    _L1_attn_in = {k: v for k, v in _L1_attn_all.items() if k in ('time_w', 'time_mix_k', 'time_mix_v', 'time_mix_r', 'Wk', 'Wv', 'Wr', 'Wo')}
    del _L1_attn_all

    def _L1_ffn_setup():
        import jax, jax.numpy as jnp
        import numpy as np
        B, T, C = (64, 96, 64)
        NH, NKV = (4, 2)
        HD = C // NH
        NREP = NH // NKV
        NE, TOPK = (8, 2)
        HID = int(8 / 3 * C)
        EPS_RMS = 1e-06

        def _rope_tables(t_len):
            inv_freq = 1.0 / 10000.0 ** (np.arange(0, HD, 2, dtype=np.float32) / HD)
            t = np.arange(t_len, dtype=np.float32)
            freqs = np.outer(t, inv_freq)
            emb = np.concatenate([freqs, freqs], axis=-1)
            return (jnp.asarray(np.cos(emb)), jnp.asarray(np.sin(emb)))

        def _rotate_half(x):
            h = x.shape[-1] // 2
            return jnp.concatenate([-x[..., h:], x[..., :h]], axis=-1)

        def _rmsnorm(v, w):
            return v * jax.lax.rsqrt(jnp.mean(v * v, axis=-1, keepdims=True) + EPS_RMS) * w
        key = jax.random.key(seed)
        ks = jax.random.split(key, 10)
        s = lambda k, shape: jax.random.normal(k, shape, jnp.float32) * 0.02
        return {'x': jax.random.normal(ks[0], (B, T, C), jnp.float32), 'ln1_w': jnp.ones((C,), jnp.float32), 'ln2_w': jnp.ones((C,), jnp.float32), 'wq': s(ks[1], (NH * HD, C)), 'wk': s(ks[2], (NKV * HD, C)), 'wv': s(ks[3], (NKV * HD, C)), 'wo': s(ks[4], (C, C)), 'router_w': s(ks[5], (NE, C)), 'w1': s(ks[6], (NE, HID, C)), 'w2': s(ks[7], (NE, C, HID)), 'w3': s(ks[8], (NE, HID, C))}
    _L1_ffn_all = _L1_ffn_setup()
    _L1_ffn_in = {k: v for k, v in _L1_ffn_all.items() if k in ('ln1_w', 'ln2_w', 'wq', 'wk', 'wv', 'wo', 'router_w', 'w1', 'w2', 'w3')}
    del _L1_ffn_all
    return {'x': x, 'txt': txt, 'L0_tok_weight': _L0_tok_in['weight'], 'L0_tok_bias': _L0_tok_in['bias'], 'L0_attn_Wks': _L0_attn_in['Wks'], 'L0_attn_Wqs': _L0_attn_in['Wqs'], 'L0_attn_Wvs': _L0_attn_in['Wvs'], 'L0_attn_Wo': _L0_attn_in['Wo'], 'L0_ffn_router_w1': _L0_ffn_in['router_w1'], 'L0_ffn_router_b1': _L0_ffn_in['router_b1'], 'L0_ffn_router_w2': _L0_ffn_in['router_w2'], 'L0_ffn_router_b2': _L0_ffn_in['router_b2'], 'L0_ffn_expert_w1': _L0_ffn_in['expert_w1'], 'L0_ffn_expert_b1': _L0_ffn_in['expert_b1'], 'L0_ffn_expert_w2': _L0_ffn_in['expert_w2'], 'L0_ffn_expert_b2': _L0_ffn_in['expert_b2'], 'L0_ffn_expert_w3': _L0_ffn_in['expert_w3'], 'L0_ffn_expert_b3': _L0_ffn_in['expert_b3'], 'L1_attn_time_w': _L1_attn_in['time_w'], 'L1_attn_time_mix_k': _L1_attn_in['time_mix_k'], 'L1_attn_time_mix_v': _L1_attn_in['time_mix_v'], 'L1_attn_time_mix_r': _L1_attn_in['time_mix_r'], 'L1_attn_Wk': _L1_attn_in['Wk'], 'L1_attn_Wv': _L1_attn_in['Wv'], 'L1_attn_Wr': _L1_attn_in['Wr'], 'L1_attn_Wo': _L1_attn_in['Wo'], 'L1_ffn_ln1_w': _L1_ffn_in['ln1_w'], 'L1_ffn_ln2_w': _L1_ffn_in['ln2_w'], 'L1_ffn_wq': _L1_ffn_in['wq'], 'L1_ffn_wk': _L1_ffn_in['wk'], 'L1_ffn_wv': _L1_ffn_in['wv'], 'L1_ffn_wo': _L1_ffn_in['wo'], 'L1_ffn_router_w': _L1_ffn_in['router_w'], 'L1_ffn_w1': _L1_ffn_in['w1'], 'L1_ffn_w2': _L1_ffn_in['w2'], 'L1_ffn_w3': _L1_ffn_in['w3']}

def reference(x, txt, L0_tok_weight, L0_tok_bias, L0_attn_Wks, L0_attn_Wqs, L0_attn_Wvs, L0_attn_Wo, L0_ffn_router_w1, L0_ffn_router_b1, L0_ffn_router_w2, L0_ffn_router_b2, L0_ffn_expert_w1, L0_ffn_expert_b1, L0_ffn_expert_w2, L0_ffn_expert_b2, L0_ffn_expert_w3, L0_ffn_expert_b3, L1_attn_time_w, L1_attn_time_mix_k, L1_attn_time_mix_v, L1_attn_time_mix_r, L1_attn_Wk, L1_attn_Wv, L1_attn_Wr, L1_attn_Wo, L1_ffn_ln1_w, L1_ffn_ln2_w, L1_ffn_wq, L1_ffn_wk, L1_ffn_wv, L1_ffn_wo, L1_ffn_router_w, L1_ffn_w1, L1_ffn_w2, L1_ffn_w3):
    import jax
    import jax.numpy as jnp

    def _L0_tok_ref(x, weight, bias):
        import jax, jax.numpy as jnp
        import numpy as np
        PH, PW = (64, 25)
        SH, SW = (64, 12)

        def _unfold(x, ph, pw, sh, sw):
            B, C, H, W = x.shape
            nh = (H - ph) // sh + 1
            nw = (W - pw) // sw + 1
            rows = jnp.arange(nh)[:, None] * sh + jnp.arange(ph)[None, :]
            cols = jnp.arange(nw)[:, None] * sw + jnp.arange(pw)[None, :]
            p = x[:, :, rows, :]
            p = p[:, :, :, :, cols]
            p = jnp.transpose(p, (0, 2, 4, 1, 3, 5))
            return p.reshape(B, nh * nw, C * ph * pw)
        p = _unfold(x, PH, PW, SH, SW)
        return jax.nn.gelu(jnp.einsum('bnk,kd->bnd', p, weight) + bias, approximate=False)

    def _L0_attn_ref(x, Wks, Wqs, Wvs, Wo):
        import jax, jax.numpy as jnp
        import numpy as np
        EPS = 1e-09

        def _glorot(key, shape):
            fan_in, fan_out = (shape[-2], shape[-1])
            std = (2.0 / (fan_in + fan_out)) ** 0.5
            return jax.random.normal(key, shape, dtype=jnp.float32) * std

        def _reference_tuple_inner(x, Wks, Wqs, Wvs, Wo):
            keys = jnp.einsum('bsd,hdk->hbsk', x, Wks)
            queries = jnp.einsum('bsd,hdk->hbsk', x, Wqs)
            values = jnp.einsum('bsd,hde->hbse', x, Wvs)
            keys = jax.nn.elu(keys) + 1.0
            queries = jax.nn.elu(queries) + 1.0
            att = jnp.einsum('hbsk,hbtk->hbst', queries, keys)
            S = att.shape[-1]
            causal = jnp.tril(jnp.ones((S, S), dtype=att.dtype))
            att = att * causal
            att = att / (jnp.sum(att, axis=-1, keepdims=True) + EPS)
            kv = jnp.einsum('hbsk,hbsd->hbsdk', keys, values)
            kv_cum = jnp.cumsum(kv, axis=2)
            numerator = jnp.einsum('hbsdk,hbsk->hbsd', kv_cum, queries)
            denominator = jnp.einsum('hbsk,hbsk->hbs', jnp.cumsum(keys, axis=2), queries)
            node = numerator / (denominator[..., None] + EPS)
            out = jnp.einsum('hbsd,hde->bse', node, Wo)
            return (out, att)
        return _reference_tuple_inner(x, Wks, Wqs, Wvs, Wo)[0]

    def _L0_ffn_ref(features, router_w1, router_b1, router_w2, router_b2, expert_w1, expert_b1, expert_w2, expert_b2, expert_w3, expert_b3):
        import jax, jax.numpy as jnp
        import numpy as np
        E, D, H, TOP_K = (6, 64, 64, 2)
        ROUTER_H = D // 2
        rh = jax.nn.relu(features @ router_w1 + router_b1)
        expert_logits = jax.nn.softmax(rh @ router_w2 + router_b2, axis=-1)
        top_w, top_i = jax.lax.top_k(expert_logits, TOP_K)
        routing_weights = jax.nn.softmax(top_w, axis=-1)
        h1 = jax.nn.relu(jnp.einsum('bsd,edh->bseh', features, expert_w1) + expert_b1)
        h2 = jax.nn.relu(jnp.einsum('bseh,ehf->bsef', h1, expert_w2) + expert_b2)
        expert_out = jnp.einsum('bsef,efo->bseo', h2, expert_w3) + expert_b3
        sel = jnp.take_along_axis(expert_out, top_i[:, :, :, None], axis=2)
        combined = jnp.sum(sel * routing_weights[..., None], axis=2)
        return combined

    def _L1_attn_ref(x, time_w, time_mix_k, time_mix_v, time_mix_r, Wk, Wv, Wr, Wo):
        import jax, jax.numpy as jnp
        import numpy as np
        B, T, C = (16, 512, 64)
        TT = T
        LAYER_ID, N_LAYER = (3, 6)
        Bx, Tx, Cx = x.shape
        maxlen = time_w.shape[0]
        xx = jnp.pad(x, ((0, 0), (1, 0), (0, 0)))[:, :-1]
        xk = x * time_mix_k + xx * (1.0 - time_mix_k)
        xv = x * time_mix_v + xx * (1.0 - time_mix_v)
        xr = x * time_mix_r + xx * (1.0 - time_mix_r)
        k = jnp.exp(jnp.clip(xk @ Wk, -60.0, 30.0))
        v = xv @ Wv
        r = xr @ Wr
        sum_k = jnp.cumsum(k, axis=1)
        kv = k * v
        t_idx = jnp.arange(Tx)
        d = t_idx[:, None] - t_idx[None, :]
        W = jnp.where(d >= 0, time_w[jnp.clip(maxlen - 1 - d, 0, maxlen - 1)], 0.0)
        wkv = jnp.einsum('tu,buc->btc', W, kv)
        rwkv = jax.nn.sigmoid(r) * wkv / sum_k
        return rwkv @ Wo

    def _L1_ffn_ref(x, ln1_w, ln2_w, wq, wk, wv, wo, router_w, w1, w2, w3):
        import jax, jax.numpy as jnp
        import numpy as np
        B, T, C = (64, 96, 64)
        NH, NKV = (4, 2)
        HD = C // NH
        NREP = NH // NKV
        NE, TOPK = (8, 2)
        HID = int(8 / 3 * C)
        EPS_RMS = 1e-06

        def _rope_tables(t_len):
            inv_freq = 1.0 / 10000.0 ** (np.arange(0, HD, 2, dtype=np.float32) / HD)
            t = np.arange(t_len, dtype=np.float32)
            freqs = np.outer(t, inv_freq)
            emb = np.concatenate([freqs, freqs], axis=-1)
            return (jnp.asarray(np.cos(emb)), jnp.asarray(np.sin(emb)))

        def _rotate_half(x):
            h = x.shape[-1] // 2
            return jnp.concatenate([-x[..., h:], x[..., :h]], axis=-1)

        def _rmsnorm(v, w):
            return v * jax.lax.rsqrt(jnp.mean(v * v, axis=-1, keepdims=True) + EPS_RMS) * w
        Bx, Tx, Cx = x.shape
        h = _rmsnorm(x, ln1_w)
        q = (h @ wq.T).reshape(Bx, Tx, NH, HD).transpose(0, 2, 1, 3)
        k = (h @ wk.T).reshape(Bx, Tx, NKV, HD).transpose(0, 2, 1, 3)
        v = (h @ wv.T).reshape(Bx, Tx, NKV, HD).transpose(0, 2, 1, 3)
        cos, sin = _rope_tables(Tx)
        cos, sin = (cos[None, None], sin[None, None])
        q = q * cos + _rotate_half(q) * sin
        k = k * cos + _rotate_half(k) * sin
        k = jnp.repeat(k, NREP, axis=1)
        v = jnp.repeat(v, NREP, axis=1)
        scores = jnp.einsum('bhtd,bhsd->bhts', q, k) / jnp.sqrt(jnp.float32(HD))
        causal = jnp.tril(jnp.ones((Tx, Tx), dtype=bool))
        scores = jnp.where(causal[None, None], scores, jnp.float32(-1e+30))
        att = jax.nn.softmax(scores, axis=-1)
        y = jnp.einsum('bhts,bhsd->bhtd', att, v).transpose(0, 2, 1, 3).reshape(Bx, Tx, Cx)
        x = x + y @ wo.T
        flat = _rmsnorm(x, ln2_w).reshape(-1, Cx)
        probs = jax.nn.softmax(flat @ router_w.T, axis=-1)
        tp, ti = jax.lax.top_k(probs, TOPK)
        tp = tp / (jnp.sum(tp, axis=-1, keepdims=True) + 1e-09)
        weights = jnp.sum(tp[..., None] * jax.nn.one_hot(ti, NE, dtype=flat.dtype), axis=1)
        out = jnp.zeros_like(flat)
        for e in range(NE):
            hh = jax.nn.silu(flat @ w1[e].T) * (flat @ w3[e].T)
            out = out + weights[:, e:e + 1] * (hh @ w2[e].T)
        return x + out.reshape(Bx, Tx, Cx)
    h = _L0_tok_ref(x, L0_tok_weight, L0_tok_bias)
    h = jnp.concatenate([h, txt], axis=1)
    h = h + _L0_attn_ref(_layernorm(h, axis=-1), L0_attn_Wks, L0_attn_Wqs, L0_attn_Wvs, L0_attn_Wo)
    h = h + _L0_ffn_ref(_layernorm(h, axis=-1), L0_ffn_router_w1, L0_ffn_router_b1, L0_ffn_router_w2, L0_ffn_router_b2, L0_ffn_expert_w1, L0_ffn_expert_b1, L0_ffn_expert_w2, L0_ffn_expert_b2, L0_ffn_expert_w3, L0_ffn_expert_b3)
    h = h + _L1_attn_ref(_layernorm(h, axis=-1), L1_attn_time_w, L1_attn_time_mix_k, L1_attn_time_mix_v, L1_attn_time_mix_r, L1_attn_Wk, L1_attn_Wv, L1_attn_Wr, L1_attn_Wo)
    h = h + _L1_ffn_ref(_layernorm(h, axis=-1), L1_ffn_ln1_w, L1_ffn_ln2_w, L1_ffn_wq, L1_ffn_wk, L1_ffn_wv, L1_ffn_wo, L1_ffn_router_w, L1_ffn_w1, L1_ffn_w2, L1_ffn_w3)
    return h

_drawn_inputs = setup_inputs


def setup_inputs(seed=0):
    import zlib

    import numpy as np

    out = dict(_drawn_inputs(seed))
    spreads = {'L0_tok_bias': (0.0, 0.1),
     'L0_ffn_router_b1': (0.0, 0.1),
     'L0_ffn_router_b2': (0.0, 0.1),
     'L0_ffn_expert_b1': (0.0, 0.532),
     'L0_ffn_expert_b2': (0.0, 0.1),
     'L0_ffn_expert_b3': (0.0, 0.1),
     'L1_ffn_ln1_w': (1.0, 0.6),
     'L1_ffn_ln2_w': (1.0, 0.6)}
    factors = {'L1_attn_time_w': 8.0,
     'L1_attn_time_mix_k': 8.0,
     'L1_attn_time_mix_v': 8.0,
     'L1_attn_time_mix_r': 8.0,
     'L1_attn_Wk': 8.0,
     'L1_attn_Wv': 8.0,
     'L1_attn_Wr': 8.0,
     'L1_attn_Wo': 8.0,
     'L1_ffn_wq': 8.0,
     'L1_ffn_wk': 8.0,
     'L1_ffn_wv': 7.217,
     'L1_ffn_wo': 6.69,
     'L1_ffn_router_w': 8.0,
     'L1_ffn_w1': 8.0,
     'L1_ffn_w2': 8.0,
     'L1_ffn_w3': 8.0}
    for name, (base, spread) in spreads.items():
        noise = np.random.default_rng([zlib.crc32(name.encode()), seed]).standard_normal(out[name].shape)
        drawn = base * np.exp(spread * noise) if base else spread * noise
        out[name] = jnp.asarray(drawn.astype(out[name].dtype))
    for name, factor in factors.items():
        out[name] = (out[name] * factor).astype(out[name].dtype)
    return out
```

```python
from contextlib import ExitStack

import numpy as np

import concourse.bass as bass
from concourse import mybir

F32 = mybir.dt.float32
F32R = mybir.dt.float32r
BF16 = mybir.dt.bfloat16
ALU = mybir.AluOpType
ACT = mybir.ActivationFunctionType
AX = mybir.AxisListType
EXP_LN = "natural_log_exp_and_others"

HEAD = 2
D = 64
IMG = 128
PH, PW, SW = 64, 25, 12
NH, NW = (IMG - PH) // PH + 1, (IMG - PW) // SW + 1
TOK = NH * NW
TXT = 128
T = TOK + TXT
HT = T // 2
T2 = 2 * T
REM = T - 128
LN_EPS, RMS_EPS, ATT_EPS = 1e-5, 1e-6, 1e-9
H0, K0 = 8, 32
E0, EH0, RH0 = 6, 64, 32
HQ, HD = 4, 16
SCORES = 2 * T + T
E1, HID = 8, 170
CH1 = (E1 * HID + 127) // 128
LAST1 = E1 * HID - 128 * (CH1 - 1)


def constants():
    half = np.arange(128) // D
    same = (half[:, None] == half[None, :]).astype(np.float32)
    parts = {}
    parts["mean"] = same / D
    parts["center"] = np.eye(128, dtype=np.float32) - same / D
    parts["eye"] = np.eye(128, dtype=np.float32)
    head = np.arange(128) // K0
    parts["headsum"] = (head[:, None] == head[None, :]).astype(np.float32)
    t, s = np.arange(128)[:, None], np.arange(T)[None, :]
    main = (s >= t).astype(np.float32)
    row, col = np.arange(128)[:, None], np.arange(2 * REM)[None, :]
    rem = ((row < 2 * REM) & (row // REM == col // REM) & (col % REM >= row % REM)).astype(np.float32)
    parts["causal"] = np.concatenate([main, main, rem], 1)
    u = np.arange(128)[:, None]
    parts["upto"] = ((s >= u) & (u < HT)).astype(np.float32)
    inv = 1.0 / 10000.0 ** (np.arange(0, HD, 2, dtype=np.float32) / HD)
    freqs = np.outer(np.arange(T, dtype=np.float32), inv)
    emb = np.concatenate([freqs, freqs], -1)
    cos, sin = np.cos(emb).T.astype(np.float32), np.sin(emb).T.astype(np.float32)
    rope_q = np.tile(np.concatenate([cos, sin], 0), (HQ, 1))
    for n in range(2):
        parts[f"rope_q{n}"] = rope_q * (np.arange(128)[:, None] // 32 % 2 == n)
    parts["rope_kc"] = np.tile(cos, (2 * HQ, 1))
    parts["rope_ks"] = np.tile(sin, (2 * HQ, 1))
    row, col = np.arange(128)[:, None], np.arange(128)[None, :]
    parts["den_of_head"] = (row == 32 * (col // 32) + HD).astype(np.float32)
    parts["slot_bias"] = np.where(np.arange(128)[:, None] // K0 % 2 == np.arange(2)[None, :], 0.0, -1e4).astype(np.float32)
    parts["key_half"] = (np.arange(128)[:, None] // (2 * K0) == np.arange(2)[None, :]).astype(np.float32)
    parts["rank"] = np.tile((E1 - np.arange(E1)).astype(np.float32), (128, 1))
    sign = np.where(np.arange(HD) < HD // 2, -1.0, 1.0)
    ext = np.concatenate([np.ones(HD), sign])
    parts["sign_q"] = np.tile(np.tile(ext, HQ) * HD ** -0.5, (128, 1)).astype(np.float32)
    parts["sign_k2"] = np.tile(np.tile(sign, 2 * HQ), (128, 1)).astype(np.float32)
    ban = np.where(np.arange(HT)[None, :] > np.arange(HT)[:, None], -1e30, 0.0)
    banned = np.zeros((128, SCORES), np.float32)
    for at in (0, HT, T + HT, 2 * T + HT):
        banned[:HT, at:at + HT] = ban
    parts["banned"] = banned
    r = np.arange(128)[:, None]
    c0 = np.arange(3 * 128)[None, :]
    parts["pick0"] = ((r < 2 * E0) & (r % E0 == c0 // EH0)).astype(np.float32)
    c1 = np.arange(CH1 * 128)[None, :]
    parts["pick1"] = ((r < 2 * E1) & (r % E1 == c1 // HID)).astype(np.float32)
    at, spans = 0, {}
    for name, a in parts.items():
        spans[name] = (at, at + a.shape[1])
        at += a.shape[1]
    return np.ascontiguousarray(np.concatenate(list(parts.values()), 1), dtype=np.float32), spans


KEEP = "rank"
CONSTS, SPANS = constants()


class Signal:

    def __init__(self, sem, per):
        self.sem, self.per = sem, per

    def at(self, t, k=0):
        return t * self.per + (self.per * HEAD + k + 1)


def pipelined(eng, tiles, body):
    body(-1, 1, (0,))
    body(0, 0, (0, 1))
    with eng.Fori(0, (tiles - 2) // 2) as k:
        body(2 * k + 1, 1, (0, 1, 2))
        body(2 * k + 2, 0, (0, 1, 2))
    body(tiles - 1, 1, (1, 2))
    body(tiles, 0, (2,))


def last_use(c, n, ring=2):
    return c - ring if c >= ring else max(j for j in range(n) if j % ring == c) - n


def build(nc, ap, out, stop=99):
    B = ap["txt"].shape[1] * 2
    P = B // 2
    COLS = P * T
    GB = min(32, B)
    GROUPS = B // GB
    TILES = P
    TILES2 = P // 2

    stack = ExitStack()

    def sbuf(ctx, name, shape, dt=F32):
        return ctx.enter_context(nc.sbuf_tensor(name, shape, dt))

    sems = {}

    def plain(name):
        if name not in sems:
            sems[name] = stack.enter_context(nc.semaphore(name))
        return sems[name]

    def signals(**per):
        made = {name: Signal(plain(name), n) for name, n in per.items()}
        with nc.Block() as block:

            @block.sync
            def _(sp):
                for sig in made.values():
                    sp.sem_clear(sig.sem)
                    sp.sem_inc(sig.sem, sig.per * HEAD)
        return made

    with stack:
        bank = [stack.enter_context(nc.psum_tensor(f"bank{i}", [128, 512], F32)) for i in range(8)]
        resid = sbuf(stack, "resid", [128, COLS])
        keep_w = SPANS[KEEP][1]
        const = sbuf(stack, "const", [128, keep_w])

        def table(name):
            a, b = SPANS[name]
            return const[:, a:b]

        w_kq = sbuf(stack, "w_kq", [128, 2, 4, 128], F32R)
        w_vo = sbuf(stack, "w_vo", [128, H0 // 2, D])
        join = sbuf(stack, "join", [128, D], F32R)
        w_r1 = sbuf(stack, "w_r1", [128, 2, RH0], F32R)
        b_r1 = sbuf(stack, "b_r1", [RH0, 1])
        w_r2 = sbuf(stack, "w_r2", [RH0 + 1, E0])
        w_e1 = sbuf(stack, "w_e1", [128, 2, 3, 128], F32R)
        b_e1 = sbuf(stack, "b_e1", [128, 3])
        w_e2 = sbuf(stack, "w_e2", [128, 3, 128])
        b_e2 = sbuf(stack, "b_e2", [128, 3])
        w_e3 = sbuf(stack, "w_e3", [128, 3, D])
        b_e3 = sbuf(stack, "b_e3", [2 * E0, D])
        pick0 = sbuf(stack, "pick0", [2 * E0, 3, 128], F32R)
        w_kv = sbuf(stack, "w_kv", [128, 2, 2 * D])
        w_r = sbuf(stack, "w_r", [128, 2, D])
        w_o = sbuf(stack, "w_o", [128, 128])
        decay = sbuf(stack, "decay", [HT, T])
        w_q = sbuf(stack, "w_q", [128, 2, 3, 128], F32R)
        w_v = sbuf(stack, "w_v", [128, 2, 32], F32R)
        w_ao = sbuf(stack, "w_ao", [128, D])
        w_rt = sbuf(stack, "w_rt", [128, 2 * E1])
        ln1 = sbuf(stack, "ln1", [128, 1])
        ln2 = sbuf(stack, "ln2", [128, 1])
        banned = sbuf(stack, "banned", [128, SCORES], BF16)
        eye_b = sbuf(stack, "eye_b", [128, HT], BF16)
        eps = sbuf(stack, "eps", [128, 3])
        ln_eps, rms_eps, att_eps = (eps[:, n:n + 1] for n in range(3))
        late = sbuf(stack, "late", [128, max(P * 4 * E1, 6 * T2)])
        logits1 = late[0:HT, 0:P * 4 * E1].rearrange("p (n e) -> p n e", e=E1)

        with ExitStack() as ctx:
            image = sbuf(ctx, "image", [128, B, IMG])
            w_tok = sbuf(ctx, "w_tok", [128, PW, 128])
            b_tok = sbuf(ctx, "b_tok", [128, 1])
            raw_kq = sbuf(ctx, "raw_kq", [128, 512])
            raw_vt = sbuf(ctx, "raw_vt", [D, H0, D])
            raw_o = sbuf(ctx, "raw_o", [D, H0, D])
            raw_r1 = sbuf(ctx, "raw_r1", [128, RH0])
            raw_e1 = sbuf(ctx, "raw_e1", [128, 384])
            raw_kvr = sbuf(ctx, "raw_kvr", [128, 3, D])
            mix = sbuf(ctx, "mix", [128, 3])
            unmix = sbuf(ctx, "unmix", [128, 3])
            raw_decay = sbuf(ctx, "raw_decay", [HT, T])
            raw_q = sbuf(ctx, "raw_q", [128, 3, 128])
            raw_q2 = sbuf(ctx, "raw_q2", [128, 3, 128])
            raw_v = sbuf(ctx, "raw_v", [128, 32])
            raw_v2 = sbuf(ctx, "raw_v2", [128, 32])
            raw_rt = sbuf(ctx, "raw_rt", [128, E1])
            spare = sbuf(ctx, "spare", [128, CONSTS.shape[1] - keep_w])

            def spare_table(name):
                a, b = SPANS[name]
                return spare[:, a - keep_w:b - keep_w]

            image_in = [plain(f"image_in{g}") for g in range(GROUPS)]
            text_in = plain("text_in")
            tok_w_in = plain("tok_w_in")
            small_in = plain("small_in")
            zeroed = plain("zeroed")
            tokens = plain("tokens")
            gelu_done = plain("gelu_done")
            vo_done = plain("vo_done")
            prep = plain("prep")

            small = []

            def load_small():
                twice = [
                    (raw_kq, "wkq"), (raw_r1, "rw1"), (raw_e1, "ew1"), (mix, "mix"), (raw_v, "wv"),
                    (raw_rt, "rt"), (ln1, "ln1"), (ln2, "ln2"), (b_tok, "btok"),
                ]
                for h in range(2):
                    rows = slice(D * h, D * h + D)
                    small.extend((dst[rows, :], ap[src]) for dst, src in twice)
                    small.append((raw_kvr[rows, :, :], ap["wkvr"]))
                    small.append((raw_q[rows, :, :], ap["wq"]))
                    small.append((w_o[rows, D * h:D * h + D], ap["wo1"]))
                for e in range(E0):
                    rows = slice(D * (e % 2), D * (e % 2) + D)
                    small.append((w_e2[rows, e // 2, D * (e % 2):D * (e % 2) + D], ap["ew2"][e]))
                for h in range(HQ):
                    small.append((w_ao[32 * h:32 * h + HD, :], ap["wao"][HD * h:HD * h + HD, :]))
                small.extend([
                    (const[:, :], ap["const"][:, 0:keep_w]), (spare[:, :], ap["const"][:, keep_w:]),
                    (raw_vt[:, :, :], ap["wvt"]), (raw_o[:, :, :], ap["wo0"]),
                    (b_r1[:, :], ap["rb1"]), (w_r2[0:RH0, :], ap["rw2"]), (w_r2[RH0:RH0 + 1, :], ap["rb2"]),
                    (b_e1[:, :], ap["eb1"]), (b_e2[:, :], ap["eb2"]), (w_e3[:, :, :], ap["ew3"]),
                    (b_e3[0:E0, :], ap["eb3"]), (b_e3[E0:2 * E0, :], ap["eb3"]),
                    (raw_decay[:, :], ap["decay"]),
                ])

            load_small()
            SMALL = 16 * len(small)

            with nc.Block() as block:

                @block.sync
                def _(sp):
                    sp.wait_ge(zeroed, 1)
                    for h in range(2):
                        sp.dma_start(w_tok[D * h:D * h + D, :, D * h:D * h + D], ap["wtok"]).then_inc(tok_w_in, 16)
                    for g in range(GROUPS):
                        sp.dma_start(image[:, g * GB:(g + 1) * GB, :], ap["x"][:, g * GB:(g + 1) * GB, :]).then_inc(image_in[g], 16)
                    stream = resid[:, :].rearrange("c (p t) -> c p t", t=T)
                    sp.dma_start(stream[:, :, TOK:T], ap["txt"]).then_inc(text_in, 16)
                    sp.wait_ge(text_in, 16)

                @block.gpsimd
                def _(pool):
                    nc.gpsimd.memset(w_tok[:, :, :], 0.0).then_inc(zeroed, 1)
                    nc.gpsimd.memset(ln_eps, LN_EPS)
                    nc.gpsimd.memset(rms_eps, RMS_EPS)
                    nc.gpsimd.memset(att_eps, ATT_EPS)
                    nc.gpsimd.memset(w_e2[:, :, :], 0.0)
                    nc.gpsimd.memset(w_o[:, :], 0.0)
                    nc.gpsimd.memset(w_ao[:, :], 0.0)
                    nc.gpsimd.memset(w_rt[:, :], 0.0).then_inc(zeroed, 1)

                @block.scalar
                def _(act):
                    act.wait_ge(zeroed, 2)
                    for dst, src in small:
                        act.dma_start(dst, src).then_inc(small_in, 16)
                    act.wait_ge(small_in, SMALL)
                    stream = resid[:, :].rearrange("c (p t) -> c p t", t=T)
                    for g in range(GROUPS):
                        act.wait_ge(tokens, g + 1)
                        got = bank[g][:, 0:GB * NW].rearrange("c (p two w) -> c p two w", two=2, w=NW)
                        for r in range(NH):
                            for odd in range(2):
                                nc.scalar.activation(
                                    stream[D * odd:D * odd + D, g * GB // 2:(g + 1) * GB // 2, r * NW:r * NW + NW],
                                    got[D * r:D * r + D, :, odd, :], ACT.Gelu,
                                    bias=b_tok[D * r:D * r + D, :],
                                ).then_inc(gelu_done, 1)

                @block.tensor
                def _(pe):
                    pe.wait_ge(tok_w_in, 32)
                    for g in range(GROUPS):
                        pe.wait_ge(image_in[g], 16)
                        for j in range(PW):
                            mm = nc.tensor.matmul(
                                bank[g][:, 0:GB * NW], w_tok[:, j, :],
                                image[:, g * GB:(g + 1) * GB, j:j + SW * (NW - 1) + 1:SW],
                                start=(j == 0), stop=(j == PW - 1))
                        mm.then_inc(tokens, 1)
                    pe.wait_ge(small_in, SMALL)
                    for h in range(H0):
                        rows = slice(D * (h % 2), D * (h % 2) + D)
                        mm = nc.tensor.matmul(bank[7][rows, D * (h // 2):D * (h // 2) + D], raw_vt[:, h, :],
                                              raw_o[:, h, :], start=True, stop=True)
                    mm.then_inc(vo_done, 1)

                @block.vector
                def _(dve):
                    count = [0]

                    def step(ins):
                        ins.then_inc(prep, 1)
                        count[0] += 1
                        return count[0]

                    def split(dst, src):
                        n = step(nc.vector.tensor_copy(dst[:, 0], src))
                        dve.wait_ge(prep, n)
                        step(nc.vector.tensor_tensor(dst[:, 1], src, dst[:, 0].bitcast(F32), ALU.subtract))

                    dve.wait_ge(small_in, SMALL)
                    split(w_kq[:, :, :, :].rearrange("p s c m -> p s (c m)"), raw_kq[:, :])
                    split(w_r1[:, :, :], raw_r1[:, :])
                    split(w_e1[:, :, :, :].rearrange("p s c m -> p s (c m)"), raw_e1[:, :])
                    step(nc.vector.tensor_copy(pick0[:, :, :].rearrange("p c m -> p (c m)"), spare_table("pick0")[0:2 * E0, :]))
                    for h in range(2):
                        rows = slice(D * h, D * h + D)
                        step(nc.vector.tensor_copy(join[rows, :], table("eye")[rows, rows]))
                    step(nc.vector.tensor_copy(banned[:, :], spare_table("banned")))
                    step(nc.vector.tensor_copy(eye_b[:, :], table("eye")[:, 0:HT]))
                    step(nc.vector.tensor_tensor(decay[:, :], raw_decay[:, :], table("upto")[0:HT, :], ALU.mult))
                    n = step(nc.vector.tensor_scalar(unmix[:, :], mix[:, :], -1.0, 1.0, ALU.mult, ALU.add))
                    dve.wait_ge(prep, n)
                    for odd in range(2):
                        now, before = slice(D * odd, D * odd + D), slice(D - D * odd, 2 * D - D * odd)
                        for rows, by in ((now, mix), (before, unmix)):
                            for n in range(3):
                                dst = w_r[rows, odd, :] if n == 2 else w_kv[rows, odd, D * n:D * n + D]
                                step(nc.vector.tensor_scalar(dst, raw_kvr[rows, n, :], by[rows, n:n + 1], None, ALU.mult))
                    step(nc.vector.tensor_tensor(raw_q2[:, 0, :], raw_q[:, 0, :], spare_table("sign_q"), ALU.mult))
                    step(nc.vector.tensor_copy(raw_q2[:, 1, :], raw_q[:, 1, :]))
                    n = step(nc.vector.tensor_tensor(raw_q2[:, 2, :], raw_q[:, 2, :], spare_table("sign_k2"), ALU.mult))
                    dve.wait_ge(prep, n)
                    step(nc.vector.tensor_scalar(raw_q[:, :, :], raw_q2[:, :, :], ln1[:, :], None, ALU.mult))
                    n = step(nc.vector.tensor_scalar(raw_v2[:, :], raw_v[:, :], ln1[:, :], None, ALU.mult))
                    dve.wait_ge(prep, n)
                    split(w_q[:, :, :, :].rearrange("p s c m -> p s (c m)"), raw_q[:, :, :].rearrange("p c m -> p (c m)"))
                    split(w_v[:, :, :], raw_v2[:, :])
                    dve.wait_ge(zeroed, 2)
                    for h in range(2):
                        rows = slice(D * h, D * h + D)
                        step(nc.vector.tensor_scalar(w_rt[rows, E1 * h:E1 * h + E1], raw_rt[rows, :], ln2[rows, :], None, ALU.mult))
                    dve.wait_ge(vo_done, 1)
                    step(nc.vector.tensor_copy(w_vo[:, :, :].rearrange("p g m -> p (g m)"), bank[7][:, 0:D * H0 // 2]))
                    dve.wait_ge(prep, count[0])

        def norm_pass(tag, src, layer_norm=True, twice=False, keep=None, xx=None, router=0, logits=None):
            W = T2
            E = E0 if router == 1 else E1
            s = signals(centred=1, squared=1, summed=1, logged=1, scaled=1, normed=1, hi_made=1, parted=1,
                        var_scaled=1, mean_square=1, rms_logged=1, rms_scaled=1, rms_normed=1, hidden=1,
                        relued=1, scored=1, logits_out=1)
            ones_set = plain(f"{tag}_ones_set")

            def cols(t):
                return bass.ds(t * W, W)

            with ExitStack() as ctx:
                sq = sbuf(ctx, f"{tag}_sq", [128, 2, W])
                lg = sbuf(ctx, f"{tag}_lg", [128, 2, W])
                rstd = sbuf(ctx, f"{tag}_rstd", [128, 2, W])
                if keep is None:
                    xn = sbuf(ctx, f"{tag}_xn", [128, 2, W])
                if twice:
                    half_ms = sbuf(ctx, f"{tag}_half_ms", [128, W])
                    ms = sbuf(ctx, f"{tag}_ms", [128, W])
                    lg2 = sbuf(ctx, f"{tag}_lg2", [128, 2, W])
                    rms = sbuf(ctx, f"{tag}_rms", [128, W])
                    hn = sbuf(ctx, f"{tag}_hn", [128, 2, W])
                if router == 1:
                    rh = sbuf(ctx, f"{tag}_rh", [RH0 + 1, 2, 2, W])

                def result(t, u):
                    if twice:
                        return hn[:, u, :]
                    return keep[:, cols(t)] if keep is not None else xn[:, u, :]

                result_ready = s["rms_normed"] if twice else s["normed"]

                with nc.Block() as block:

                    @block.tensor
                    def _(pe):
                        def body(t, u, stages):
                            if 0 in stages and layer_norm:
                                pe.wait_ge(s["normed"].sem, s["normed"].at(t - 1))
                                nc.tensor.matmul(bank[1 - u][:, 0:W], table("center"), src[:, cols(t + 1)],
                                                 start=True, stop=True).then_inc(s["centred"].sem, 1)
                            if 2 in stages and router == 1:
                                pe.wait_ge(s["parted"].sem, s["parted"].at(t - 1))
                                pe.wait_ge(s["relued"].sem, s["relued"].at(t - 2))
                                for b in range(2):
                                    for part in range(2):
                                        mm = nc.tensor.matmul(bank[4 + b][0:RH0, 0:W], w_r1[:, part, :],
                                                              xx[:, b, cols(t - 1)], start=(part == 0), stop=(part == 1))
                                mm.then_inc(s["hidden"].sem, 1)
                            if 1 in stages:
                                pe.wait_ge(s["squared"].sem, s["squared"].at(t))
                                bank_read = s["var_scaled"] if twice else s["scaled"]
                                pe.wait_ge(bank_read.sem, bank_read.at(t - 2))
                                nc.tensor.matmul(bank[2 + u][:, 0:W], table("mean"), sq[:, u, :],
                                                 start=True, stop=True).then_inc(s["summed"].sem, 1)
                            if 2 in stages and router:
                                pe.wait_ge(s["logits_out"].sem, s["logits_out"].at(t - 2))
                                if router == 1:
                                    pe.wait_ge(s["relued"].sem, s["relued"].at(t - 1))
                                    for n in range(8):
                                        at = n // 4 * T + n % 2 * HT
                                        mm = nc.tensor.matmul(bank[6][0:HT, n * E:n * E + E],
                                                              rh[:, 1 - u, n // 2 % 2, at:at + HT], w_r2[:, :],
                                                              start=True, stop=True)
                                else:
                                    pe.wait_ge(result_ready.sem, result_ready.at(t - 1))
                                    for n in range(4):
                                        mm = nc.tensor.matmul(bank[6][0:HT, n * 2 * E:(n + 1) * 2 * E],
                                                              xn[:, 1 - u, n * HT:n * HT + HT], w_rt[:, :],
                                                              start=True, stop=True)
                                mm.then_inc(s["scored"].sem, 1)

                        if router == 1:
                            pe.wait_ge(ones_set, 1)
                        pipelined(pe, TILES2, body)

                    @block.scalar
                    def _(act):
                        nc.scalar.preload_act_table_set(EXP_LN)

                        def body(t, u, stages):
                            if 0 in stages:
                                act.wait_ge(s["summed"].sem, s["summed"].at(t - 1))
                                if layer_norm:
                                    act.wait_ge(s["centred"].sem, s["centred"].at(t + 1))
                                got = bank[1 - u][:, 0:W] if layer_norm else src[:, cols(t + 1)]
                                nc.scalar.activation(sq[:, 1 - u, :], got, ACT.Square).then_inc(s["squared"].sem, 1)
                            if 2 in stages and router == 1:
                                act.wait_ge(s["hidden"].sem, s["hidden"].at(t - 1))
                                act.wait_ge(s["scored"].sem, s["scored"].at(t - 3))
                                for b in range(2):
                                    last = nc.scalar.activation(rh[0:RH0, 1 - u, b, :], bank[4 + b][0:RH0, 0:W],
                                                                ACT.Relu, bias=b_r1[:, :])
                                last.then_inc(s["relued"].sem, 1)
                            if 1 in stages:
                                act.wait_ge(s["summed"].sem, s["summed"].at(t))
                                nc.scalar.activation(lg[:, u, :], bank[2 + u][:, 0:W], ACT.Ln,
                                                     bias=ln_eps if layer_norm else rms_eps).then_inc(s["logged"].sem, 1)
                                act.wait_ge(s["logged"].sem, s["logged"].at(t))
                                rstd_read = s["mean_square"] if twice else s["normed"]
                                act.wait_ge(rstd_read.sem, rstd_read.at(t - 2))
                                nc.scalar.activation(rstd[:, u, :], lg[:, u, :], ACT.Exp, scale=-0.5).then_inc(s["scaled"].sem, 1)
                                if twice:
                                    act.wait_ge(s["mean_square"].sem, s["mean_square"].at(t))
                                    nc.scalar.activation(lg2[:, u, :], ms[:, :], ACT.Ln, bias=rms_eps).then_inc(s["rms_logged"].sem, 1)
                                    act.wait_ge(s["rms_logged"].sem, s["rms_logged"].at(t))
                                    act.wait_ge(s["rms_normed"].sem, s["rms_normed"].at(t - 1))
                                    nc.scalar.activation(rms[:, :], lg2[:, u, :], ACT.Exp, scale=-0.5).then_inc(s["rms_scaled"].sem, 1)
                        pipelined(act, TILES2, body)

                    @block.gpsimd
                    def _(pool):
                        if router == 1:
                            nc.gpsimd.memset(rh[:, :, :, :], 1.0).then_inc(ones_set, 1)

                        def body(t, u, stages):
                            if 1 in stages and xx is not None:
                                pool.wait_ge(result_ready.sem, result_ready.at(t))
                                for b in range(2):
                                    rows = slice(D * b, D * b + D)
                                    last = nc.gpsimd.tensor_copy(xx[rows, b, cols(t)], result(t, u)[rows, :])
                                last.then_inc(s["hi_made"].sem, 1)
                        if xx is not None:
                            pipelined(pool, TILES2, body)

                    @block.vector
                    def _(dve):
                        def body(t, u, stages):
                            if 1 in stages:
                                dve.wait_ge(s["scaled"].sem, s["scaled"].at(t))
                                if router == 2:
                                    dve.wait_ge(s["scored"].sem, s["scored"].at(t - 2))
                                if xx is not None:
                                    dve.wait_ge(s["hi_made"].sem, s["hi_made"].at(t - 2))
                                first = bank[u][:, 0:W] if layer_norm else src[:, cols(t)]
                                dst = keep[:, cols(t)] if keep is not None else xn[:, u, :]
                                nc.vector.tensor_tensor(dst, first, rstd[:, u, :], ALU.mult).then_inc(s["normed"].sem, 1)
                                if twice:
                                    nc.vector.tensor_tensor(half_ms[:, :], bank[2 + u][:, 0:W], rstd[:, u, :],
                                                            ALU.mult).then_inc(s["var_scaled"].sem, 1)
                                    dve.wait_ge(s["var_scaled"].sem, s["var_scaled"].at(t))
                                    dve.wait_ge(s["rms_logged"].sem, s["rms_logged"].at(t - 1))
                                    nc.vector.tensor_tensor(ms[:, :], half_ms[:, :], rstd[:, u, :],
                                                            ALU.mult).then_inc(s["mean_square"].sem, 1)
                                    dve.wait_ge(s["normed"].sem, s["normed"].at(t))
                                    dve.wait_ge(s["rms_scaled"].sem, s["rms_scaled"].at(t))
                                    nc.vector.tensor_tensor(hn[:, u, :], dst, rms[:, :], ALU.mult).then_inc(s["rms_normed"].sem, 1)
                                if xx is not None:
                                    dve.wait_ge(result_ready.sem, result_ready.at(t))
                                    dve.wait_ge(s["hi_made"].sem, s["hi_made"].at(t))
                                    for b in range(2):
                                        hi, lo = slice(D * b, D * b + D), slice(D - D * b, 2 * D - D * b)
                                        last = nc.vector.tensor_tensor(xx[lo, b, cols(t)], result(t, u)[hi, :],
                                                                       xx[hi, b, cols(t)].bitcast(F32), ALU.subtract)
                                    last.then_inc(s["parted"].sem, 1)
                            if 2 in stages and router:
                                dve.wait_ge(s["scored"].sem, s["scored"].at(t - 1))
                                flat = logits[:, :, :].rearrange("p n e -> p (n e)")
                                for q in range(2):
                                    dst = flat[:, bass.ds((t - 1) * (8 * E) + q * 4 * E, 4 * E)]
                                    got = bank[6][0:HT, q * 4 * E:(q + 1) * 4 * E]
                                    if router == 2:
                                        dst = dst.rearrange("p (b j e) -> p j b e", b=2, j=2)
                                        got = got.rearrange("p (j b e) -> p j b e", b=2, j=2)
                                    last = nc.vector.tensor_copy(dst, got)
                                last.then_inc(s["logits_out"].sem, 1)
                        pipelined(dve, TILES2, body)

        def linear_attention(xx):
            s = signals(turned=1, rows_out=1, kq=4, kq_neg=4, kq_exp=4, kq_elu=4, k_made=2, key_sum=2, qk=2, fixed=1, den=2, den_log=2,
                        den_inv=2, q_normed=2, scores=8, masked=8, mixed=4, mixed_out=4, out=1, added=1)

            def cols(t, n=T):
                return bass.ds(t * T, n)

            with ExitStack() as ctx:
                xl = sbuf(ctx, "a_xl", [128, 2, T], F32R)
                xt = sbuf(ctx, "a_xt", [128, 2, 3, D])
                ek = sbuf(ctx, "a_ek", [128, 2, T2])
                xr = sbuf(ctx, "a_xr", [128, 128], F32R)
                kr = sbuf(ctx, "a_kr", [128, 2, 2, 2, 128])
                neg = sbuf(ctx, "a_neg", [128, 2, T2])
                restart = sbuf(ctx, "a_restart", [128, T2])
                ones_set, zeroed = plain("a_ones_set"), plain("a_zeroed")
                k = sbuf(ctx, "a_k", [128, 2, T2])
                kz = sbuf(ctx, "a_kz", [128, 2, 2, 2, T2])
                q = sbuf(ctx, "a_q", [128, 2, T2])
                ksum = sbuf(ctx, "a_ksum", [128, 2, T2])
                qk = sbuf(ctx, "a_qk", [128, 2, T2])
                dl = sbuf(ctx, "a_dl", [128, 2, T2])
                di = sbuf(ctx, "a_di", [128, 2, 2, T2])
                qn = sbuf(ctx, "a_qn", [128, 2, 2, 2, T2])
                sc = sbuf(ctx, "a_sc", [128, 4, 2 * T + 2 * REM])
                gs = sbuf(ctx, "a_gs", [128, 2, H0 // 2, T2])
                SCB, GB_, PB = (0, 1), (2, 3), (4, 5)

                def batches(rows):
                    return rows.rearrange("p (b t) -> p b t", b=2)

                with nc.Block() as block:

                    @block.tensor
                    def _(pe):
                        def scores(t, u, h):
                            c, ks, qs = h // 4, h % 4 // 2, h % 2
                            if h % 4 == 0:
                                pe.wait_ge(s["k_made"].sem, s["k_made"].at(t, c))
                            pe.wait_ge(s["q_normed"].sem, s["q_normed"].at(t, c))
                            pe.wait_ge(s["masked"].sem, s["masked"].at(t, h - 2))
                            to = bank[SCB[h % 2]]
                            for b in range(2):
                                nc.tensor.matmul(to[:, b * T:b * T + T], kz[:, u, c, ks, b * T:b * T + 128],
                                                 qn[:, u, c, qs, b * T:b * T + T], start=True, stop=True)
                            nc.tensor.matmul(to[:, T2:T2 + 2 * REM], kr[:, u, c, ks, :],
                                             batches(qn[:, u, c, qs, :])[:, :, 128:T],
                                             start=True, stop=True).then_inc(s["scores"].sem, 1)

                        def mixtures(t, u, g):
                            if g == 0:
                                pe.wait_ge(s["rows_out"].sem, s["rows_out"].at(t))
                            pe.wait_ge(s["masked"].sem, s["masked"].at(t, 2 * g + 1))
                            pe.wait_ge(s["mixed_out"].sem, s["mixed_out"].at(t, g - 2))
                            to = bank[GB_[g % 2]]
                            for b in range(2):
                                for hh in range(2):
                                    nc.tensor.matmul(to[D * hh:D * hh + D, b * T:b * T + T], xt[:, u, b, :],
                                                     sc[:, (2 * g + hh) % 4, b * T:b * T + T], start=(b == 0), stop=False,
                                                     skip_group_check=True)
                            for hh in range(2):
                                mm = nc.tensor.matmul(batches(to[D * hh:D * hh + D, 0:T2])[:, :, 128:T], xt[:, u, 2, :],
                                                      sc[:, (2 * g + hh) % 4, T2:T2 + 2 * REM], start=False, stop=True,
                                                      skip_group_check=True)
                            mm.then_inc(s["mixed"].sem, 1)

                        def project(t, c):
                            if c < 2:
                                pe.wait_ge(s["den_log"].sem, s["den_log"].at(t - 1, c))
                            pe.wait_ge(s["kq_elu"].sem, s["kq_elu"].at(t, c - 2))
                            for part in range(2):
                                mm = nc.tensor.matmul(bank[PB[c % 2]][:, 0:T2], w_kq[:, part, c, :], xx[:, :, cols(t)],
                                                      start=(part == 0), stop=(part == 1))
                            mm.then_inc(s["kq"].sem, 1)

                        def denominators(t, c):
                            pe.wait_ge(s["qk"].sem, s["qk"].at(t, c))
                            nc.tensor.matmul(bank[PB[c]][:, 0:T2], table("headsum"), qk[:, c, :],
                                             start=True, stop=True).then_inc(s["den"].sem, 1)

                        def body(t, u, stages):
                            if 0 in stages:
                                project(t + 1, 0)
                            if 2 in stages:
                                mixtures(t - 1, 1 - u, 3)
                            if 0 in stages:
                                project(t + 1, 1)
                            if 1 in stages:
                                scores(t, u, 0)
                                scores(t, u, 1)
                                scores(t, u, 2)
                            if 2 in stages:
                                pe.wait_ge(s["added"].sem, s["added"].at(t - 2))
                                pe.wait_ge(s["mixed_out"].sem, s["mixed_out"].at(t - 1, 3))
                                for g in range(4):
                                    for b in range(2):
                                        mm = nc.tensor.matmul(bank[7][D * b:D * b + D, 0:T], w_vo[:, g, :],
                                                              gs[:, 1 - u, g, b * T:b * T + T], start=(g == 0), stop=(g == 3))
                                mm.then_inc(s["out"].sem, 1)
                            if 1 in stages:
                                mixtures(t, u, 0)
                                scores(t, u, 3)
                            if 0 in stages:
                                pe.wait_ge(s["fixed"].sem, s["fixed"].at(t + 1))
                                pe.wait_ge(s["rows_out"].sem, s["rows_out"].at(t))
                                for n, tokens in enumerate((xl[:, 0, 0:128], xl[:, 1, 0:128], xr[:, :])):
                                    mm = nc.tensor.matmul(bank[6][:, D * n:D * n + D], tokens, join[:, :], start=True, stop=True)
                                mm.then_inc(s["turned"].sem, 1)
                                project(t + 1, 2)
                                project(t + 1, 3)
                            if 1 in stages:
                                scores(t, u, 4)
                                mixtures(t, u, 1)
                                scores(t, u, 5)
                            if 0 in stages:
                                denominators(t + 1, 0)
                            if 1 in stages:
                                scores(t, u, 6)
                            if 0 in stages:
                                denominators(t + 1, 1)
                            if 1 in stages:
                                mixtures(t, u, 2)
                                scores(t, u, 7)
                        pipelined(pe, TILES, body)

                    @block.scalar
                    def _(act):
                        nc.scalar.preload_act_table_set(EXP_LN)

                        def mixed_out(t, u, g):
                            act.wait_ge(s["mixed"].sem, s["mixed"].at(t, g))
                            if g == 0:
                                act.wait_ge(s["out"].sem, s["out"].at(t - 2))
                            nc.scalar.copy(gs[:, u, g, :], bank[GB_[g % 2]][:, 0:T2]).then_inc(s["mixed_out"].sem, 1)

                        def exp(t, c):
                            act.wait_ge(s["kq"].sem, s["kq"].at(t, c))
                            act.wait_ge(s["kq_exp"].sem, s["kq_exp"].at(t, c - 2))
                            nc.scalar.activation(neg[:, c % 2, :], bank[PB[c % 2]][:, 0:T2], ACT.Relu, scale=-1.0).then_inc(s["kq_neg"].sem, 1)
                            act.wait_ge(s["kq_neg"].sem, s["kq_neg"].at(t, c))
                            act.wait_ge(s["kq_elu"].sem, s["kq_elu"].at(t, c - 2))
                            nc.scalar.activation(ek[:, c % 2, :], neg[:, c % 2, :], ACT.Exp, scale=-1.0).then_inc(s["kq_exp"].sem, 1)

                        def body(t, u, stages):
                            if 0 in stages:
                                exp(t + 1, 0)
                            if 2 in stages:
                                mixed_out(t - 1, 1 - u, 3)
                            if 0 in stages:
                                exp(t + 1, 1)
                            if 1 in stages:
                                mixed_out(t, u, 0)
                            if 0 in stages:
                                exp(t + 1, 2)
                                exp(t + 1, 3)
                            if 1 in stages:
                                mixed_out(t, u, 1)
                            if 0 in stages:
                                for c in range(2):
                                    act.wait_ge(s["den"].sem, s["den"].at(t + 1, c))
                                    nc.scalar.activation(dl[:, c, :], bank[PB[c]][:, 0:T2], ACT.Ln, bias=att_eps).then_inc(s["den_log"].sem, 1)
                                    act.wait_ge(s["den_log"].sem, s["den_log"].at(t + 1, c))
                                    act.wait_ge(s["q_normed"].sem, s["q_normed"].at(t, c))
                                    for slot in range(2):
                                        last = nc.scalar.activation(di[:, c, slot, :], dl[:, c, :], ACT.Exp, scale=-1.0,
                                                                    bias=table("slot_bias")[:, slot:slot + 1])
                                    last.then_inc(s["den_inv"].sem, 1)
                            if 1 in stages:
                                mixed_out(t, u, 2)
                        pipelined(act, TILES, body)

                    @block.gpsimd
                    def _(pool):
                        nc.gpsimd.memset(kr[:, :, :, :, :], 0.0)
                        nc.gpsimd.memset(xr[:, :].bitcast(F32), 0.0).then_inc(zeroed, 1)
                        pool.wait_ge(zeroed, 1)
                        nc.gpsimd.memset(restart[:, 1:T], 1.0)
                        nc.gpsimd.memset(restart[:, T + 1:T2], 1.0)
                        nc.gpsimd.memset(restart[:, 0:T + 1:T], 0.0).then_inc(ones_set, 1)

                        def body(t, u, stages):
                            if 0 in stages:
                                pool.wait_ge(s["turned"].sem, s["turned"].at(t))
                                nc.gpsimd.tensor_copy(xr[:, 0:2 * REM].rearrange("p (b t) -> p b t", b=2), xx[:, :, bass.ds((t + 1) * T + 128, REM)])
                                nc.gpsimd.tensor_copy(xl[:, :, :], xx[:, :, cols(t + 1)]).then_inc(s["fixed"].sem, 1)
                                for c in range(2):
                                    pool.wait_ge(s["kq_elu"].sem, s["kq_elu"].at(t + 1, c))
                                    pool.wait_ge(s["scores"].sem, s["scores"].at(t - 1, 7))
                                    for half in range(2):
                                        last = nc.gpsimd.tensor_tensor(kz[:, 1 - u, c, half, :], k[:, c, :],
                                                                       table("key_half")[:, half:half + 1].broadcast_to([128, T2]), ALU.mult)
                                    last.then_inc(s["k_made"].sem, 1)
                                for c in range(2):
                                    pool.wait_ge(s["den_inv"].sem, s["den_inv"].at(t + 1, c))
                                    pool.wait_ge(s["kq_elu"].sem, s["kq_elu"].at(t + 1, c + 2))
                                    pool.wait_ge(s["scores"].sem, s["scores"].at(t - 1, 7))
                                    for slot in range(2):
                                        last = nc.gpsimd.tensor_tensor(qn[:, 1 - u, c, slot, :], q[:, c, :], di[:, c, slot, :], ALU.mult)
                                    last.then_inc(s["q_normed"].sem, 1)
                        pipelined(pool, TILES, body)

                    @block.vector
                    def _(dve):
                        dve.wait_ge(ones_set, 1)

                        def mask(t, u, h):
                            dve.wait_ge(s["scores"].sem, s["scores"].at(t, h))
                            dve.wait_ge(s["mixed"].sem, s["mixed"].at(t, h // 2 - 2))
                            w = 2 * T + 2 * REM
                            nc.vector.tensor_tensor(sc[:, h % 4, :], bank[SCB[h % 2]][:, 0:w], table("causal"), ALU.mult).then_inc(s["masked"].sem, 1)

                        def elu(t, u, c):
                            dve.wait_ge(s["kq_exp"].sem, s["kq_exp"].at(t, c))
                            if c < 2:
                                dve.wait_ge(s["k_made"].sem, s["k_made"].at(t - 1, c))
                                dve.wait_ge(s["key_sum"].sem, s["key_sum"].at(t - 1, c))
                                dve.wait_ge(s["scores"].sem, s["scores"].at(t - 2, 7))
                            else:
                                dve.wait_ge(s["q_normed"].sem, s["q_normed"].at(t - 1, c - 2))
                            dst = k[:, c, :] if c < 2 else q[:, c - 2, :]
                            nc.vector.scalar_tensor_tensor(out=dst, in0=bank[PB[c % 2]][:, 0:T2], scalar=1.0, in1=ek[:, c % 2, :],
                                                           op0=ALU.add, op1=ALU.max).then_inc(s["kq_elu"].sem, 1)

                        def keys(t, u, c):
                            elu(t, u, c)
                            dve.wait_ge(s["kq_elu"].sem, s["kq_elu"].at(t, c))
                            for half in range(2):
                                nc.vector.tensor_scalar(batches(kr[:, u, c, half, 0:2 * REM]), batches(k[:, c, :])[:, :, 128:T],
                                                        table("key_half")[:, half:half + 1], None, ALU.mult)
                            nc.vector.tensor_tensor_scan(ksum[:, c, :], restart[:, :], k[:, c, :], 0.0,
                                                         op0=ALU.mult, op1=ALU.add).then_inc(s["key_sum"].sem, 1)

                        def queries(t, u, c):
                            elu(t, u, c + 2)
                            dve.wait_ge(s["kq_elu"].sem, s["kq_elu"].at(t, c + 2))
                            dve.wait_ge(s["key_sum"].sem, s["key_sum"].at(t, c))
                            dve.wait_ge(s["den"].sem, s["den"].at(t - 1, c))
                            nc.vector.tensor_tensor(qk[:, c, :], q[:, c, :], ksum[:, c, :], ALU.mult).then_inc(s["qk"].sem, 1)

                        def body(t, u, stages):
                            if 1 in stages:
                                mask(t, u, 0)
                            if 0 in stages:
                                keys(t + 1, 1 - u, 0)
                            if 1 in stages:
                                mask(t, u, 1)
                            if 0 in stages:
                                keys(t + 1, 1 - u, 1)
                            if 1 in stages:
                                mask(t, u, 2)
                            if 2 in stages:
                                dve.wait_ge(s["out"].sem, s["out"].at(t - 1))
                                nc.vector.tensor_tensor(resid[:, cols(t - 1)], bank[7][:, 0:T], resid[:, cols(t - 1)], ALU.add).then_inc(s["added"].sem, 1)
                            if 1 in stages:
                                mask(t, u, 3)
                            if 0 in stages:
                                dve.wait_ge(s["turned"].sem, s["turned"].at(t + 1))
                                dve.wait_ge(s["mixed"].sem, s["mixed"].at(t - 1, 3))
                                nc.vector.tensor_copy(xt[:, 1 - u, :, :].rearrange("p w c -> p (w c)"), bank[6][:, 0:3 * D]).then_inc(s["rows_out"].sem, 1)
                            if 0 in stages:
                                queries(t + 1, 1 - u, 0)
                            if 1 in stages:
                                mask(t, u, 4)
                            if 0 in stages:
                                queries(t + 1, 1 - u, 1)
                            if 1 in stages:
                                mask(t, u, 5)
                                mask(t, u, 6)
                                mask(t, u, 7)
                        pipelined(dve, TILES, body)

        def choose_experts(tag, logits, E, gates):
            N = P * 4
            made = plain(f"{tag}_chosen")
            exp_done = plain(f"{tag}_exp_done")
            gap_made = plain(f"{tag}_gap_made")

            with ExitStack() as ctx:
                prob = sbuf(ctx, f"{tag}_prob", [HT, N, E])
                one = sbuf(ctx, f"{tag}_one", [HT, N, E])
                two = sbuf(ctx, f"{tag}_two", [HT, N, E])
                top = sbuf(ctx, f"{tag}_top", [HT, 6, N])

                def wide(row):
                    return top[:, row, :].unsqueeze(2).broadcast_to([HT, N, E])

                rank = table("rank")[0:HT, 0:E].unsqueeze(1).broadcast_to([HT, N, E])
                BEST, SECOND, GAP, W1, W2, TMP = range(6)

                with nc.Block() as block:

                    @block.scalar
                    def _(act):
                        nc.scalar.preload_act_table_set(EXP_LN)
                        act.wait_ge(made, 2)
                        nc.scalar.activation(prob[:, :, :], prob[:, :, :], ACT.Exp).then_inc(exp_done, 1)
                        if E == E0:
                            act.wait_ge(gap_made, 1)
                            nc.scalar.activation(top[:, W2, :], top[:, GAP, :], ACT.Exp).then_inc(exp_done, 1)

                    @block.vector
                    def _(dve):
                        count = [0]

                        def chain(ins):
                            ins.then_inc(made, 1)
                            count[0] += 1
                            dve.wait_ge(made, count[0])

                        def tt(dst, a, b, op):
                            chain(nc.vector.tensor_tensor(dst, a, b, op))

                        def first_of(onehot, row):
                            tt(onehot, prob[:, :, :], wide(row), ALU.is_ge)
                            tt(onehot, onehot, rank, ALU.mult)
                            chain(nc.vector.tensor_reduce(top[:, TMP, :], onehot, AX.X, ALU.max))
                            tt(onehot, onehot, wide(TMP), ALU.is_equal)

                        chain(nc.vector.tensor_reduce(top[:, TMP, :], logits[:, :, :], AX.X, ALU.max))
                        tt(prob[:, :, :], logits[:, :, :], wide(TMP), ALU.subtract)
                        dve.wait_ge(exp_done, 1)
                        chain(nc.vector.tensor_reduce(top[:, TMP, :], prob[:, :, :], AX.X, ALU.add))
                        chain(nc.vector.reciprocal(top[:, GAP, :], top[:, TMP, :]))
                        tt(prob[:, :, :], prob[:, :, :], wide(GAP), ALU.mult)
                        chain(nc.vector.tensor_reduce(top[:, BEST, :], prob[:, :, :], AX.X, ALU.max))
                        first_of(one[:, :, :], BEST)
                        chain(nc.vector.scalar_tensor_tensor(out=prob[:, :, :], in0=one[:, :, :], scalar=-2.0,
                                                             in1=prob[:, :, :], op0=ALU.mult, op1=ALU.add))
                        chain(nc.vector.tensor_reduce(top[:, SECOND, :], prob[:, :, :], AX.X, ALU.max))
                        first_of(two[:, :, :], SECOND)
                        if E == E0:
                            nc.vector.tensor_tensor(top[:, GAP, :], top[:, SECOND, :], top[:, BEST, :],
                                                    ALU.subtract).then_inc(gap_made, 1)
                            dve.wait_ge(exp_done, 2)
                            chain(nc.vector.tensor_scalar(top[:, TMP, :], top[:, W2, :], 1.0, None, ALU.add))
                            chain(nc.vector.reciprocal(top[:, W1, :], top[:, TMP, :]))
                            tt(top[:, W2, :], top[:, W2, :], top[:, W1, :], ALU.mult)
                        else:
                            tt(top[:, TMP, :], top[:, BEST, :], top[:, SECOND, :], ALU.add)
                            chain(nc.vector.tensor_scalar(top[:, TMP, :], top[:, TMP, :], ATT_EPS, None, ALU.add))
                            chain(nc.vector.reciprocal(top[:, GAP, :], top[:, TMP, :]))
                            tt(top[:, W1, :], top[:, BEST, :], top[:, GAP, :], ALU.mult)
                            tt(top[:, W2, :], top[:, SECOND, :], top[:, GAP, :], ALU.mult)
                        tt(one[:, :, :], one[:, :, :], wide(W1), ALU.mult)
                        tt(two[:, :, :], two[:, :, :], wide(W2), ALU.mult)
                        tt(one[:, :, :], one[:, :, :], two[:, :, :], ALU.add)
                        chain(nc.vector.tensor_copy(gates[:, :, 0:E], one[:, :, :]))
                        tt(gates[:, :, E:2 * E], one[:, :, :], gates[:, :, 0:E].bitcast(F32), ALU.subtract)

        def experts0(xx, gates):
            s = signals(gate_fixed=1, gate_rows=1, gate_out=1, h1=3, h1_out=3, h2=3, h2_out=3, spread=3, gated=3, out=1, added=1)
            CH = E0 // 2

            def cols(t):
                return bass.ds(t * T, T)

            with ExitStack() as ctx:
                h1 = sbuf(ctx, "m_h1", [128, 2, CH, T2])
                h2 = sbuf(ctx, "m_h2", [128, CH, T2])
                hg = sbuf(ctx, "m_hg", [128, 2, CH, T2])
                gf = sbuf(ctx, "m_gf", [HT, 4, 2 * E0])
                gt = sbuf(ctx, "m_gt", [2 * E0, 2, T2], F32R)
                H1B, H2B, GTB, OUTB = (0, 1), (2, 3), 6, 7
                SPB = (4, 5)

                with nc.Block() as block:

                    @block.tensor
                    def _(pe):
                        def first(t, u, c):
                            pe.wait_ge(s["h1_out"].sem, s["h1_out"].at(t, last_use(c, CH)))
                            for part in range(2):
                                mm = nc.tensor.matmul(bank[H1B[c % 2]][:, 0:T2], w_e1[:, part, c, :], xx[:, :, cols(t)],
                                                      start=(part == 0), stop=(part == 1))
                            mm.then_inc(s["h1"].sem, 1)

                        def body(t, u, stages):
                            for c in range(CH):
                                if 1 in stages:
                                    pe.wait_ge(s["h1_out"].sem, s["h1_out"].at(t, c))
                                    pe.wait_ge(s["h2_out"].sem, s["h2_out"].at(t, last_use(c, CH)))
                                    nc.tensor.matmul(bank[H2B[c % 2]][:, 0:T2], w_e2[:, c, :], h1[:, u, c, :],
                                                     start=True, stop=True).then_inc(s["h2"].sem, 1)
                                    pe.wait_ge(s["gate_out"].sem, s["gate_out"].at(t))
                                    pe.wait_ge(s["gated"].sem, s["gated"].at(t, last_use(c, CH)))
                                    nc.tensor.matmul(bank[SPB[c % 2]][:, 0:T2], pick0[:, c, :], gt[:, u, :],
                                                     start=True, stop=True).then_inc(s["spread"].sem, 1)
                                if 0 in stages:
                                    first(t + 1, 1 - u, c)
                                if 0 in stages and c == 0:
                                    pe.wait_ge(s["gate_fixed"].sem, s["gate_fixed"].at(t + 1))
                                    pe.wait_ge(s["gate_out"].sem, s["gate_out"].at(t))
                                    for n in range(4):
                                        mm = nc.tensor.transpose(bank[GTB][0:2 * E0, n * HT:n * HT + HT], gf[:, n, :],
                                                                 table("eye")[0:HT, 0:HT])
                                    mm.then_inc(s["gate_rows"].sem, 1)
                                if 2 in stages and c == 0:
                                    pe.wait_ge(s["added"].sem, s["added"].at(t - 2))
                                    pe.wait_ge(s["gated"].sem, s["gated"].at(t - 1, CH - 1))
                                    for g in range(CH):
                                        for b in range(2):
                                            nc.tensor.matmul(bank[OUTB][D * b:D * b + D, 0:T], w_e3[:, g, :],
                                                             hg[:, 1 - u, g, b * T:b * T + T], start=(g == 0), stop=False)
                                    for b in range(2):
                                        mm = nc.tensor.matmul(bank[OUTB][D * b:D * b + D, 0:T], b_e3[:, :],
                                                              gt[:, 1 - u, b * T:b * T + T].bitcast(F32), start=False, stop=True)
                                    mm.then_inc(s["out"].sem, 1)
                        pipelined(pe, TILES, body)

                    @block.scalar
                    def _(act):
                        def body(t, u, stages):
                            for c in range(CH):
                                if 1 in stages:
                                    act.wait_ge(s["h2"].sem, s["h2"].at(t, c))
                                    act.wait_ge(s["gated"].sem, s["gated"].at(t, c - CH))
                                    nc.scalar.activation(h2[:, c, :], bank[H2B[c % 2]][:, 0:T2], ACT.Relu,
                                                         bias=b_e2[:, c:c + 1]).then_inc(s["h2_out"].sem, 1)
                                if 0 in stages:
                                    act.wait_ge(s["h1"].sem, s["h1"].at(t + 1, c))
                                    act.wait_ge(s["h2"].sem, s["h2"].at(t - 1, c))
                                    nc.scalar.activation(h1[:, 1 - u, c, :], bank[H1B[c % 2]][:, 0:T2], ACT.Relu,
                                                         bias=b_e1[:, c:c + 1]).then_inc(s["h1_out"].sem, 1)
                                if 0 in stages and c == 0:
                                    act.wait_ge(s["gate_rows"].sem, s["gate_rows"].at(t + 1))
                                    act.wait_ge(s["out"].sem, s["out"].at(t - 1))
                                    nc.scalar.copy(gt[:, 1 - u, :], bank[GTB][0:2 * E0, 0:T2]).then_inc(s["gate_out"].sem, 1)
                        pipelined(act, TILES, body)

                    @block.gpsimd
                    def _(pool):
                        flat = gates[:, :, :].rearrange("p n e -> p (n e)")

                        def body(t, u, stages):
                            if 0 in stages:
                                pool.wait_ge(s["gate_rows"].sem, s["gate_rows"].at(t))
                                nc.gpsimd.tensor_copy(gf[:, :, :].rearrange("p n e -> p (n e)"),
                                                      flat[:, bass.ds((t + 1) * (8 * E0), 8 * E0)].bitcast(F32)).then_inc(s["gate_fixed"].sem, 1)
                        pipelined(pool, TILES, body)

                    @block.vector
                    def _(dve):
                        def body(t, u, stages):
                            for c in range(CH):
                                if 1 in stages:
                                    dve.wait_ge(s["h2_out"].sem, s["h2_out"].at(t, c))
                                    dve.wait_ge(s["spread"].sem, s["spread"].at(t, c))
                                    dve.wait_ge(s["out"].sem, s["out"].at(t - 2))
                                    nc.vector.tensor_tensor(hg[:, u, c, :], bank[SPB[c % 2]][:, 0:T2], h2[:, c, :], ALU.mult).then_inc(s["gated"].sem, 1)
                                if 2 in stages and c == 0:
                                    dve.wait_ge(s["out"].sem, s["out"].at(t - 1))
                                    nc.vector.tensor_tensor(resid[:, cols(t - 1)], bank[OUTB][:, 0:T], resid[:, cols(t - 1)], ALU.add).then_inc(s["added"].sem, 1)
                        pipelined(dve, TILES, body)

        def experts1(xx, gates):
            s = signals(gate_fixed=1, gate_rows=1, gate_out=1, up=CH1, silu=CH1, product=CH1, gated=CH1, out=1, added=1)

            def cols(t):
                return bass.ds(t * T, T)

            with ExitStack() as ctx:
                w1 = sbuf(ctx, "e_w1", [128, 2, CH1 * 128], F32R)
                w3 = sbuf(ctx, "e_w3", [128, 2, CH1 * 128], F32R)
                w2 = sbuf(ctx, "e_w2", [128, CH1, D])
                pick1 = sbuf(ctx, "e_pick", [2 * E1, CH1, 128], F32R)
                loaded, prep = plain("e_loaded"), plain("e_prep")
                with ExitStack() as raw_ctx:
                    raw1 = sbuf(raw_ctx, "e_raw1", [128, E1 * HID])
                    raw3 = sbuf(raw_ctx, "e_raw3", [128, E1 * HID])
                    raw_pick = sbuf(raw_ctx, "e_raw_pick", [2 * E1, CH1 * 128])

                    with nc.Block() as block:

                        @block.sync
                        def _(sp):
                            for h in range(2):
                                sp.dma_start(raw1[D * h:D * h + D, :], ap["w1"]).then_inc(loaded, 16)
                                sp.dma_start(raw3[D * h:D * h + D, :], ap["w3"]).then_inc(loaded, 16)
                            a, b = SPANS["pick1"]
                            sp.dma_start(raw_pick[:, :], ap["const"][0:2 * E1, a:b]).then_inc(loaded, 16)
                            sp.dma_start(w2[:, 0:CH1 - 1, :], ap["w2"][0:128 * (CH1 - 1), :].rearrange("(c p) d -> p c d", p=128)).then_inc(loaded, 16)
                            sp.dma_start(w2[0:LAST1, CH1 - 1, :], ap["w2"][128 * (CH1 - 1):, :]).then_inc(loaded, 16)

                        @block.vector
                        def _(dve):
                            n = [0]
                            dve.wait_ge(loaded, 16 * 7)
                            nc.vector.tensor_copy(pick1[:, :, :].rearrange("p c m -> p (c m)"), raw_pick[:, :])
                            for raw, w in ((raw1, w1), (raw3, w3)):
                                nc.vector.tensor_scalar(raw[:, :], raw[:, :], ln2[:, :], None, ALU.mult).then_inc(prep, 1)
                                n[0] += 1
                                dve.wait_ge(prep, n[0])
                                nc.vector.tensor_copy(w[:, 0, 0:E1 * HID], raw[:, :]).then_inc(prep, 1)
                                n[0] += 1
                                dve.wait_ge(prep, n[0])
                                nc.vector.tensor_tensor(w[:, 1, 0:E1 * HID], raw[:, :], w[:, 0, 0:E1 * HID].bitcast(F32), ALU.subtract)

                LAG, RING = 2, 6
                silu = sbuf(ctx, "e_silu", [128, 2, T2])
                prod = sbuf(ctx, "e_prod", [128, 2, T2])
                hg = sbuf(ctx, "e_hg", [128, RING, T2])
                gf = sbuf(ctx, "e_gf", [HT, 4, 2 * E1])
                gt = sbuf(ctx, "e_gt", [2 * E1, 2, T2], F32R)
                AB, BB, SPB, OUTB = (0, 1), (2, 3), (4, 5), (6, 7)

                def height(c):
                    return LAST1 if c == CH1 - 1 else 128

                with nc.Block() as block:

                    @block.tensor
                    def _(pe):
                        def down(t, u, c):
                            pe.wait_ge(s["gated"].sem, s["gated"].at(t, c))
                            if c == 0:
                                pe.wait_ge(s["added"].sem, s["added"].at(t - 2))
                            n = height(c)
                            for b in range(2):
                                mm = nc.tensor.matmul(bank[OUTB[u]][D * b:D * b + D, 0:T], w2[0:n, c, :],
                                                      hg[0:n, c % RING, b * T:b * T + T],
                                                      start=(c == 0), stop=(c == CH1 - 1))
                            if c == CH1 - 1:
                                mm.then_inc(s["out"].sem, 1)

                        def body(t, u, stages):
                            if 1 in stages:
                                pe.wait_ge(s["gate_fixed"].sem, s["gate_fixed"].at(t))
                                pe.wait_ge(s["gated"].sem, s["gated"].at(t, -2))
                                for n in range(4):
                                    mm = nc.tensor.transpose(bank[SPB[0]][0:2 * E1, n * HT:n * HT + HT], gf[:, n, :],
                                                             table("eye")[0:HT, 0:HT])
                                mm.then_inc(s["gate_rows"].sem, 1)
                            for c in range(CH1):
                                if 1 in stages:
                                    L = (CH1 * u + c) % 2
                                    n = height(c)
                                    pe.wait_ge(s["product"].sem, s["product"].at(t, c - 2))
                                    for to, w in ((AB[L], w1), (BB[L], w3)):
                                        for part in range(2):
                                            nc.tensor.matmul(bank[to][0:n, 0:T2], w[:, part, 128 * c:128 * c + n], xx[:, :, cols(t)],
                                                             start=(part == 0), stop=(part == 1))
                                    if c == 0:
                                        pe.wait_ge(s["gate_out"].sem, s["gate_out"].at(t))
                                    pe.wait_ge(s["gated"].sem, s["gated"].at(t, max(c - 2, -1)))
                                    mm = nc.tensor.matmul(bank[SPB[(c + 1) % 2]][0:n, 0:T2], pick1[:, c, 0:n], gt[:, u, :],
                                                          start=True, stop=True)
                                    mm.then_inc(s["up"].sem, 1)
                                if c < LAG:
                                    if 2 in stages:
                                        down(t - 1, 1 - u, c + CH1 - LAG)
                                elif 1 in stages:
                                    down(t, u, c - LAG)
                        pipelined(pe, TILES, body)

                    @block.scalar
                    def _(act):
                        def body(t, u, stages):
                            if 1 in stages:
                                act.wait_ge(s["gate_rows"].sem, s["gate_rows"].at(t))
                                act.wait_ge(s["up"].sem, s["up"].at(t - 2, CH1 - 1))
                                nc.scalar.copy(gt[:, u, :], bank[SPB[0]][0:2 * E1, 0:T2]).then_inc(s["gate_out"].sem, 1)
                                for c in range(CH1):
                                    n = height(c)
                                    act.wait_ge(s["up"].sem, s["up"].at(t, c))
                                    act.wait_ge(s["product"].sem, s["product"].at(t, c - 2))
                                    L = (CH1 * u + c) % 2
                                    nc.scalar.activation(silu[0:n, L, :], bank[AB[L]][0:n, 0:T2], ACT.Silu).then_inc(s["silu"].sem, 1)
                        pipelined(act, TILES, body)

                    @block.gpsimd
                    def _(pool):
                        flat = gates[:, :, :].rearrange("p n e -> p (n e)")

                        def body(t, u, stages):
                            if 1 in stages:
                                pool.wait_ge(s["gate_rows"].sem, s["gate_rows"].at(t - 1))
                                nc.gpsimd.tensor_copy(gf[:, :, :].rearrange("p n e -> p (n e)"),
                                                      flat[:, bass.ds(t * (8 * E1), 8 * E1)].bitcast(F32)).then_inc(s["gate_fixed"].sem, 1)
                        pipelined(pool, TILES, body)

                    @block.vector
                    def _(dve):
                        def body(t, u, stages):
                            for c in range(CH1):
                                if 1 in stages:
                                    L = (CH1 * u + c) % 2
                                    n = height(c)
                                    dve.wait_ge(s["silu"].sem, s["silu"].at(t, c))
                                    nc.vector.tensor_tensor(prod[0:n, L, :], bank[BB[L]][0:n, 0:T2], silu[0:n, L, :], ALU.mult).then_inc(s["product"].sem, 1)
                                    dve.wait_ge(s["product"].sem, s["product"].at(t, c))
                                    dve.wait_ge(s["up"].sem, s["up"].at(t, c))
                                    nc.vector.tensor_tensor(hg[0:n, c % RING, :], bank[SPB[(c + 1) % 2]][0:n, 0:T2], prod[0:n, L, :], ALU.mult).then_inc(s["gated"].sem, 1)
                                if c == LAG and 2 in stages:
                                    dve.wait_ge(s["out"].sem, s["out"].at(t - 1))
                                    nc.vector.tensor_tensor(resid[:, cols(t - 1)], bank[OUTB[1 - u]][:, 0:T], resid[:, cols(t - 1)], ALU.add).then_inc(s["added"].sem, 1)
                        pipelined(dve, TILES, body)

        def time_mixing(xn):
            s = signals(stacked=1, shifted=1, kv=1, clipped=1, k_exp=1, kv_made=1, r=1, r_exp=1, k_sum=1, den=1, inv=1, wkv=1,
                        rwkv=1, out=1, added=1)

            def cols(t):
                return bass.ds(t * T, T)

            with ExitStack() as ctx:
                st = sbuf(ctx, "t_st", [128, 2, 2, T])
                kc = sbuf(ctx, "t_kc", [HT, 4, D])
                kk = sbuf(ctx, "t_kk", [HT, 2, 2, D])
                kv = sbuf(ctx, "t_kv", [HT, 2, 2, D])
                er = sbuf(ctx, "t_er", [128, T])
                dn = sbuf(ctx, "t_dn", [128, T])
                di = sbuf(ctx, "t_di", [128, T])
                rw = sbuf(ctx, "t_rw", [128, 2, T])
                KVB, RB, SB, WB, OB = (0, 1), 2, 3, 4, 5
                zero_set = plain("t_zero_set")

                with nc.Block() as block:

                    @block.gpsimd
                    def _(pool):
                        nc.gpsimd.memset(st[:, :, :, :], 0.0).then_inc(zero_set, 1)
                        pool.wait_ge(zero_set, 1)

                        def body(t, u, stages):
                            if 0 in stages:
                                pool.wait_ge(s["kv"].sem, s["kv"].at(t - 1))
                                pool.wait_ge(s["r"].sem, s["r"].at(t - 1))
                                for b in range(2):
                                    now = slice(D * b, D * b + D)
                                    last = nc.gpsimd.tensor_copy(st[now, 1 - u, b, :], xn[now, cols(t + 1)])
                                last.then_inc(s["stacked"].sem, 1)
                        pipelined(pool, TILES, body)

                    @block.tensor
                    def _(pe):
                        def body(t, u, stages):
                            if 1 in stages:
                                pe.wait_ge(s["stacked"].sem, s["stacked"].at(t))
                                pe.wait_ge(s["shifted"].sem, s["shifted"].at(t))
                                pe.wait_ge(s["kv_made"].sem, s["kv_made"].at(t - 2))
                                for b in range(2):
                                    for j in range(2):
                                        mm = nc.tensor.matmul(bank[KVB[u]][0:HT, (2 * j + b) * 128:(2 * j + b) * 128 + 128],
                                                              st[:, u, b, HT * j:HT * j + HT], w_kv[:, b, :], start=True, stop=True)
                                mm.then_inc(s["kv"].sem, 1)
                                pe.wait_ge(s["r_exp"].sem, s["r_exp"].at(t - 1))
                                for b in range(2):
                                    mm = nc.tensor.matmul(bank[RB][D * b:D * b + D, 0:T], w_r[:, b, :], st[:, u, b, :],
                                                          start=True, stop=True)
                                mm.then_inc(s["r"].sem, 1)
                            if 2 in stages:
                                pe.wait_ge(s["rwkv"].sem, s["rwkv"].at(t - 1))
                                pe.wait_ge(s["added"].sem, s["added"].at(t - 2))
                                nc.tensor.matmul(bank[OB][:, 0:T], w_o[:, :], rw[:, 1 - u, :], start=True, stop=True).then_inc(s["out"].sem, 1)
                            if 1 in stages:
                                upto = table("upto")
                                pe.wait_ge(s["k_exp"].sem, s["k_exp"].at(t))
                                pe.wait_ge(s["den"].sem, s["den"].at(t - 1))
                                lhs = kk[:, :, :, :].rearrange("p j b d -> p j (b d)")
                                nc.tensor.matmul(bank[SB][:, 0:T], lhs[:, 0, :], upto[0:HT, 0:T], start=True, stop=False)
                                nc.tensor.matmul(bank[SB][:, HT:T], lhs[:, 1, :], upto[0:HT, 0:HT], start=False,
                                                 stop=True).then_inc(s["k_sum"].sem, 1)
                                pe.wait_ge(s["kv_made"].sem, s["kv_made"].at(t))
                                pe.wait_ge(s["rwkv"].sem, s["rwkv"].at(t - 1))
                                lhs = kv[:, :, :, :].rearrange("p j b d -> p j (b d)")
                                nc.tensor.matmul(bank[WB][:, 0:T], lhs[:, 0, :], decay[:, 0:T], start=True, stop=False)
                                nc.tensor.matmul(bank[WB][:, HT:T], lhs[:, 1, :], decay[:, 0:HT], start=False,
                                                 stop=True).then_inc(s["wkv"].sem, 1)
                        pipelined(pe, TILES, body)

                    @block.scalar
                    def _(act):
                        nc.scalar.preload_act_table_set(EXP_LN)

                        def body(t, u, stages):
                            if 1 in stages:
                                act.wait_ge(s["clipped"].sem, s["clipped"].at(t))
                                act.wait_ge(s["k_sum"].sem, s["k_sum"].at(t - 1))
                                act.wait_ge(s["kv_made"].sem, s["kv_made"].at(t - 1))
                                nc.scalar.activation(kk[:, :, :, :].rearrange("p j b d -> p (j b) d"), kc[:, :, :], ACT.Exp).then_inc(s["k_exp"].sem, 1)
                                act.wait_ge(s["r"].sem, s["r"].at(t))
                                act.wait_ge(s["den"].sem, s["den"].at(t - 1))
                                nc.scalar.activation(er[:, :], bank[RB][:, 0:T], ACT.Exp, scale=-1.0).then_inc(s["r_exp"].sem, 1)
                        pipelined(act, TILES, body)

                    @block.vector
                    def _(dve):
                        dve.wait_ge(zero_set, 1)

                        def body(t, u, stages):
                            if 1 in stages:
                                got = bank[KVB[u]][0:HT, :].rearrange("p (n w d) -> p n w d", w=2, d=D)
                                dve.wait_ge(s["kv"].sem, s["kv"].at(t))
                                dve.wait_ge(s["k_exp"].sem, s["k_exp"].at(t - 1))
                                nc.vector.tensor_scalar(kc[:, :, :], got[:, :, 0, :], -60.0, 30.0, ALU.max, ALU.min).then_inc(s["clipped"].sem, 1)
                            if 0 in stages:
                                dve.wait_ge(s["kv"].sem, s["kv"].at(t - 1))
                                dve.wait_ge(s["r"].sem, s["r"].at(t - 1))
                                for b in range(2):
                                    now, before = slice(D * b, D * b + D), slice(D - D * b, 2 * D - D * b)
                                    last = nc.vector.tensor_copy(st[before, 1 - u, b, 1:T], xn[now, bass.ds((t + 1) * T, T - 1)])
                                last.then_inc(s["shifted"].sem, 1)
                            if 1 in stages:
                                dve.wait_ge(s["k_exp"].sem, s["k_exp"].at(t))
                                dve.wait_ge(s["wkv"].sem, s["wkv"].at(t - 1))
                                nc.vector.tensor_tensor(kv[:, :, :, :].rearrange("p j b d -> p (j b) d"), got[:, :, 1, :],
                                                        kk[:, :, :, :].rearrange("p j b d -> p (j b) d"), ALU.mult).then_inc(s["kv_made"].sem, 1)
                            if 2 in stages:
                                dve.wait_ge(s["out"].sem, s["out"].at(t - 1))
                                nc.vector.tensor_tensor(resid[:, cols(t - 1)], bank[OB][:, 0:T], resid[:, cols(t - 1)], ALU.add).then_inc(s["added"].sem, 1)
                            if 1 in stages:
                                dve.wait_ge(s["r_exp"].sem, s["r_exp"].at(t))
                                dve.wait_ge(s["k_sum"].sem, s["k_sum"].at(t))
                                nc.vector.scalar_tensor_tensor(out=dn[:, :], in0=er[:, :], scalar=1.0, in1=bank[SB][:, 0:T],
                                                               op0=ALU.add, op1=ALU.mult).then_inc(s["den"].sem, 1)
                                dve.wait_ge(s["den"].sem, s["den"].at(t))
                                nc.vector.reciprocal(di[:, :], dn[:, :]).then_inc(s["inv"].sem, 1)
                                dve.wait_ge(s["inv"].sem, s["inv"].at(t))
                                dve.wait_ge(s["wkv"].sem, s["wkv"].at(t))
                                dve.wait_ge(s["out"].sem, s["out"].at(t - 2))
                                nc.vector.tensor_tensor(rw[:, u, :], bank[WB][:, 0:T], di[:, :], ALU.mult).then_inc(s["rwkv"].sem, 1)
                        pipelined(dve, TILES, body)

        def softmax_attention(y, xx):
            s = signals(fixed=1, proj=3, turned_q=1, part_k=2, k_summed=1, k_made=1, v=1, v_out=1, scores=HQ, maxed=HQ, less_max=HQ,
                        exped=HQ, att=HQ, att_out=HQ, y_half=1, y_out=1, den=1, den_log=1, den_inv=1, y_normed=1,
                        out=1, y_added=1, added=1)

            def cols(t):
                return bass.ds(t * T, T)

            with ExitStack() as ctx:
                xs = sbuf(ctx, "s_xs", [128, 2, 2, T], F32R)
                qz = sbuf(ctx, "s_qz", [128, 2, 2, T2])
                k1 = sbuf(ctx, "s_k1", [128, 2, T2])
                kr = sbuf(ctx, "s_kr", [128, T2])
                kz = late[:, 0:4 * T2].rearrange("p (u k t) -> p u k t", u=2, k=2)
                va = sbuf(ctx, "s_va", [HT, 2, 4, 2, 32])
                mx = sbuf(ctx, "s_mx", [HT, HQ, 4])
                pr = sbuf(ctx, "s_pr", [HT, HQ, SCORES])
                at = sbuf(ctx, "s_at", [HT, HQ, 2, T + HT])
                ysb = late[:, 4 * T2:5 * T2]
                di = late[:, 5 * T2:6 * T2]
                SC, ATB, YB, M0, M1, OB = (0, 1), (2, 3), 4, 5, 6, 7
                ones_set = plain("s_ones_set")

                def batches(rows):
                    return rows.rearrange("p (b t) -> p b t", b=2)

                def both(name):
                    return table(name).unsqueeze(1).broadcast_to([128, 2, T])

                def halves(rows):
                    return (rows[:, 0:T].rearrange("p (b s) -> p b s", b=2),
                            rows[:, T:SCORES].rearrange("p (b s) -> p b s", b=2))

                with nc.Block() as block:

                    @block.gpsimd
                    def _(pool):
                        nc.gpsimd.memset(va[:, :, :, :, :], 1.0).then_inc(ones_set, 1)

                        def body(t, u, stages):
                            if 0 in stages:
                                pool.wait_ge(s["v"].sem, s["v"].at(t - 1))
                                nc.gpsimd.tensor_copy(xs[:, 1 - u, :, :], xx[:, :, cols(t + 1)]).then_inc(s["fixed"].sem, 1)
                                pool.wait_ge(s["part_k"].sem, s["part_k"].at(t + 1, 1))
                                pool.wait_ge(s["k_made"].sem, s["k_made"].at(t))
                                nc.gpsimd.tensor_tensor(kr[:, :], k1[:, 0, :], k1[:, 1, :], ALU.add).then_inc(s["k_summed"].sem, 1)
                                pool.wait_ge(s["k_summed"].sem, s["k_summed"].at(t + 1))
                                pool.wait_ge(s["scores"].sem, s["scores"].at(t - 1, HQ - 1))
                                for half in range(2):
                                    last = nc.gpsimd.tensor_tensor(kz[:, 1 - u, half, :], kr[:, :],
                                                                   table("key_half")[:, half:half + 1].broadcast_to([128, T2]), ALU.mult)
                                last.then_inc(s["k_made"].sem, 1)
                            if 2 in stages:
                                pool.wait_ge(s["y_added"].sem, s["y_added"].at(t - 1))
                                nc.gpsimd.tensor_tensor(resid[:, cols(t - 1)], resid[:, cols(t - 1)], y[:, cols(t - 1)], ALU.add).then_inc(s["added"].sem, 1)
                        pipelined(pool, TILES, body)

                    @block.tensor
                    def _(pe):
                        def project(t, u, c, to):
                            for part in range(2):
                                mm = nc.tensor.matmul(bank[to][:, 0:T2], w_q[:, part, c, :], xs[:, u, :, :],
                                                      start=(part == 0), stop=(part == 1))
                            mm.then_inc(s["proj"].sem, 1)

                        def scores(t, u, h):
                            if h == 0:
                                pe.wait_ge(s["turned_q"].sem, s["turned_q"].at(t))
                                pe.wait_ge(s["k_made"].sem, s["k_made"].at(t))
                            pe.wait_ge(s["less_max"].sem, s["less_max"].at(t, h - 2))
                            to = bank[SC[h % 2]][0:HT, 0:SCORES]
                            nc.tensor.matmul(to, eye_b[:, :], banned[:, :], start=True, stop=False, skip_group_check=True)
                            for j in range(2):
                                for b in range(2):
                                    w = HT + HT * j
                                    c0 = j * T + b * w
                                    q0 = b * T + j * HT
                                    mm = nc.tensor.matmul(to[:, c0:c0 + w], qz[:, u, h % 2, q0:q0 + HT], kz[:, u, h // 2, b * T:b * T + w],
                                                          start=False, stop=True, skip_group_check=True)
                            mm.then_inc(s["scores"].sem, 1)

                        def turn(t, h):
                            pe.wait_ge(s["exped"].sem, s["exped"].at(t, h))
                            pe.wait_ge(s["att_out"].sem, s["att_out"].at(t, h - 2))
                            for b in range(2):
                                for n, c0 in enumerate((b * HT, T + b * T, T + b * T + HT)):
                                    d0 = b * (T + HT) + n * HT
                                    mm = nc.tensor.transpose(bank[ATB[h % 2]][0:HT, d0:d0 + HT], pr[:, h, c0:c0 + HT],
                                                             table("eye")[0:HT, 0:HT])
                            mm.then_inc(s["att"].sem, 1)

                        def values(t, u):
                            pe.wait_ge(s["att_out"].sem, s["att_out"].at(t, HQ - 1))
                            pe.wait_ge(s["v_out"].sem, s["v_out"].at(t))
                            pe.wait_ge(s["y_out"].sem, s["y_out"].at(t - 1))
                            for b in range(2):
                                for j in range(2):
                                    for h in range(HQ):
                                        mm = nc.tensor.matmul(bank[YB][32 * h:32 * h + 32, b * T + j * HT:b * T + T],
                                                              va[:, u, 2 * b + j, h // 2, :],
                                                              at[:, h, b, j * T:T + j * HT], start=(j == 0), stop=(j == 1))
                            mm.then_inc(s["y_half"].sem, 1)

                        def body(t, u, stages):
                            if 0 in stages:
                                pe.wait_ge(s["fixed"].sem, s["fixed"].at(t + 1))
                                pe.wait_ge(s["part_k"].sem, s["part_k"].at(t, 1))
                                project(t + 1, 1 - u, 0, M0)
                                pe.wait_ge(s["v_out"].sem, s["v_out"].at(t))
                                project(t + 1, 1 - u, 1, M1)
                            if 1 in stages:
                                scores(t, u, 0)
                                scores(t, u, 1)
                            if 2 in stages:
                                turn(t - 1, HQ - 1)
                            if 0 in stages:
                                pe.wait_ge(s["turned_q"].sem, s["turned_q"].at(t + 1))
                                project(t + 1, 1 - u, 2, M0)
                                pe.wait_ge(s["part_k"].sem, s["part_k"].at(t + 1, 0))
                                for b in range(2):
                                    for j in range(2):
                                        for part in range(2):
                                            n = 2 * b + j
                                            mm = nc.tensor.matmul(bank[M1][0:HT, 32 * n:32 * n + 32], xs[:, 1 - u, b, HT * j:HT * j + HT],
                                                                  w_v[:, part, :], start=(part == 0), stop=(part == 1))
                                mm.then_inc(s["v"].sem, 1)
                            if 1 in stages:
                                scores(t, u, 2)
                                turn(t, 0)
                            if 2 in stages:
                                values(t - 1, 1 - u)
                            if 1 in stages:
                                scores(t, u, 3)
                                turn(t, 1)
                            if 2 in stages:
                                pe.wait_ge(s["y_out"].sem, s["y_out"].at(t - 1))
                                pe.wait_ge(s["y_added"].sem, s["y_added"].at(t - 2))
                                nc.tensor.matmul(bank[OB][:, 0:T2], table("den_of_head"), ysb[:, :], start=True, stop=True).then_inc(s["den"].sem, 1)
                            if 1 in stages:
                                turn(t, 2)
                            if 2 in stages:
                                pe.wait_ge(s["y_normed"].sem, s["y_normed"].at(t - 1))
                                for b in range(2):
                                    mm = nc.tensor.matmul(bank[OB][D * b:D * b + D, 0:T], w_ao[:, :], ysb[:, b * T:b * T + T],
                                                          start=True, stop=True)
                                mm.then_inc(s["out"].sem, 1)
                        pe.wait_ge(ones_set, 1)
                        pipelined(pe, TILES, body)

                    @block.scalar
                    def _(act):
                        nc.scalar.preload_act_table_set(EXP_LN)

                        def exp(t, h):
                            act.wait_ge(s["less_max"].sem, s["less_max"].at(t, h))
                            nc.scalar.activation(pr[:, h, :], pr[:, h, :], ACT.Exp).then_inc(s["exped"].sem, 1)

                        def att_out(t, h):
                            act.wait_ge(s["att"].sem, s["att"].at(t, h))
                            act.wait_ge(s["y_half"].sem, s["y_half"].at(t - 1))
                            nc.scalar.copy(at[:, h, :, :].rearrange("p b s -> p (b s)"), bank[ATB[h % 2]][0:HT, 0:SCORES]).then_inc(s["att_out"].sem, 1)

                        def body(t, u, stages):
                            if 1 in stages:
                                exp(t, 0)
                            if 2 in stages:
                                att_out(t - 1, HQ - 1)
                            if 1 in stages:
                                exp(t, 1)
                            if 2 in stages:
                                act.wait_ge(s["y_half"].sem, s["y_half"].at(t - 1))
                                act.wait_ge(s["out"].sem, s["out"].at(t - 2))
                                nc.scalar.copy(ysb[:, :], bank[YB][:, 0:T2]).then_inc(s["y_out"].sem, 1)
                            if 1 in stages:
                                att_out(t, 0)
                                exp(t, 2)
                                att_out(t, 1)
                            if 2 in stages:
                                act.wait_ge(s["den"].sem, s["den"].at(t - 1))
                                act.wait_ge(s["y_normed"].sem, s["y_normed"].at(t - 2))
                                nc.scalar.activation(di[:, :], bank[OB][:, 0:T2], ACT.Ln).then_inc(s["den_log"].sem, 1)
                                act.wait_ge(s["den_log"].sem, s["den_log"].at(t - 1))
                                nc.scalar.activation(di[:, :], di[:, :], ACT.Exp, scale=-1.0).then_inc(s["den_inv"].sem, 1)
                            if 1 in stages:
                                exp(t, 3)
                                att_out(t, 2)
                        pipelined(act, TILES, body)

                    @block.vector
                    def _(dve):
                        dve.wait_ge(ones_set, 1)

                        def soften(t, h):
                            dve.wait_ge(s["scores"].sem, s["scores"].at(t, h))
                            dve.wait_ge(s["less_max"].sem, s["less_max"].at(t - 1, h))
                            dve.wait_ge(s["att"].sem, s["att"].at(t - 1, h))
                            got = halves(bank[SC[h % 2]][0:HT, 0:SCORES])
                            for j in range(2):
                                last = nc.vector.tensor_reduce(mx[:, h, 2 * j:2 * j + 2], got[j], AX.X, ALU.max)
                            last.then_inc(s["maxed"].sem, 1)
                            dve.wait_ge(s["maxed"].sem, s["maxed"].at(t, h))
                            for j in range(2):
                                w = HT + HT * j
                                last = nc.vector.tensor_tensor(halves(pr[:, h, :])[j], got[j],
                                                               mx[:, h, 2 * j:2 * j + 2].unsqueeze(2).broadcast_to([HT, 2, w]),
                                                               ALU.subtract)
                            last.then_inc(s["less_max"].sem, 1)

                        def body(t, u, stages):
                            if 0 in stages:
                                dve.wait_ge(s["proj"].sem, s["proj"].at(t + 1, 0))
                                dve.wait_ge(s["scores"].sem, s["scores"].at(t - 1, HQ - 1))
                                for n in range(2):
                                    last = nc.vector.tensor_tensor(batches(qz[:, 1 - u, n, :]), batches(bank[M0][:, 0:T2]), both(f"rope_q{n}"), ALU.mult)
                                last.then_inc(s["turned_q"].sem, 1)
                                dve.wait_ge(s["proj"].sem, s["proj"].at(t + 1, 1))
                                dve.wait_ge(s["k_summed"].sem, s["k_summed"].at(t))
                                nc.vector.tensor_tensor(batches(k1[:, 0, :]), batches(bank[M1][:, 0:T2]), both("rope_kc"), ALU.mult).then_inc(s["part_k"].sem, 1)
                            if 1 in stages:
                                soften(t, 0)
                                soften(t, 1)
                            if 0 in stages:
                                dve.wait_ge(s["proj"].sem, s["proj"].at(t + 1, 2))
                                nc.vector.tensor_tensor(batches(k1[:, 1, :]), batches(bank[M0][:, 0:T2]), both("rope_ks"), ALU.mult).then_inc(s["part_k"].sem, 1)
                                dve.wait_ge(s["v"].sem, s["v"].at(t + 1))
                                dve.wait_ge(s["y_half"].sem, s["y_half"].at(t - 1))
                                got = bank[M1][0:HT, 0:128].rearrange("p (n g d) -> p n g d", n=4, g=2)
                                nc.vector.tensor_copy(va[:, 1 - u, :, :, 0:HD], got).then_inc(s["v_out"].sem, 1)
                            if 1 in stages:
                                soften(t, 2)
                                soften(t, 3)
                            if 2 in stages:
                                dve.wait_ge(s["den_inv"].sem, s["den_inv"].at(t - 1))
                                nc.vector.tensor_tensor(ysb[:, :], ysb[:, :], di[:, :], ALU.mult).then_inc(s["y_normed"].sem, 1)
                                dve.wait_ge(s["out"].sem, s["out"].at(t - 1))
                                nc.vector.tensor_tensor(y[:, cols(t - 1)], bank[OB][:, 0:T], y[:, cols(t - 1)], ALU.add).then_inc(s["y_added"].sem, 1)
                        pipelined(dve, TILES, body)

        parts = sbuf(stack, "parts", [128, 2, COLS], F32R)
        if stop >= 1:
            norm_pass("n1", resid, xx=parts)
            linear_attention(parts)
        if stop >= 2:
            with ExitStack() as ctx:
                logits0 = sbuf(ctx, "logits0", [HT, P * 4, E0])
                gates0 = sbuf(ctx, "gates0", [HT, P * 4, 2 * E0], F32R)
                norm_pass("n2", resid, xx=parts, router=1, logits=logits0)
                choose_experts("c0", logits0, E0, gates0)
                experts0(parts, gates0)
        if stop >= 3:
            with ExitStack() as ctx:
                normed2 = sbuf(ctx, "normed2", [128, COLS])
                norm_pass("n3", resid, keep=normed2)
                time_mixing(normed2)
        if stop >= 4:
            with ExitStack() as ctx:
                y = sbuf(ctx, "y", [128, COLS])
                norm_pass("n4", resid, twice=True, keep=y, xx=parts)
                softmax_attention(y, parts)
                norm_pass("n5", y, layer_norm=False, xx=parts, router=2, logits=logits1)
            if stop >= 5:
                with ExitStack() as ctx:
                    gates1 = sbuf(ctx, "gates1", [HT, P * 4, 2 * E1], F32R)
                    choose_experts("c1", logits1, E1, gates1)
                    experts1(parts, gates1)

        stored = plain("stored")
        with nc.Block() as block:

            @block.sync
            def _(sp):
                PIECES = 4
                w = COLS // PIECES
                for n in range(PIECES):
                    sp.dma_start(out[:, n * w:(n + 1) * w], resid[:, n * w:(n + 1) * w]).then_inc(stored, 16)
                sp.wait_ge(stored, 16 * PIECES)


def layouts(v):
    import numpy as np

    c = np.ascontiguousarray
    x, txt = v["x"], v["txt"]
    B = x.shape[0]
    out = {
        "x": c(x[:, 0].transpose(1, 0, 2)),
        "txt": c(txt.reshape(B // 2, 2, TXT, D).transpose(1, 3, 0, 2).reshape(128, B // 2, TXT)),
        "const": CONSTS,
        "wtok": c(v["L0_tok_weight"].reshape(PH, PW, D)),
        "btok": v["L0_tok_bias"].reshape(D, 1),
    }
    keys = v["L0_attn_Wks"].transpose(1, 0, 2).reshape(D, H0 * K0)
    queries = v["L0_attn_Wqs"].transpose(1, 0, 2).reshape(D, H0 * K0)
    out["wkq"] = c(np.concatenate([keys, queries], 1))
    out["wvt"] = c(v["L0_attn_Wvs"].transpose(2, 0, 1))
    out["wo0"] = c(v["L0_attn_Wo"].transpose(1, 0, 2))
    out["rw1"] = v["L0_ffn_router_w1"]
    out["rb1"] = v["L0_ffn_router_b1"].reshape(RH0, 1)
    out["rw2"] = v["L0_ffn_router_w2"]
    out["rb2"] = v["L0_ffn_router_b2"].reshape(1, E0)
    out["ew1"] = c(v["L0_ffn_expert_w1"].transpose(1, 0, 2).reshape(D, E0 * EH0))
    out["eb1"] = c(v["L0_ffn_expert_b1"].reshape(3, 128).T)
    out["ew2"] = v["L0_ffn_expert_w2"]
    out["eb2"] = c(v["L0_ffn_expert_b2"].reshape(3, 128).T)
    out["ew3"] = c(v["L0_ffn_expert_w3"].reshape(3, 128, D).transpose(1, 0, 2))
    out["eb3"] = v["L0_ffn_expert_b3"]
    out["wkvr"] = c(np.stack([v["L1_attn_Wk"], v["L1_attn_Wv"], v["L1_attn_Wr"]], 1))
    out["mix"] = c(np.stack([v[f"L1_attn_time_mix_{n}"].reshape(D) for n in "kvr"], 1))
    out["wo1"] = v["L1_attn_Wo"]
    time_w = v["L1_attn_time_w"]
    u, t = np.arange(HT)[:, None], np.arange(T)[None, :]
    out["decay"] = c(time_w[np.clip(time_w.shape[0] - 1 - (t - u), 0, time_w.shape[0] - 1)])
    out["ln1"] = v["L1_ffn_ln1_w"].reshape(D, 1)
    out["ln2"] = v["L1_ffn_ln2_w"].reshape(D, 1)
    swap = (np.arange(HD) + HD // 2) % HD
    q = v["L1_ffn_wq"].reshape(HQ, HD, D)
    k = v["L1_ffn_wk"].reshape(2, HD, D)[np.arange(HQ) // 2]
    q = np.concatenate([q, q[:, swap]], 1)
    k1, k2 = np.concatenate([k, k], 1), np.concatenate([k[:, swap], k[:, swap]], 1)
    out["wq"] = c(np.stack([a.reshape(128, D).T for a in (q, k1, k2)], 1))
    out["wv"] = c(v["L1_ffn_wv"].T)
    out["wao"] = c(v["L1_ffn_wo"].T)
    out["rt"] = c(v["L1_ffn_router_w"].T)
    out["w1"] = c(v["L1_ffn_w1"].reshape(E1 * HID, D).T)
    out["w3"] = c(v["L1_ffn_w3"].reshape(E1 * HID, D).T)
    out["w2"] = c(v["L1_ffn_w2"].transpose(0, 2, 1).reshape(E1 * HID, D))
    return out


def kernel(**inputs):
    import numpy as np
    import concourse.bacc as bacc
    from concourse.bass_utils import run_bass_kernel_spmd

    arrays = layouts({k: np.asarray(a) for k, a in inputs.items()})
    B = inputs["x"].shape[0]
    nc = bacc.Bacc("TRN2", target_bir_lowering=False, num_devices=1)
    ap = {k: nc.dram_tensor(f"in_{k}", a.shape, mybir.dt.from_np(a.dtype), kind="ExternalInput").ap()
          for k, a in arrays.items()}
    out = nc.dram_tensor("out_h", [128, B // 2 * T], F32, kind="ExternalOutput").ap()
    build(nc, ap, out)
    run = run_bass_kernel_spmd(nc, [{f"in_{k}": a for k, a in arrays.items()}], core_ids=[0])
    got = run.results[0]["out_h"]
    return np.ascontiguousarray(got.reshape(2, D, B // 2, T).transpose(2, 0, 3, 1).reshape(B, T, D))
```

```python
from contextlib import ExitStack

import numpy as np

import concourse.bass as bass
from concourse import mybir

F32 = mybir.dt.float32
F32R = mybir.dt.float32r
BF16 = mybir.dt.bfloat16
ALU = mybir.AluOpType
ACT = mybir.ActivationFunctionType
AX = mybir.AxisListType
EXP_LN = "natural_log_exp_and_others"

HEAD = 4
D = 64
IMG = 128
PH, PW, SW = 64, 25, 12
NH, NW = (IMG - PH) // PH + 1, (IMG - PW) // SW + 1
TOK = NH * NW
TXT = 128
T = TOK + TXT
HT = T // 2
T2 = 2 * T
REM = T - 128
LN_EPS, RMS_EPS, ATT_EPS = 1e-5, 1e-6, 1e-9
H0, K0 = 8, 32
E0, EH0, RH0 = 6, 64, 32
HQ, HD = 4, 16
SCORES = 2 * T + T
E1, HID = 8, 170
CH1 = (E1 * HID + 127) // 128
LAST1 = E1 * HID - 128 * (CH1 - 1)


def constants():
    half = np.arange(128) // D
    same = (half[:, None] == half[None, :]).astype(np.float32)
    parts = {}
    parts["mean"] = same / D
    parts["center"] = np.eye(128, dtype=np.float32) - same / D
    head = np.arange(128) // K0
    parts["headsum"] = (head[:, None] == head[None, :]).astype(np.float32)
    t, s = np.arange(128)[:, None], np.arange(T)[None, :]
    main = (s >= t).astype(np.float32)
    row, col = np.arange(128)[:, None], np.arange(2 * REM)[None, :]
    rem = ((row < 2 * REM) & (row // REM == col // REM) & (col % REM >= row % REM)).astype(np.float32)
    parts["causal"] = np.concatenate([main, main, rem, rem], 1)
    u = np.arange(128)[:, None]
    parts["upto"] = ((s >= u) & (u < HT)).astype(np.float32)
    inv = 1.0 / 10000.0 ** (np.arange(0, HD, 2, dtype=np.float32) / HD)
    freqs = np.outer(np.arange(T, dtype=np.float32), inv)
    emb = np.concatenate([freqs, freqs], -1)
    cos, sin = np.cos(emb).T.astype(np.float32), np.sin(emb).T.astype(np.float32)
    rope_q = np.tile(np.concatenate([cos, sin], 0), (HQ, 1))
    for n in range(2):
        parts[f"rope_q{n}"] = rope_q * (np.arange(128)[:, None] // 32 % 2 == n)
    parts["rope_kc"] = np.tile(cos, (2 * HQ, 1))
    parts["rope_ks"] = np.tile(sin, (2 * HQ, 1))
    row, col = np.arange(128)[:, None], np.arange(128)[None, :]
    parts["eye"] = np.eye(128, dtype=np.float32)
    parts["den_of_head"] = (row == 32 * (col // 32) + HD).astype(np.float32)
    parts["slot_bias"] = np.where(np.arange(128)[:, None] // K0 % 2 == np.arange(2)[None, :], 0.0, -1e4).astype(np.float32)
    parts["key_half"] = (np.arange(128)[:, None] // (2 * K0) == np.arange(2)[None, :]).astype(np.float32)
    parts["rank"] = np.tile((E1 - np.arange(E1)).astype(np.float32), (128, 1))
    sign = np.where(np.arange(HD) < HD // 2, -1.0, 1.0)
    ext = np.concatenate([np.ones(HD), sign])
    parts["sign_q"] = np.tile(np.tile(ext, HQ) * HD ** -0.5, (128, 1)).astype(np.float32)
    parts["sign_k2"] = np.tile(np.tile(sign, 2 * HQ), (128, 1)).astype(np.float32)
    ban = np.where(np.arange(HT)[None, :] > np.arange(HT)[:, None], -1e30, 0.0)
    banned = np.zeros((128, SCORES), np.float32)
    for at in (0, HT, T + HT, 2 * T + HT):
        banned[:HT, at:at + HT] = ban
    parts["banned"] = banned
    r = np.arange(128)[:, None]
    c0 = np.arange(3 * 128)[None, :]
    parts["pick0"] = ((r < 2 * E0) & (r % E0 == c0 // EH0)).astype(np.float32)
    c1 = np.arange(CH1 * 128)[None, :]
    parts["pick1"] = ((r < 2 * E1) & (r % E1 == c1 // HID)).astype(np.float32)
    at, spans = 0, {}
    for name, a in parts.items():
        spans[name] = (at, at + a.shape[1])
        at += a.shape[1]
    return np.ascontiguousarray(np.concatenate(list(parts.values()), 1), dtype=np.float32), spans


KEEP = "rank"
CONSTS, SPANS = constants()


class Signal:

    def __init__(self, sem, per):
        self.sem, self.per = sem, per

    def at(self, t, k=0):
        return t * self.per + (self.per * HEAD + k + 1)


def pipelined(eng, tiles, body, last=2, first=0, unroll=2):
    def step(t):
        body(t, t % unroll, [s for s in range(first, last + 1) if 0 <= t + 1 - s < tiles])

    full, rounds = last - 1, (tiles - last + first) // unroll
    for t in range(first - 1, full):
        step(t)
    if rounds > 0:
        with eng.Fori(0, rounds) as k:
            for v in range(unroll):
                body(unroll * k + (full + v), (full + v) % unroll, list(range(first, last + 1)))
    for t in range(full + unroll * rounds, tiles + last - 1):
        step(t)


def build(nc, ap, out, stop=99):
    B = ap["txt"].shape[1] * 2
    P = B // 2
    COLS = P * T
    GB = min(32, B)
    GROUPS = B // GB
    TILES = P
    TILES2 = P // 2

    stack = ExitStack()

    def sbuf(ctx, name, shape, dt=F32):
        return ctx.enter_context(nc.sbuf_tensor(name, shape, dt))

    sems = {}

    def plain(name):
        if name not in sems:
            sems[name] = stack.enter_context(nc.semaphore(name))
        return sems[name]

    def signals(**per):
        made = {name: Signal(plain(name), n) for name, n in per.items()}
        with nc.Block() as block:

            @block.sync
            def _(sp):
                for sig in made.values():
                    sp.sem_clear(sig.sem)
                    sp.sem_inc(sig.sem, sig.per * HEAD)
        return made

    with stack:
        bank = [stack.enter_context(nc.psum_tensor(f"bank{i}", [128, 512], F32)) for i in range(8)]
        resid = sbuf(stack, "resid", [128, COLS])
        keep_w = SPANS[KEEP][1]
        const = sbuf(stack, "const", [128, keep_w])

        def table(name):
            a, b = SPANS[name]
            return const[:, a:b]

        w_kq = sbuf(stack, "w_kq", [128, 2, 4, 128], F32R)
        w_vo = sbuf(stack, "w_vo", [128, H0 // 2, D])
        join = sbuf(stack, "join", [128, D], F32R)
        w_r1 = sbuf(stack, "w_r1", [128, 2, RH0], F32R)
        b_r1 = sbuf(stack, "b_r1", [RH0, 1])
        w_r2 = sbuf(stack, "w_r2", [128, 2 * E0])
        w_e1 = sbuf(stack, "w_e1", [128, 2, 3, 128], F32R)
        b_e1 = sbuf(stack, "b_e1", [128, 3])
        w_e2 = sbuf(stack, "w_e2", [128, 3, 128])
        b_e2 = sbuf(stack, "b_e2", [128, 3])
        w_e3 = sbuf(stack, "w_e3", [128, 3, D])
        b_e3 = sbuf(stack, "b_e3", [2 * E0, D])
        pick0 = sbuf(stack, "pick0", [2 * E0, 3, 128], F32R)
        w_kv = sbuf(stack, "w_kv", [128, 2, 2 * D])
        w_r = sbuf(stack, "w_r", [128, 2, D])
        w_o = sbuf(stack, "w_o", [128, 128])
        decay = sbuf(stack, "decay", [HT, T])
        w_q = sbuf(stack, "w_q", [128, 2, 3, 128], F32R)
        w_v = sbuf(stack, "w_v", [128, 2, 32], F32R)
        w_ao = sbuf(stack, "w_ao", [128, D])
        w_rt = sbuf(stack, "w_rt", [128, 2 * E1])
        ln1 = sbuf(stack, "ln1", [128, 1])
        ln2 = sbuf(stack, "ln2", [128, 1])
        banned = sbuf(stack, "banned", [128, SCORES], BF16)
        eye_b = sbuf(stack, "eye_b", [128, HT], BF16)
        eps = sbuf(stack, "eps", [128, 3])
        ln_eps, rms_eps, att_eps = (eps[:, n:n + 1] for n in range(3))
        late = sbuf(stack, "late", [128, max(P * 4 * E1, 6 * T2)])
        logits1 = late[0:HT, 0:P * 4 * E1].rearrange("p (n e) -> p n e", e=E1)

        with ExitStack() as ctx:
            image = sbuf(ctx, "image", [128, B, IMG])
            w_tok = sbuf(ctx, "w_tok", [128, PW, 128])
            b_tok = sbuf(ctx, "b_tok", [128, 1])
            raw_kq = sbuf(ctx, "raw_kq", [128, 512])
            raw_vt = sbuf(ctx, "raw_vt", [D, H0, D])
            raw_o = sbuf(ctx, "raw_o", [D, H0, D])
            raw_r1 = sbuf(ctx, "raw_r1", [128, RH0])
            raw_e1 = sbuf(ctx, "raw_e1", [128, 384])
            raw_kvr = sbuf(ctx, "raw_kvr", [128, 3, D])
            mix = sbuf(ctx, "mix", [128, 3])
            unmix = sbuf(ctx, "unmix", [128, 3])
            raw_decay = sbuf(ctx, "raw_decay", [HT, T])
            raw_q = sbuf(ctx, "raw_q", [128, 3, 128])
            raw_q2 = sbuf(ctx, "raw_q2", [128, 3, 128])
            raw_v = sbuf(ctx, "raw_v", [128, 32])
            raw_v2 = sbuf(ctx, "raw_v2", [128, 32])
            raw_rt = sbuf(ctx, "raw_rt", [128, E1])
            spare = sbuf(ctx, "spare", [128, CONSTS.shape[1] - keep_w])

            def spare_table(name):
                a, b = SPANS[name]
                return spare[:, a - keep_w:b - keep_w]

            image_in = [plain(f"image_in{g}") for g in range(GROUPS)]
            text_in = plain("text_in")
            tok_w_in = plain("tok_w_in")
            small_in = plain("small_in")
            zeroed = plain("zeroed")
            tokens = plain("tokens")
            gelu_done = plain("gelu_done")
            vo_done = plain("vo_done")
            prep = plain("prep")

            small = []

            def load_small():
                twice = [
                    (raw_kq, "wkq"), (raw_r1, "rw1"), (raw_e1, "ew1"), (mix, "mix"), (raw_v, "wv"),
                    (raw_rt, "rt"), (ln1, "ln1"), (ln2, "ln2"), (b_tok, "btok"),
                ]
                for h in range(2):
                    rows = slice(D * h, D * h + D)
                    small.extend((dst[rows, :], ap[src]) for dst, src in twice)
                    small.append((raw_kvr[rows, :, :], ap["wkvr"]))
                    small.append((raw_q[rows, :, :], ap["wq"]))
                    small.append((w_o[rows, D * h:D * h + D], ap["wo1"]))
                    small.append((w_r2[D * h:D * h + RH0, E0 * h:E0 * h + E0], ap["rw2"]))
                    small.append((w_r2[D * h + RH0:D * h + RH0 + 1, E0 * h:E0 * h + E0], ap["rb2"]))
                for e in range(E0):
                    rows = slice(D * (e % 2), D * (e % 2) + D)
                    small.append((w_e2[rows, e // 2, D * (e % 2):D * (e % 2) + D], ap["ew2"][e]))
                for h in range(HQ):
                    small.append((w_ao[32 * h:32 * h + HD, :], ap["wao"][HD * h:HD * h + HD, :]))
                small.extend([
                    (const[:, :], ap["const"][:, 0:keep_w]), (spare[:, :], ap["const"][:, keep_w:]),
                    (raw_vt[:, :, :], ap["wvt"]), (raw_o[:, :, :], ap["wo0"]),
                    (b_r1[:, :], ap["rb1"]), 
                    (b_e1[:, :], ap["eb1"]), (b_e2[:, :], ap["eb2"]), (w_e3[:, :, :], ap["ew3"]),
                    (b_e3[0:E0, :], ap["eb3"]), (b_e3[E0:2 * E0, :], ap["eb3"]),
                    (raw_decay[:, :], ap["decay"]),
                ])

            load_small()
            SMALL = 16 * len(small)

            with nc.Block() as block:

                @block.sync
                def _(sp):
                    sp.wait_ge(zeroed, 1)
                    for h in range(2):
                        sp.dma_start(w_tok[D * h:D * h + D, :, D * h:D * h + D], ap["wtok"]).then_inc(tok_w_in, 16)
                    for g in range(GROUPS):
                        sp.dma_start(image[:, g * GB:(g + 1) * GB, :], ap["x"][:, g * GB:(g + 1) * GB, :]).then_inc(image_in[g], 16)
                    stream = resid[:, :].rearrange("c (p t) -> c p t", t=T)
                    sp.dma_start(stream[:, :, TOK:T], ap["txt"]).then_inc(text_in, 16)
                    sp.wait_ge(text_in, 16)

                @block.gpsimd
                def _(pool):
                    nc.gpsimd.memset(w_tok[:, :, :], 0.0).then_inc(zeroed, 1)
                    nc.gpsimd.memset(ln_eps, LN_EPS)
                    nc.gpsimd.memset(rms_eps, RMS_EPS)
                    nc.gpsimd.memset(att_eps, ATT_EPS)
                    nc.gpsimd.memset(w_e2[:, :, :], 0.0)
                    nc.gpsimd.memset(w_o[:, :], 0.0)
                    nc.gpsimd.memset(w_ao[:, :], 0.0)
                    nc.gpsimd.memset(w_r2[:, :], 0.0)
                    nc.gpsimd.memset(w_rt[:, :], 0.0).then_inc(zeroed, 1)

                @block.scalar
                def _(act):
                    act.wait_ge(zeroed, 2)
                    for dst, src in small:
                        act.dma_start(dst, src).then_inc(small_in, 16)
                    act.wait_ge(small_in, SMALL)
                    stream = resid[:, :].rearrange("c (p t) -> c p t", t=T)
                    for g in range(GROUPS):
                        act.wait_ge(tokens, g + 1)
                        got = bank[g][:, 0:GB * NW].rearrange("c (p two w) -> c p two w", two=2, w=NW)
                        for r in range(NH):
                            for odd in range(2):
                                nc.scalar.activation(
                                    stream[D * odd:D * odd + D, g * GB // 2:(g + 1) * GB // 2, r * NW:r * NW + NW],
                                    got[D * r:D * r + D, :, odd, :], ACT.Gelu,
                                    bias=b_tok[D * r:D * r + D, :],
                                ).then_inc(gelu_done, 1)

                @block.tensor
                def _(pe):
                    pe.wait_ge(tok_w_in, 32)
                    for g in range(GROUPS):
                        pe.wait_ge(image_in[g], 16)
                        for j in range(PW):
                            mm = nc.tensor.matmul(
                                bank[g][:, 0:GB * NW], w_tok[:, j, :],
                                image[:, g * GB:(g + 1) * GB, j:j + SW * (NW - 1) + 1:SW],
                                start=(j == 0), stop=(j == PW - 1))
                        mm.then_inc(tokens, 1)
                    pe.wait_ge(small_in, SMALL)
                    for h in range(H0):
                        rows = slice(D * (h % 2), D * (h % 2) + D)
                        mm = nc.tensor.matmul(bank[7][rows, D * (h // 2):D * (h // 2) + D], raw_vt[:, h, :],
                                              raw_o[:, h, :], start=True, stop=True)
                    mm.then_inc(vo_done, 1)

                @block.vector
                def _(dve):
                    count = [0]

                    def step(ins):
                        ins.then_inc(prep, 1)
                        count[0] += 1
                        return count[0]

                    def split(dst, src):
                        n = step(nc.vector.tensor_copy(dst[:, 0], src))
                        dve.wait_ge(prep, n)
                        step(nc.vector.tensor_tensor(dst[:, 1], src, dst[:, 0].bitcast(F32), ALU.subtract))

                    dve.wait_ge(small_in, SMALL)
                    split(w_kq[:, :, :, :].rearrange("p s c m -> p s (c m)"), raw_kq[:, :])
                    split(w_r1[:, :, :], raw_r1[:, :])
                    split(w_e1[:, :, :, :].rearrange("p s c m -> p s (c m)"), raw_e1[:, :])
                    step(nc.vector.tensor_copy(pick0[:, :, :].rearrange("p c m -> p (c m)"), spare_table("pick0")[0:2 * E0, :]))
                    for h in range(2):
                        rows = slice(D * h, D * h + D)
                        step(nc.vector.tensor_copy(join[rows, :], table("eye")[rows, rows]))
                    step(nc.vector.tensor_copy(banned[:, :], spare_table("banned")))
                    step(nc.vector.tensor_copy(eye_b[:, :], table("eye")[:, 0:HT]))
                    step(nc.vector.tensor_tensor(decay[:, :], raw_decay[:, :], table("upto")[0:HT, :], ALU.mult))
                    n = step(nc.vector.tensor_scalar(unmix[:, :], mix[:, :], -1.0, 1.0, ALU.mult, ALU.add))
                    dve.wait_ge(prep, n)
                    for odd in range(2):
                        now, before = slice(D * odd, D * odd + D), slice(D - D * odd, 2 * D - D * odd)
                        for rows, by in ((now, mix), (before, unmix)):
                            for n in range(3):
                                dst = w_r[rows, odd, :] if n == 2 else w_kv[rows, odd, D * n:D * n + D]
                                step(nc.vector.tensor_scalar(dst, raw_kvr[rows, n, :], by[rows, n:n + 1], None, ALU.mult))
                    step(nc.vector.tensor_tensor(raw_q2[:, 0, :], raw_q[:, 0, :], spare_table("sign_q"), ALU.mult))
                    step(nc.vector.tensor_copy(raw_q2[:, 1, :], raw_q[:, 1, :]))
                    n = step(nc.vector.tensor_tensor(raw_q2[:, 2, :], raw_q[:, 2, :], spare_table("sign_k2"), ALU.mult))
                    dve.wait_ge(prep, n)
                    step(nc.vector.tensor_scalar(raw_q[:, :, :], raw_q2[:, :, :], ln1[:, :], None, ALU.mult))
                    n = step(nc.vector.tensor_scalar(raw_v2[:, :], raw_v[:, :], ln1[:, :], None, ALU.mult))
                    dve.wait_ge(prep, n)
                    split(w_q[:, :, :, :].rearrange("p s c m -> p s (c m)"), raw_q[:, :, :].rearrange("p c m -> p (c m)"))
                    split(w_v[:, :, :], raw_v2[:, :])
                    dve.wait_ge(zeroed, 2)
                    for h in range(2):
                        rows = slice(D * h, D * h + D)
                        step(nc.vector.tensor_scalar(w_rt[rows, E1 * h:E1 * h + E1], raw_rt[rows, :], ln2[rows, :], None, ALU.mult))
                    dve.wait_ge(vo_done, 1)
                    step(nc.vector.tensor_copy(w_vo[:, :, :].rearrange("p g m -> p (g m)"), bank[7][:, 0:D * H0 // 2]))
                    dve.wait_ge(prep, count[0])

        def norm_pass(tag, src, layer_norm=True, twice=False, keep=None, xx=None, router=0, logits=None):
            W = T2
            E = E0 if router == 1 else E1
            READY = 2 if twice else 1
            LAST = {0: READY + 1 if xx is not None else READY, 1: 5, 2: 3}[router]
            s = signals(centred=1, squared=1, summed=1, logged=1, scaled=1, normed=1, even_hi_made=1, odd_hi_made=1, parted=1,
                        var_scaled=1, mean_square=1, rms_logged=1, rms_scaled=1, rms_normed=1, hidden=1,
                        relued=1, odd_relued=1, scored=1, logits_out=1)
            ones_set = plain(f"{tag}_ones_set")

            def cols(t):
                return bass.ds(t * W, W)

            with ExitStack() as ctx:
                sq = sbuf(ctx, f"{tag}_sq", [128, 2, W])
                lg = sbuf(ctx, f"{tag}_lg", [128, 2, W])
                rstd = sbuf(ctx, f"{tag}_rstd", [128, 2, W])
                if keep is None:
                    xn = sbuf(ctx, f"{tag}_xn", [128, 2, W])
                if twice:
                    half_ms = sbuf(ctx, f"{tag}_half_ms", [128, W])
                    ms = sbuf(ctx, f"{tag}_ms", [128, 2, W])
                    lg2 = sbuf(ctx, f"{tag}_lg2", [128, 2, W])
                    rms = sbuf(ctx, f"{tag}_rms", [128, 2, W])
                    hn = sbuf(ctx, f"{tag}_hn", [128, 2, W])
                if router == 1:
                    rh = sbuf(ctx, f"{tag}_rh", [128, 2, W])

                RING = 3 if router == 1 else 4
                UNROLL = 2 * RING if RING % 2 else RING
                SUM, HIDDEN = (RING, RING + 1), (5, 6)
                SCORE = (7, 7) if router == 1 else (6, 7)

                def scores(u):
                    return bank[SCORE[u]][0:HT, 0:8 * E]


                def result(t, u):
                    if twice:
                        return hn[:, u, :]
                    return keep[:, cols(t)] if keep is not None else xn[:, u, :]

                result_ready = s["rms_normed"] if twice else s["normed"]

                with nc.Block() as block:

                    @block.tensor
                    def _(pe):
                        def body(t, slot, stages):
                            u = slot % 2
                            if 1 in stages:
                                pe.wait_ge(s["squared"].sem, s["squared"].at(t))
                                bank_read = s["var_scaled"] if twice else s["logged"]
                                pe.wait_ge(bank_read.sem, bank_read.at(t - 2))
                                nc.tensor.matmul(bank[SUM[u]][:, 0:W], table("mean"), sq[:, u, :],
                                                 start=True, stop=True).then_inc(s["summed"].sem, 1)
                            if -1 in stages and layer_norm:
                                pe.wait_ge(s["normed"].sem, s["normed"].at(t + 2 - RING))
                                nc.tensor.matmul(bank[(slot + 2) % RING][:, 0:W], table("center"), src[:, cols(t + 2)],
                                                 start=True, stop=True).then_inc(s["centred"].sem, 1)
                            if 3 in stages and router == 1:
                                pe.wait_ge(s["parted"].sem, s["parted"].at(t - 2))
                                pe.wait_ge(s["relued"].sem, s["relued"].at(t - 3))
                                pe.wait_ge(s["odd_relued"].sem, s["odd_relued"].at(t - 3))
                                for b in range(2):
                                    for part in range(2):
                                        mm = nc.tensor.matmul(bank[HIDDEN[b]][0:RH0, 0:W], w_r1[:, part, :],
                                                              xx[:, b, cols(t - 2)], start=(part == 0), stop=(part == 1))
                                mm.then_inc(s["hidden"].sem, 1)
                            if 4 in stages and router == 1:
                                pe.wait_ge(s["relued"].sem, s["relued"].at(t - 3))
                                pe.wait_ge(s["odd_relued"].sem, s["odd_relued"].at(t - 3))
                                pe.wait_ge(s["logits_out"].sem, s["logits_out"].at(t - 4))
                                for n in range(4):
                                    mm = nc.tensor.matmul(scores(1 - u)[:, n * 2 * E:(n + 1) * 2 * E],
                                                          rh[:, 1 - u, n * HT:n * HT + HT], w_r2[:, :], start=True, stop=True)
                                mm.then_inc(s["scored"].sem, 1)
                            if 2 in stages and router == 2:
                                pe.wait_ge(s["normed"].sem, s["normed"].at(t - 1))
                                pe.wait_ge(s["logits_out"].sem, s["logits_out"].at(t - 3))
                                for n in range(4):
                                    mm = nc.tensor.matmul(scores(1 - u)[:, n * 2 * E:(n + 1) * 2 * E],
                                                          xn[:, 1 - u, n * HT:n * HT + HT], w_rt[:, :], start=True, stop=True)
                                mm.then_inc(s["scored"].sem, 1)

                        if router == 1:
                            pe.wait_ge(ones_set, 3)
                        pipelined(pe, TILES2, body, LAST, first=-1, unroll=UNROLL)

                    @block.scalar
                    def _(act):
                        nc.scalar.preload_act_table_set(EXP_LN)
                        if router == 1:
                            act.wait_ge(ones_set, 3)

                        def body(t, slot, stages):
                            u = slot % 2
                            if 0 in stages:
                                act.wait_ge(s["summed"].sem, s["summed"].at(t - 1))
                                if layer_norm:
                                    act.wait_ge(s["centred"].sem, s["centred"].at(t + 1))
                                got = bank[(slot + 1) % RING][:, 0:W] if layer_norm else src[:, cols(t + 1)]
                                nc.scalar.activation(sq[:, 1 - u, :], got, ACT.Square).then_inc(s["squared"].sem, 1)
                            if READY + 1 in stages and router == 2:
                                r, ru = t - READY, (u - READY) % 2
                                act.wait_ge(result_ready.sem, result_ready.at(r))
                                nc.scalar.copy(xx[0:D, 0, cols(r)], result(r, ru)[0:D, :]).then_inc(s["even_hi_made"].sem, 1)
                            if 1 in stages:
                                act.wait_ge(s["summed"].sem, s["summed"].at(t))
                                act.wait_ge(s["scaled"].sem, s["scaled"].at(t - 2))
                                nc.scalar.activation(lg[:, u, :], bank[SUM[u]][:, 0:W], ACT.Ln,
                                                     bias=ln_eps if layer_norm else rms_eps).then_inc(s["logged"].sem, 1)
                            if 1 in stages:
                                act.wait_ge(s["logged"].sem, s["logged"].at(t))
                                rstd_read = s["mean_square"] if twice else s["normed"]
                                act.wait_ge(rstd_read.sem, rstd_read.at(t - 2))
                                nc.scalar.activation(rstd[:, u, :], lg[:, u, :], ACT.Exp, scale=-0.5).then_inc(s["scaled"].sem, 1)
                            if 2 in stages and twice:
                                act.wait_ge(s["mean_square"].sem, s["mean_square"].at(t - 1))
                                act.wait_ge(s["rms_scaled"].sem, s["rms_scaled"].at(t - 3))
                                nc.scalar.activation(lg2[:, 1 - u, :], ms[:, 1 - u, :], ACT.Ln, bias=rms_eps).then_inc(s["rms_logged"].sem, 1)
                                act.wait_ge(s["rms_logged"].sem, s["rms_logged"].at(t - 1))
                                act.wait_ge(s["rms_normed"].sem, s["rms_normed"].at(t - 3))
                                nc.scalar.activation(rms[:, 1 - u, :], lg2[:, 1 - u, :], ACT.Exp, scale=-0.5).then_inc(s["rms_scaled"].sem, 1)
                            if 3 in stages and router == 1:
                                act.wait_ge(s["hidden"].sem, s["hidden"].at(t - 2))
                                act.wait_ge(s["scored"].sem, s["scored"].at(t - 4))
                                nc.scalar.activation(rh[D:D + RH0, u, :], bank[HIDDEN[1]][0:RH0, 0:W], ACT.Relu,
                                                     bias=b_r1[:, :]).then_inc(s["odd_relued"].sem, 1)
                        pipelined(act, TILES2, body, LAST, first=-1, unroll=UNROLL)

                    @block.gpsimd
                    def _(pool):
                        if router == 1:
                            nc.gpsimd.memset(rh[:, :, :], 0.0).then_inc(ones_set, 1)
                            pool.wait_ge(ones_set, 1)
                            for at in (RH0, D + RH0):
                                nc.gpsimd.memset(rh[at:at + 1, :, :], 1.0).then_inc(ones_set, 1)

                        def body(t, slot, stages):
                            u = slot % 2
                            if READY in stages:
                                r, ru = t + 1 - READY, (u + 1 - READY) % 2
                                pool.wait_ge(result_ready.sem, result_ready.at(r))
                                nc.gpsimd.tensor_copy(xx[D:2 * D, 1, cols(r)], result(r, ru)[D:2 * D, :]).then_inc(s["odd_hi_made"].sem, 1)
                        if xx is not None:
                            pipelined(pool, TILES2, body, LAST, first=-1, unroll=UNROLL)

                    @block.vector
                    def _(dve):
                        if router == 1:
                            dve.wait_ge(ones_set, 3)

                        def body(t, slot, stages):
                            u = slot % 2
                            if LAST in stages and router:
                                r = t + 1 - LAST
                                dve.wait_ge(s["scored"].sem, s["scored"].at(r))
                                flat = logits[:, :, :].rearrange("p n e -> p (n e)")
                                for q in range(2):
                                    dst = flat[:, bass.ds(r * (8 * E) + q * 4 * E, 4 * E)].rearrange("p (b j e) -> p j b e", b=2, j=2)
                                    got = scores((u + 1 - LAST) % 2)[:, q * 4 * E:(q + 1) * 4 * E].rearrange("p (j b e) -> p j b e", b=2, j=2)
                                    last = nc.vector.tensor_copy(dst, got)
                                last.then_inc(s["logits_out"].sem, 1)
                            if 1 in stages:
                                dve.wait_ge(s["scaled"].sem, s["scaled"].at(t))
                                if router == 2:
                                    dve.wait_ge(s["scored"].sem, s["scored"].at(t - 2))
                                if xx is not None and keep is None:
                                    dve.wait_ge(s["parted"].sem, s["parted"].at(t - 2))
                                first = bank[slot % RING][:, 0:W] if layer_norm else src[:, cols(t)]
                                dst = keep[:, cols(t)] if keep is not None else xn[:, u, :]
                                nc.vector.tensor_tensor(dst, first, rstd[:, u, :], ALU.mult).then_inc(s["normed"].sem, 1)
                            if 1 in stages and twice:
                                dve.wait_ge(s["mean_square"].sem, s["mean_square"].at(t - 1))
                                nc.vector.tensor_tensor(half_ms[:, :], bank[SUM[u]][:, 0:W], rstd[:, u, :],
                                                        ALU.mult).then_inc(s["var_scaled"].sem, 1)
                                dve.wait_ge(s["var_scaled"].sem, s["var_scaled"].at(t))
                                dve.wait_ge(s["rms_logged"].sem, s["rms_logged"].at(t - 2))
                                nc.vector.tensor_tensor(ms[:, u, :], half_ms[:, :], rstd[:, u, :],
                                                        ALU.mult).then_inc(s["mean_square"].sem, 1)
                            if 2 in stages and twice:
                                dve.wait_ge(s["rms_scaled"].sem, s["rms_scaled"].at(t - 1))
                                dve.wait_ge(s["normed"].sem, s["normed"].at(t - 1))
                                dve.wait_ge(s["parted"].sem, s["parted"].at(t - 3))
                                nc.vector.tensor_tensor(hn[:, 1 - u, :], keep[:, cols(t - 1)], rms[:, 1 - u, :], ALU.mult).then_inc(s["rms_normed"].sem, 1)
                            if READY + 1 in stages and xx is not None:
                                r, ru = t - READY, (u - READY) % 2
                                dve.wait_ge(result_ready.sem, result_ready.at(r))
                                dve.wait_ge(s["even_hi_made"].sem, s["even_hi_made"].at(r))
                                dve.wait_ge(s["odd_hi_made"].sem, s["odd_hi_made"].at(r))
                                for b in range(2):
                                    hi, lo = slice(D * b, D * b + D), slice(D - D * b, 2 * D - D * b)
                                    last = nc.vector.tensor_tensor(xx[lo, b, cols(r)], result(r, ru)[hi, :],
                                                                   xx[hi, b, cols(r)].bitcast(F32), ALU.subtract)
                                last.then_inc(s["parted"].sem, 1)
                            if READY in stages and xx is not None and router != 2:
                                r, ru = t + 1 - READY, (u + 1 - READY) % 2
                                dve.wait_ge(result_ready.sem, result_ready.at(r))
                                nc.vector.tensor_copy(xx[0:D, 0, cols(r)], result(r, ru)[0:D, :]).then_inc(s["even_hi_made"].sem, 1)
                            if 3 in stages and router == 1:
                                dve.wait_ge(s["hidden"].sem, s["hidden"].at(t - 2))
                                dve.wait_ge(s["scored"].sem, s["scored"].at(t - 4))
                                nc.vector.tensor_scalar(rh[0:RH0, u, :], bank[HIDDEN[0]][0:RH0, 0:W],
                                                        b_r1[:, :], 0.0, ALU.add, ALU.max).then_inc(s["relued"].sem, 1)
                            if 1 in stages and not layer_norm:
                                nc.vector.tensor_tensor(resid[:, cols(t)], resid[:, cols(t)], src[:, cols(t)], ALU.add)
                        pipelined(dve, TILES2, body, LAST, first=-1, unroll=UNROLL)

        def linear_attention(xx):
            s = signals(turned=1, rows_out=1, kq=4, kq_neg=4, kq_exp=4, kq_elu=4, k_made=2, key_sum=2, qk=2, fixed=1, den=2, den_log=2,
                        den_inv=2, q_normed=2, scores=8, masked=8, mixed=4, mixed_out=4, out=1, added=1)

            def cols(t, n=T):
                return bass.ds(t * T, n)

            with ExitStack() as ctx:
                xl = sbuf(ctx, "a_xl", [128, 2, T], F32R)
                xt = sbuf(ctx, "a_xt", [128, 2, 3, D])
                ek = sbuf(ctx, "a_ek", [128, 2, T2])
                xr = sbuf(ctx, "a_xr", [128, 128], F32R)
                kr = sbuf(ctx, "a_kr", [128, 2, 2, 2, 128])
                neg = sbuf(ctx, "a_neg", [128, 2, T2])
                restart = sbuf(ctx, "a_restart", [128, T2])
                ones_set, zeroed = plain("a_ones_set"), plain("a_zeroed")
                k = sbuf(ctx, "a_k", [128, 2, T2])
                kz = sbuf(ctx, "a_kz", [128, 2, 2, 2, T2])
                q = sbuf(ctx, "a_q", [128, 2, T2])
                ksum = sbuf(ctx, "a_ksum", [128, 2, T2])
                qk = sbuf(ctx, "a_qk", [128, 2, T2])
                dl = sbuf(ctx, "a_dl", [128, 2, T2])
                di = sbuf(ctx, "a_di", [128, 2, 2, T2])
                qn = sbuf(ctx, "a_qn", [128, 2, 2, 2, T2])
                sc = sbuf(ctx, "a_sc", [128, 4, T2 + 4 * REM])
                gs = sbuf(ctx, "a_gs", [128, 2, H0 // 2, T2])
                SCB, GB_, PB = (0, 1), (2, 3), (4, 5)

                def batches(rows):
                    return rows.rearrange("p (b t) -> p b t", b=2)

                with nc.Block() as block:

                    @block.tensor
                    def _(pe):
                        def scores(t, u, h):
                            c, ks, qs = h // 4, h % 4 // 2, h % 2
                            if h % 4 == 0:
                                pe.wait_ge(s["k_made"].sem, s["k_made"].at(t, c))
                            pe.wait_ge(s["q_normed"].sem, s["q_normed"].at(t, c))
                            pe.wait_ge(s["masked"].sem, s["masked"].at(t, h - 2))
                            to = bank[SCB[h % 2]]
                            for b in range(2):
                                mm = nc.tensor.matmul(to[:, b * T:b * T + T], kz[:, u, c, ks, b * T:b * T + 128],
                                                 qn[:, u, c, qs, b * T:b * T + T], start=True, stop=True)
                            if qs == 0:
                                mm = nc.tensor.matmul(to[:, T2:T2 + 4 * REM], kr[:, u, c, ks, :],
                                                      qn[:, u, c, :, :].rearrange("p n (b t) -> p n b t", b=2)[:, :, :, 128:T],
                                                      start=True, stop=True)
                            mm.then_inc(s["scores"].sem, 1)

                        def mixtures(t, u, g):
                            if g == 0:
                                pe.wait_ge(s["rows_out"].sem, s["rows_out"].at(t))
                            pe.wait_ge(s["masked"].sem, s["masked"].at(t, 2 * g + 1))
                            pe.wait_ge(s["mixed_out"].sem, s["mixed_out"].at(t, g - 2))
                            to = bank[GB_[g % 2]]
                            for b in range(2):
                                for hh in range(2):
                                    nc.tensor.matmul(to[D * hh:D * hh + D, b * T:b * T + T], xt[:, u, b, :],
                                                     sc[:, (2 * g + hh) % 4, b * T:b * T + T], start=(b == 0), stop=False,
                                                     skip_group_check=True)
                            for hh in range(2):
                                mm = nc.tensor.matmul(batches(to[D * hh:D * hh + D, 0:T2])[:, :, 128:T], xt[:, u, 2, :],
                                                      sc[:, 2 * g % 4, T2 + 2 * REM * hh:T2 + 2 * REM * hh + 2 * REM], start=False, stop=True,
                                                      skip_group_check=True)
                            mm.then_inc(s["mixed"].sem, 1)

                        def project(t, c):
                            if c < 2:
                                pe.wait_ge(s["den_log"].sem, s["den_log"].at(t - 1, c))
                            pe.wait_ge(s["kq_elu"].sem, s["kq_elu"].at(t, c - 2))
                            for part in range(2):
                                mm = nc.tensor.matmul(bank[PB[c % 2]][:, 0:T2], w_kq[:, part, c, :], xx[:, :, cols(t)],
                                                      start=(part == 0), stop=(part == 1))
                            mm.then_inc(s["kq"].sem, 1)

                        def denominators(t, c):
                            pe.wait_ge(s["qk"].sem, s["qk"].at(t, c))
                            nc.tensor.matmul(bank[PB[c]][:, 0:T2], table("headsum"), qk[:, c, :],
                                             start=True, stop=True).then_inc(s["den"].sem, 1)

                        def body(t, u, stages):
                            if 0 in stages:
                                project(t + 1, 0)
                                project(t + 1, 1)
                            if 2 in stages:
                                mixtures(t - 1, 1 - u, 3)
                            if 1 in stages:
                                scores(t, u, 0)
                                scores(t, u, 1)
                            if 2 in stages:
                                pe.wait_ge(s["added"].sem, s["added"].at(t - 2))
                                pe.wait_ge(s["mixed_out"].sem, s["mixed_out"].at(t - 1, 3))
                                for g in range(4):
                                    for b in range(2):
                                        mm = nc.tensor.matmul(bank[7][D * b:D * b + D, 0:T], w_vo[:, g, :],
                                                              gs[:, 1 - u, g, b * T:b * T + T], start=(g == 0), stop=(g == 3))
                                mm.then_inc(s["out"].sem, 1)
                            if 1 in stages:
                                scores(t, u, 2)
                            if 0 in stages:
                                project(t + 1, 2)
                            if 1 in stages:
                                mixtures(t, u, 0)
                                scores(t, u, 3)
                            if 0 in stages:
                                pe.wait_ge(s["fixed"].sem, s["fixed"].at(t + 1))
                                pe.wait_ge(s["rows_out"].sem, s["rows_out"].at(t))
                                for n, tokens in enumerate((xl[:, 0, 0:128], xl[:, 1, 0:128], xr[:, :])):
                                    mm = nc.tensor.matmul(bank[6][:, D * n:D * n + D], tokens, join[:, :], start=True, stop=True)
                                mm.then_inc(s["turned"].sem, 1)
                                project(t + 1, 3)
                            if 1 in stages:
                                scores(t, u, 4)
                                mixtures(t, u, 1)
                                scores(t, u, 5)
                            if 0 in stages:
                                denominators(t + 1, 0)
                            if 1 in stages:
                                scores(t, u, 6)
                            if 0 in stages:
                                denominators(t + 1, 1)
                            if 1 in stages:
                                mixtures(t, u, 2)
                                scores(t, u, 7)
                        pipelined(pe, TILES, body)

                    @block.scalar
                    def _(act):
                        nc.scalar.preload_act_table_set(EXP_LN)

                        def mixed_out(t, u, g):
                            act.wait_ge(s["mixed"].sem, s["mixed"].at(t, g))
                            if g == 0:
                                act.wait_ge(s["out"].sem, s["out"].at(t - 2))
                            nc.scalar.copy(gs[:, u, g, :], bank[GB_[g % 2]][:, 0:T2]).then_inc(s["mixed_out"].sem, 1)

                        def exp(t, c):
                            act.wait_ge(s["kq"].sem, s["kq"].at(t, c))
                            act.wait_ge(s["kq_exp"].sem, s["kq_exp"].at(t, c - 2))
                            nc.scalar.activation(neg[:, c % 2, :], bank[PB[c % 2]][:, 0:T2], ACT.Relu, scale=-1.0).then_inc(s["kq_neg"].sem, 1)
                            act.wait_ge(s["kq_neg"].sem, s["kq_neg"].at(t, c))
                            act.wait_ge(s["kq_elu"].sem, s["kq_elu"].at(t, c - 2))
                            nc.scalar.activation(ek[:, c % 2, :], neg[:, c % 2, :], ACT.Exp, scale=-1.0).then_inc(s["kq_exp"].sem, 1)

                        def body(t, u, stages):
                            if 0 in stages:
                                exp(t + 1, 0)
                            if 2 in stages:
                                mixed_out(t - 1, 1 - u, 3)
                            if 0 in stages:
                                exp(t + 1, 1)
                            if 0 in stages:
                                exp(t + 1, 2)
                            if 1 in stages:
                                mixed_out(t, u, 0)
                            if 0 in stages:
                                exp(t + 1, 3)
                            if 1 in stages:
                                mixed_out(t, u, 1)
                            if 0 in stages:
                                for c in range(2):
                                    act.wait_ge(s["den"].sem, s["den"].at(t + 1, c))
                                    nc.scalar.activation(dl[:, c, :], bank[PB[c]][:, 0:T2], ACT.Ln, bias=att_eps).then_inc(s["den_log"].sem, 1)
                                    act.wait_ge(s["den_log"].sem, s["den_log"].at(t + 1, c))
                                    act.wait_ge(s["q_normed"].sem, s["q_normed"].at(t, c))
                                    for slot in range(2):
                                        last = nc.scalar.activation(di[:, c, slot, :], dl[:, c, :], ACT.Exp, scale=-1.0,
                                                                    bias=table("slot_bias")[:, slot:slot + 1])
                                    last.then_inc(s["den_inv"].sem, 1)
                            if 1 in stages:
                                mixed_out(t, u, 2)
                        pipelined(act, TILES, body)

                    @block.gpsimd
                    def _(pool):
                        nc.gpsimd.memset(kr[:, :, :, :, :], 0.0)
                        nc.gpsimd.memset(xr[:, :].bitcast(F32), 0.0).then_inc(zeroed, 1)
                        pool.wait_ge(zeroed, 1)
                        nc.gpsimd.memset(restart[:, 1:T], 1.0)
                        nc.gpsimd.memset(restart[:, T + 1:T2], 1.0)
                        nc.gpsimd.memset(restart[:, 0:T + 1:T], 0.0).then_inc(ones_set, 1)

                        def body(t, u, stages):
                            if 0 in stages:
                                pool.wait_ge(s["turned"].sem, s["turned"].at(t))
                                nc.gpsimd.tensor_copy(xr[:, 0:2 * REM].rearrange("p (b t) -> p b t", b=2), xx[:, :, bass.ds((t + 1) * T + 128, REM)])
                                nc.gpsimd.tensor_copy(xl[:, :, :], xx[:, :, cols(t + 1)]).then_inc(s["fixed"].sem, 1)
                                for c in range(2):
                                    pool.wait_ge(s["kq_elu"].sem, s["kq_elu"].at(t + 1, c))
                                    pool.wait_ge(s["scores"].sem, s["scores"].at(t - 1, 7))
                                    for half in range(2):
                                        last = nc.gpsimd.tensor_tensor(kz[:, 1 - u, c, half, :], k[:, c, :],
                                                                       table("key_half")[:, half:half + 1].broadcast_to([128, T2]), ALU.mult)
                                    last.then_inc(s["k_made"].sem, 1)
                                for c in range(2):
                                    pool.wait_ge(s["den_inv"].sem, s["den_inv"].at(t + 1, c))
                                    pool.wait_ge(s["kq_elu"].sem, s["kq_elu"].at(t + 1, c + 2))
                                    pool.wait_ge(s["scores"].sem, s["scores"].at(t - 1, 7))
                                    for slot in range(2):
                                        last = nc.gpsimd.tensor_tensor(qn[:, 1 - u, c, slot, :], q[:, c, :], di[:, c, slot, :], ALU.mult)
                                    last.then_inc(s["q_normed"].sem, 1)
                        pipelined(pool, TILES, body)

                    @block.vector
                    def _(dve):
                        dve.wait_ge(ones_set, 1)

                        def mask(t, u, h):
                            dve.wait_ge(s["scores"].sem, s["scores"].at(t, h))
                            dve.wait_ge(s["mixed"].sem, s["mixed"].at(t, h // 2 - 2))
                            w = T2 + (4 * REM if h % 2 == 0 else 0)
                            nc.vector.tensor_tensor(sc[:, h % 4, 0:w], bank[SCB[h % 2]][:, 0:w], table("causal")[:, 0:w], ALU.mult).then_inc(s["masked"].sem, 1)

                        def elu(t, u, c):
                            dve.wait_ge(s["kq_exp"].sem, s["kq_exp"].at(t, c))
                            if c < 2:
                                dve.wait_ge(s["k_made"].sem, s["k_made"].at(t - 1, c))
                                dve.wait_ge(s["key_sum"].sem, s["key_sum"].at(t - 1, c))
                                dve.wait_ge(s["scores"].sem, s["scores"].at(t - 2, 7))
                            else:
                                dve.wait_ge(s["q_normed"].sem, s["q_normed"].at(t - 1, c - 2))
                            dst = k[:, c, :] if c < 2 else q[:, c - 2, :]
                            nc.vector.scalar_tensor_tensor(out=dst, in0=bank[PB[c % 2]][:, 0:T2], scalar=1.0, in1=ek[:, c % 2, :],
                                                           op0=ALU.add, op1=ALU.max).then_inc(s["kq_elu"].sem, 1)

                        def keys(t, u, c):
                            elu(t, u, c)
                            dve.wait_ge(s["kq_elu"].sem, s["kq_elu"].at(t, c))
                            for half in range(2):
                                nc.vector.tensor_scalar(batches(kr[:, u, c, half, 0:2 * REM]), batches(k[:, c, :])[:, :, 128:T],
                                                        table("key_half")[:, half:half + 1], None, ALU.mult)
                            nc.vector.tensor_tensor_scan(ksum[:, c, :], restart[:, :], k[:, c, :], 0.0,
                                                         op0=ALU.mult, op1=ALU.add).then_inc(s["key_sum"].sem, 1)

                        def queries(t, u, c):
                            elu(t, u, c + 2)
                            dve.wait_ge(s["kq_elu"].sem, s["kq_elu"].at(t, c + 2))
                            dve.wait_ge(s["key_sum"].sem, s["key_sum"].at(t, c))
                            dve.wait_ge(s["den"].sem, s["den"].at(t - 1, c))
                            nc.vector.tensor_tensor(qk[:, c, :], q[:, c, :], ksum[:, c, :], ALU.mult).then_inc(s["qk"].sem, 1)

                        def body(t, u, stages):
                            if 1 in stages:
                                mask(t, u, 0)
                            if 0 in stages:
                                keys(t + 1, 1 - u, 0)
                            if 1 in stages:
                                mask(t, u, 1)
                            if 0 in stages:
                                keys(t + 1, 1 - u, 1)
                            if 1 in stages:
                                mask(t, u, 2)
                            if 1 in stages:
                                mask(t, u, 3)
                            if 0 in stages:
                                queries(t + 1, 1 - u, 0)
                            if 1 in stages:
                                mask(t, u, 4)
                            if 0 in stages:
                                queries(t + 1, 1 - u, 1)
                            if 1 in stages:
                                mask(t, u, 5)
                            if 2 in stages:
                                dve.wait_ge(s["out"].sem, s["out"].at(t - 1))
                                nc.vector.tensor_tensor(resid[:, cols(t - 1)], bank[7][:, 0:T], resid[:, cols(t - 1)], ALU.add).then_inc(s["added"].sem, 1)
                            if 1 in stages:
                                mask(t, u, 6)
                            if 0 in stages:
                                dve.wait_ge(s["turned"].sem, s["turned"].at(t + 1))
                                dve.wait_ge(s["mixed"].sem, s["mixed"].at(t - 1, 3))
                                nc.vector.tensor_copy(xt[:, 1 - u, :, :].rearrange("p w c -> p (w c)"), bank[6][:, 0:3 * D]).then_inc(s["rows_out"].sem, 1)
                            if 1 in stages:
                                mask(t, u, 7)
                        pipelined(dve, TILES, body)

        def choose_experts(tag, logits, E, gates, weights=None):
            N = P * 4
            made = plain(f"{tag}_chosen")
            exp_done = plain(f"{tag}_exp_done")
            gap_made = plain(f"{tag}_gap_made")

            with ExitStack() as ctx:
                prob = logits
                one = sbuf(ctx, f"{tag}_one", [HT, N, E])
                two = sbuf(ctx, f"{tag}_two", [HT, N, E])
                if weights:
                    assert CH1 * 128 <= SPANS["eye"][0]
                    raw = const[:, 0:CH1 * 128]
                top = sbuf(ctx, f"{tag}_top", [HT, 6, N])

                def wide(row):
                    return top[:, row, :].unsqueeze(2).broadcast_to([HT, N, E])

                rank = table("rank")[0:HT, 0:E].unsqueeze(1).broadcast_to([HT, N, E])
                BEST, SECOND, GAP, W1, W2, TMP = range(6)

                loaded, scaled, hi_made, lo_made = (plain(f"{tag}_{n}") for n in ("loaded", "scaled", "hi_made", "lo_made"))
                w2_in = plain(f"{tag}_w2_in")

                with nc.Block() as block:

                    @block.sync
                    def _(sp):
                        if weights:
                            w1, w3, w2 = weights
                            sp.dma_start(w2[:, 0:CH1 - 1, :], ap["w2"][0:128 * (CH1 - 1), :].rearrange("(c p) d -> p c d", p=128)).then_inc(w2_in, 16)
                            sp.dma_start(w2[0:LAST1, CH1 - 1, :], ap["w2"][128 * (CH1 - 1):, :]).then_inc(w2_in, 16)
                            for n, name in enumerate(("w1", "w3")):
                                if n:
                                    sp.wait_ge(lo_made, n)
                                for h in range(2):
                                    sp.dma_start(raw[D * h:D * h + D, 0:E1 * HID], ap[name]).then_inc(loaded, 16)
                            sp.wait_ge(lo_made, 2)
                            a, b = SPANS["pick1"]
                            sp.dma_start(raw[0:2 * E1, :], ap["const"][0:2 * E1, a:b]).then_inc(loaded, 16)
                            sp.wait_ge(w2_in, 32)
                            sp.wait_ge(loaded, 80)

                    @block.gpsimd
                    def _(pool):
                        if weights:
                            for n, w in enumerate(weights[0:2]):
                                pool.wait_ge(hi_made, n + 1)
                                nc.gpsimd.tensor_tensor(w[:, 1, 0:E1 * HID], raw[:, 0:E1 * HID], w[:, 0, 0:E1 * HID].bitcast(F32), ALU.subtract).then_inc(lo_made, 1)
                            pool.wait_ge(lo_made, 2)

                    @block.scalar
                    def _(act):
                        nc.scalar.preload_act_table_set(EXP_LN)
                        act.wait_ge(made, 2)
                        nc.scalar.activation(prob[:, :, :], prob[:, :, :], ACT.Exp).then_inc(exp_done, 1)
                        if E == E0:
                            act.wait_ge(gap_made, 1)
                            nc.scalar.activation(top[:, W2, :], top[:, GAP, :], ACT.Exp).then_inc(exp_done, 1)
                        if weights:
                            for n, w in enumerate(weights[0:2]):
                                act.wait_ge(loaded, 32 * (n + 1))
                                nc.scalar.activation(raw[:, 0:E1 * HID], raw[:, 0:E1 * HID], ACT.Copy, scale=ln2[:, :]).then_inc(scaled, 1)
                                act.wait_ge(scaled, n + 1)
                                nc.scalar.copy(w[:, 0, 0:E1 * HID], raw[:, 0:E1 * HID]).then_inc(hi_made, 1)
                            act.wait_ge(hi_made, 2)

                    @block.vector
                    def _(dve):
                        count = [0]

                        def chain(ins):
                            ins.then_inc(made, 1)
                            count[0] += 1
                            dve.wait_ge(made, count[0])

                        def tt(dst, a, b, op):
                            chain(nc.vector.tensor_tensor(dst, a, b, op))

                        def first_of(onehot, row):
                            tt(onehot, prob[:, :, :], wide(row), ALU.is_ge)
                            tt(onehot, onehot, rank, ALU.mult)
                            chain(nc.vector.tensor_reduce(top[:, TMP, :], onehot, AX.X, ALU.max))
                            tt(onehot, onehot, wide(TMP), ALU.is_equal)

                        chain(nc.vector.tensor_reduce(top[:, TMP, :], logits[:, :, :], AX.X, ALU.max))
                        tt(prob[:, :, :], logits[:, :, :], wide(TMP), ALU.subtract)
                        dve.wait_ge(exp_done, 1)
                        chain(nc.vector.tensor_reduce(top[:, TMP, :], prob[:, :, :], AX.X, ALU.add))
                        chain(nc.vector.reciprocal(top[:, GAP, :], top[:, TMP, :]))
                        tt(prob[:, :, :], prob[:, :, :], wide(GAP), ALU.mult)
                        chain(nc.vector.tensor_reduce(top[:, BEST, :], prob[:, :, :], AX.X, ALU.max))
                        first_of(one[:, :, :], BEST)
                        chain(nc.vector.scalar_tensor_tensor(out=prob[:, :, :], in0=one[:, :, :], scalar=-2.0,
                                                             in1=prob[:, :, :], op0=ALU.mult, op1=ALU.add))
                        chain(nc.vector.tensor_reduce(top[:, SECOND, :], prob[:, :, :], AX.X, ALU.max))
                        first_of(two[:, :, :], SECOND)
                        if E == E0:
                            nc.vector.tensor_tensor(top[:, GAP, :], top[:, SECOND, :], top[:, BEST, :],
                                                    ALU.subtract).then_inc(gap_made, 1)
                            dve.wait_ge(exp_done, 2)
                            chain(nc.vector.tensor_scalar(top[:, TMP, :], top[:, W2, :], 1.0, None, ALU.add))
                            chain(nc.vector.reciprocal(top[:, W1, :], top[:, TMP, :]))
                            tt(top[:, W2, :], top[:, W2, :], top[:, W1, :], ALU.mult)
                        else:
                            tt(top[:, TMP, :], top[:, BEST, :], top[:, SECOND, :], ALU.add)
                            chain(nc.vector.tensor_scalar(top[:, TMP, :], top[:, TMP, :], ATT_EPS, None, ALU.add))
                            chain(nc.vector.reciprocal(top[:, GAP, :], top[:, TMP, :]))
                            tt(top[:, W1, :], top[:, BEST, :], top[:, GAP, :], ALU.mult)
                            tt(top[:, W2, :], top[:, SECOND, :], top[:, GAP, :], ALU.mult)
                        tt(one[:, :, :], one[:, :, :], wide(W1), ALU.mult)
                        tt(two[:, :, :], two[:, :, :], wide(W2), ALU.mult)
                        tt(one[:, :, :], one[:, :, :], two[:, :, :], ALU.add)
                        chain(nc.vector.tensor_copy(gates[:, :, 0:E], one[:, :, :]))
                        tt(gates[:, :, E:2 * E], one[:, :, :], gates[:, :, 0:E].bitcast(F32), ALU.subtract)

        def experts0(xx, gates):
            s = signals(gate_fixed=1, gate_rows=1, gate_out=1, h1=3, h1_out=3, h2=3, h2_out=3, spread=3, gated=3, out=1, added=1)
            CH = E0 // 2

            def cols(t):
                return bass.ds(t * T, T)

            with ExitStack() as ctx:
                h1 = sbuf(ctx, "m_h1", [128, 2, CH, T2])
                h2 = sbuf(ctx, "m_h2", [128, CH, T2])
                hg = sbuf(ctx, "m_hg", [128, 2, CH, T2])
                gf = sbuf(ctx, "m_gf", [HT, 4, 2 * E0])
                gt = sbuf(ctx, "m_gt", [2 * E0, 2, T2], F32R)
                H1B, H2B, GTB, OUTB = (0, 1), (2, 3), 6, 7
                SPB = (4, 5)

                def slot(u, c):
                    return (CH * u + c) % 2

                with nc.Block() as block:

                    @block.tensor
                    def _(pe):
                        def first(t, u, c):
                            pe.wait_ge(s["h1_out"].sem, s["h1_out"].at(t, c - 2))
                            for part in range(2):
                                mm = nc.tensor.matmul(bank[H1B[slot(u, c)]][:, 0:T2], w_e1[:, part, c, :], xx[:, :, cols(t)],
                                                      start=(part == 0), stop=(part == 1))
                            mm.then_inc(s["h1"].sem, 1)

                        def body(t, u, stages):
                            for c in range(CH):
                                if 1 in stages:
                                    pe.wait_ge(s["h1_out"].sem, s["h1_out"].at(t, c))
                                    pe.wait_ge(s["h2_out"].sem, s["h2_out"].at(t, c - 2))
                                    nc.tensor.matmul(bank[H2B[slot(u, c)]][:, 0:T2], w_e2[:, c, :], h1[:, u, c, :],
                                                     start=True, stop=True).then_inc(s["h2"].sem, 1)
                                    pe.wait_ge(s["gate_out"].sem, s["gate_out"].at(t))
                                    pe.wait_ge(s["gated"].sem, s["gated"].at(t, c - 2))
                                    nc.tensor.matmul(bank[SPB[slot(u, c)]][:, 0:T2], pick0[:, c, :], gt[:, u, :],
                                                     start=True, stop=True).then_inc(s["spread"].sem, 1)
                                if 0 in stages:
                                    first(t + 1, 1 - u, c)
                                if 0 in stages and c == 0:
                                    pe.wait_ge(s["gate_fixed"].sem, s["gate_fixed"].at(t + 1))
                                    pe.wait_ge(s["gate_out"].sem, s["gate_out"].at(t))
                                    for n in range(4):
                                        mm = nc.tensor.transpose(bank[GTB][0:2 * E0, n * HT:n * HT + HT], gf[:, n, :],
                                                                 table("eye")[0:HT, 0:HT])
                                    mm.then_inc(s["gate_rows"].sem, 1)
                                if 2 in stages and c == 0:
                                    pe.wait_ge(s["added"].sem, s["added"].at(t - 2))
                                    pe.wait_ge(s["gated"].sem, s["gated"].at(t - 1, CH - 1))
                                    for g in range(CH):
                                        for b in range(2):
                                            nc.tensor.matmul(bank[OUTB][D * b:D * b + D, 0:T], w_e3[:, g, :],
                                                             hg[:, 1 - u, g, b * T:b * T + T], start=(g == 0), stop=False)
                                    for b in range(2):
                                        mm = nc.tensor.matmul(bank[OUTB][D * b:D * b + D, 0:T], b_e3[:, :],
                                                              gt[:, 1 - u, b * T:b * T + T].bitcast(F32), start=False, stop=True)
                                    mm.then_inc(s["out"].sem, 1)
                        pipelined(pe, TILES, body)

                    @block.scalar
                    def _(act):
                        def body(t, u, stages):
                            for c in range(CH):
                                if 1 in stages:
                                    act.wait_ge(s["h2"].sem, s["h2"].at(t, c))
                                    act.wait_ge(s["gated"].sem, s["gated"].at(t, c - CH))
                                    nc.scalar.activation(h2[:, c, :], bank[H2B[slot(u, c)]][:, 0:T2], ACT.Relu,
                                                         bias=b_e2[:, c:c + 1]).then_inc(s["h2_out"].sem, 1)
                                if 0 in stages:
                                    act.wait_ge(s["h1"].sem, s["h1"].at(t + 1, c))
                                    act.wait_ge(s["h2"].sem, s["h2"].at(t - 1, c))
                                    nc.scalar.activation(h1[:, 1 - u, c, :], bank[H1B[slot(1 - u, c)]][:, 0:T2], ACT.Relu,
                                                         bias=b_e1[:, c:c + 1]).then_inc(s["h1_out"].sem, 1)
                                if 0 in stages and c == 0:
                                    act.wait_ge(s["gate_rows"].sem, s["gate_rows"].at(t + 1))
                                    act.wait_ge(s["out"].sem, s["out"].at(t - 1))
                                    nc.scalar.copy(gt[:, 1 - u, :], bank[GTB][0:2 * E0, 0:T2]).then_inc(s["gate_out"].sem, 1)
                        pipelined(act, TILES, body)

                    @block.gpsimd
                    def _(pool):
                        flat = gates[:, :, :].rearrange("p n e -> p (n e)")

                        def body(t, u, stages):
                            if 0 in stages:
                                pool.wait_ge(s["gate_rows"].sem, s["gate_rows"].at(t))
                                nc.gpsimd.tensor_copy(gf[:, :, :].rearrange("p n e -> p (n e)"),
                                                      flat[:, bass.ds((t + 1) * (8 * E0), 8 * E0)].bitcast(F32)).then_inc(s["gate_fixed"].sem, 1)
                        pipelined(pool, TILES, body)

                    @block.vector
                    def _(dve):
                        def body(t, u, stages):
                            for c in range(CH):
                                if 1 in stages:
                                    dve.wait_ge(s["h2_out"].sem, s["h2_out"].at(t, c))
                                    dve.wait_ge(s["spread"].sem, s["spread"].at(t, c))
                                    dve.wait_ge(s["out"].sem, s["out"].at(t - 2))
                                    nc.vector.tensor_tensor(hg[:, u, c, :], bank[SPB[slot(u, c)]][:, 0:T2], h2[:, c, :], ALU.mult).then_inc(s["gated"].sem, 1)
                                if 2 in stages and c == 0:
                                    dve.wait_ge(s["out"].sem, s["out"].at(t - 1))
                                    nc.vector.tensor_tensor(resid[:, cols(t - 1)], bank[OUTB][:, 0:T], resid[:, cols(t - 1)], ALU.add).then_inc(s["added"].sem, 1)
                        pipelined(dve, TILES, body)

        def experts1(xx, gates, weights):
            s = signals(gate_fixed=1, gate_rows=1, gate_out=1, up=CH1, silu=CH1, product=CH1, gated=CH1, out=1, added=1)

            def cols(t):
                return bass.ds(t * T, T)

            with ExitStack() as ctx:
                w1, w3, w2 = weights
                pick1 = sbuf(ctx, "e_pick", [2 * E1, CH1, 128], F32R)
                pick_made = plain("e_pick_made")
                LAG, RING = 2, 6
                silu = sbuf(ctx, "e_silu", [128, 2, T2])
                prod = sbuf(ctx, "e_prod", [128, 2, T2])
                hg = sbuf(ctx, "e_hg", [128, RING, T2])
                gf = sbuf(ctx, "e_gf", [HT, 4, 2 * E1])
                gt = sbuf(ctx, "e_gt", [2 * E1, 2, T2], F32R)
                AB, BB, SPB, OUTB = (0, 1), (2, 3), (4, 5), (6, 7)

                def height(c):
                    return LAST1 if c == CH1 - 1 else 128

                with nc.Block() as block:

                    @block.scalar
                    def _(act):
                        nc.scalar.copy(pick1[:, :, :].rearrange("p c m -> p (c m)"), const[0:2 * E1, 0:CH1 * 128]).then_inc(pick_made, 1)
                        act.wait_ge(pick_made, 1)

                with nc.Block() as block:

                    @block.sync
                    def _(sp):
                        n = P // PIECES
                        for piece in range(PIECES):
                            sp.wait_ge(s["added"].sem, s["added"].at((piece + 1) * n - 1))
                            at = slice(piece * n * T, (piece + 1) * n * T)
                            sp.dma_start(out[:, at], resid[:, at]).then_inc(stored, 16)
                        sp.wait_ge(stored, 16 * PIECES)

                    @block.tensor
                    def _(pe):
                        def down(t, u, c):
                            pe.wait_ge(s["gated"].sem, s["gated"].at(t, c))
                            n = height(c)
                            for b in range(2):
                                mm = nc.tensor.matmul(bank[OUTB[u]][D * b:D * b + D, 0:T], w2[0:n, c, :],
                                                      hg[0:n, c % RING, b * T:b * T + T],
                                                      start=(c == 0), stop=(c == CH1 - 1))
                            if c == CH1 - 1:
                                mm.then_inc(s["out"].sem, 1)

                        def body(t, u, stages):
                            for c in range(CH1):
                                if 0 in stages and c == CH1 // 2:
                                    pe.wait_ge(s["gate_fixed"].sem, s["gate_fixed"].at(t + 1))
                                    pe.wait_ge(s["added"].sem, s["added"].at(t - 1))
                                    for n in range(4):
                                        mm = nc.tensor.transpose(bank[OUTB[1 - u]][0:2 * E1, n * HT:n * HT + HT], gf[:, n, :],
                                                                 table("eye")[0:HT, 0:HT])
                                    mm.then_inc(s["gate_rows"].sem, 1)
                                if 1 in stages:
                                    L = (CH1 * u + c) % 2
                                    n = height(c)
                                    pe.wait_ge(s["product"].sem, s["product"].at(t, c - 2))
                                    for to, w in ((AB[L], w1), (BB[L], w3)):
                                        for part in range(2):
                                            nc.tensor.matmul(bank[to][0:n, 0:T2], w[:, part, 128 * c:128 * c + n], xx[:, :, cols(t)],
                                                             start=(part == 0), stop=(part == 1))
                                    if c == 0:
                                        pe.wait_ge(s["gate_out"].sem, s["gate_out"].at(t))
                                    pe.wait_ge(s["gated"].sem, s["gated"].at(t, c - 2))
                                    mm = nc.tensor.matmul(bank[SPB[L]][0:n, 0:T2], pick1[:, c, 0:n], gt[:, u, :],
                                                          start=True, stop=True)
                                    mm.then_inc(s["up"].sem, 1)
                                if c < LAG:
                                    if 2 in stages:
                                        down(t - 1, 1 - u, c + CH1 - LAG)
                                elif 1 in stages:
                                    down(t, u, c - LAG)
                        pipelined(pe, TILES, body)

                    @block.scalar
                    def _(act):
                        def body(t, u, stages):
                            for c in range(CH1):
                                if 0 in stages and c == CH1 // 2:
                                    act.wait_ge(s["gate_rows"].sem, s["gate_rows"].at(t + 1))
                                    act.wait_ge(s["up"].sem, s["up"].at(t - 1, CH1 - 1))
                                    nc.scalar.copy(gt[:, 1 - u, :], bank[OUTB[1 - u]][0:2 * E1, 0:T2]).then_inc(s["gate_out"].sem, 1)
                                if 1 in stages:
                                    n = height(c)
                                    L = (CH1 * u + c) % 2
                                    act.wait_ge(s["up"].sem, s["up"].at(t, c))
                                    act.wait_ge(s["product"].sem, s["product"].at(t, c - 2))
                                    nc.scalar.activation(silu[0:n, L, :], bank[AB[L]][0:n, 0:T2], ACT.Silu).then_inc(s["silu"].sem, 1)
                        pipelined(act, TILES, body)

                    @block.gpsimd
                    def _(pool):
                        flat = gates[:, :, :].rearrange("p n e -> p (n e)")

                        def body(t, u, stages):
                            if 0 in stages:
                                pool.wait_ge(s["gate_rows"].sem, s["gate_rows"].at(t))
                                nc.gpsimd.tensor_copy(gf[:, :, :].rearrange("p n e -> p (n e)"),
                                                      flat[:, bass.ds((t + 1) * (8 * E1), 8 * E1)].bitcast(F32)).then_inc(s["gate_fixed"].sem, 1)
                        pipelined(pool, TILES, body)

                    @block.vector
                    def _(dve):
                        def body(t, u, stages):
                            for c in range(CH1):
                                if 1 in stages:
                                    L = (CH1 * u + c) % 2
                                    n = height(c)
                                    dve.wait_ge(s["silu"].sem, s["silu"].at(t, c))
                                    nc.vector.tensor_tensor(prod[0:n, L, :], bank[BB[L]][0:n, 0:T2], silu[0:n, L, :], ALU.mult).then_inc(s["product"].sem, 1)
                                    dve.wait_ge(s["product"].sem, s["product"].at(t, c))
                                    dve.wait_ge(s["up"].sem, s["up"].at(t, c))
                                    nc.vector.tensor_tensor(hg[0:n, c % RING, :], bank[SPB[L]][0:n, 0:T2], prod[0:n, L, :], ALU.mult).then_inc(s["gated"].sem, 1)
                                if c == LAG and 2 in stages:
                                    dve.wait_ge(s["out"].sem, s["out"].at(t - 1))
                                    nc.vector.tensor_tensor(resid[:, cols(t - 1)], bank[OUTB[1 - u]][:, 0:T], resid[:, cols(t - 1)], ALU.add).then_inc(s["added"].sem, 1)
                        pipelined(dve, TILES, body)

        def time_mixing(xn):
            s = signals(stacked=1, shifted=1, kv=1, clipped=1, k_exp=1, kv_made=1, r=1, r_exp=1, k_sum=1, den=1, inv=1, wkv=1,
                        rwkv=1, out=1, added=1)

            def cols(t):
                return bass.ds(t * T, T)

            with ExitStack() as ctx:
                st = sbuf(ctx, "t_st", [128, 2, 2, T])
                kc = sbuf(ctx, "t_kc", [HT, 4, D])
                kk = sbuf(ctx, "t_kk", [HT, 2, 2, D])
                kv = sbuf(ctx, "t_kv", [HT, 2, 2, D])
                er = sbuf(ctx, "t_er", [128, T])
                dn = sbuf(ctx, "t_dn", [128, T])
                di = sbuf(ctx, "t_di", [128, T])
                rw = sbuf(ctx, "t_rw", [128, 2, T])
                KVB, RB, SB, WB, OB = (0, 1), 2, 3, 4, 5
                zero_set = plain("t_zero_set")

                with nc.Block() as block:

                    @block.gpsimd
                    def _(pool):
                        nc.gpsimd.memset(st[:, :, :, :], 0.0).then_inc(zero_set, 1)
                        pool.wait_ge(zero_set, 1)

                        def body(t, u, stages):
                            if 0 in stages:
                                pool.wait_ge(s["kv"].sem, s["kv"].at(t - 1))
                                pool.wait_ge(s["r"].sem, s["r"].at(t - 1))
                                for b in range(2):
                                    now = slice(D * b, D * b + D)
                                    last = nc.gpsimd.tensor_copy(st[now, 1 - u, b, :], xn[now, cols(t + 1)])
                                last.then_inc(s["stacked"].sem, 1)
                        pipelined(pool, TILES, body, 3)

                    @block.tensor
                    def _(pe):
                        upto = table("upto")

                        def body(t, u, stages):
                            if 1 in stages:
                                pe.wait_ge(s["stacked"].sem, s["stacked"].at(t))
                                pe.wait_ge(s["shifted"].sem, s["shifted"].at(t))
                                pe.wait_ge(s["kv_made"].sem, s["kv_made"].at(t - 2))
                                for b in range(2):
                                    for j in range(2):
                                        mm = nc.tensor.matmul(bank[KVB[u]][0:HT, (2 * j + b) * 128:(2 * j + b) * 128 + 128],
                                                              st[:, u, b, HT * j:HT * j + HT], w_kv[:, b, :], start=True, stop=True)
                                mm.then_inc(s["kv"].sem, 1)
                            if 2 in stages:
                                pe.wait_ge(s["k_exp"].sem, s["k_exp"].at(t - 1))
                                pe.wait_ge(s["den"].sem, s["den"].at(t - 2))
                                lhs = kk[:, :, :, :].rearrange("p j b d -> p j (b d)")
                                nc.tensor.matmul(bank[SB][:, 0:T], lhs[:, 0, :], upto[0:HT, 0:T], start=True, stop=False)
                                nc.tensor.matmul(bank[SB][:, HT:T], lhs[:, 1, :], upto[0:HT, 0:HT], start=False,
                                                 stop=True).then_inc(s["k_sum"].sem, 1)
                            if 1 in stages:
                                pe.wait_ge(s["r_exp"].sem, s["r_exp"].at(t - 1))
                                for b in range(2):
                                    mm = nc.tensor.matmul(bank[RB][D * b:D * b + D, 0:T], w_r[:, b, :], st[:, u, b, :],
                                                          start=True, stop=True)
                                mm.then_inc(s["r"].sem, 1)
                            if 2 in stages:
                                pe.wait_ge(s["kv_made"].sem, s["kv_made"].at(t - 1))
                                pe.wait_ge(s["rwkv"].sem, s["rwkv"].at(t - 2))
                                lhs = kv[:, :, :, :].rearrange("p j b d -> p j (b d)")
                                nc.tensor.matmul(bank[WB][:, 0:T], lhs[:, 0, :], decay[:, 0:T], start=True, stop=False)
                                nc.tensor.matmul(bank[WB][:, HT:T], lhs[:, 1, :], decay[:, 0:HT], start=False,
                                                 stop=True).then_inc(s["wkv"].sem, 1)
                            if 3 in stages:
                                pe.wait_ge(s["rwkv"].sem, s["rwkv"].at(t - 2))
                                pe.wait_ge(s["added"].sem, s["added"].at(t - 3))
                                nc.tensor.matmul(bank[OB][:, 0:T], w_o[:, :], rw[:, u, :], start=True, stop=True).then_inc(s["out"].sem, 1)
                        pipelined(pe, TILES, body, 3)

                    @block.scalar
                    def _(act):
                        nc.scalar.preload_act_table_set(EXP_LN)

                        def body(t, u, stages):
                            if 1 in stages:
                                act.wait_ge(s["clipped"].sem, s["clipped"].at(t))
                                act.wait_ge(s["k_sum"].sem, s["k_sum"].at(t - 1))
                                act.wait_ge(s["kv_made"].sem, s["kv_made"].at(t - 1))
                                nc.scalar.activation(kk[:, :, :, :].rearrange("p j b d -> p (j b) d"), kc[:, :, :], ACT.Exp).then_inc(s["k_exp"].sem, 1)
                                act.wait_ge(s["r"].sem, s["r"].at(t))
                                act.wait_ge(s["den"].sem, s["den"].at(t - 1))
                                nc.scalar.activation(er[:, :], bank[RB][:, 0:T], ACT.Exp, scale=-1.0).then_inc(s["r_exp"].sem, 1)
                        pipelined(act, TILES, body, 3)

                    @block.vector
                    def _(dve):
                        dve.wait_ge(zero_set, 1)

                        def body(t, u, stages):
                            if 2 in stages:
                                dve.wait_ge(s["k_exp"].sem, s["k_exp"].at(t - 1))
                                dve.wait_ge(s["wkv"].sem, s["wkv"].at(t - 2))
                                got = bank[KVB[1 - u]][0:HT, :].rearrange("p (n w d) -> p n w d", w=2, d=D)
                                nc.vector.tensor_tensor(kv[:, :, :, :].rearrange("p j b d -> p (j b) d"), got[:, :, 1, :],
                                                        kk[:, :, :, :].rearrange("p j b d -> p (j b) d"), ALU.mult).then_inc(s["kv_made"].sem, 1)
                            if 0 in stages:
                                dve.wait_ge(s["kv"].sem, s["kv"].at(t - 1))
                                dve.wait_ge(s["r"].sem, s["r"].at(t - 1))
                                for b in range(2):
                                    now, before = slice(D * b, D * b + D), slice(D - D * b, 2 * D - D * b)
                                    last = nc.vector.tensor_copy(st[before, 1 - u, b, 1:T], xn[now, bass.ds((t + 1) * T, T - 1)])
                                last.then_inc(s["shifted"].sem, 1)
                            if 1 in stages:
                                got = bank[KVB[u]][0:HT, :].rearrange("p (n w d) -> p n w d", w=2, d=D)
                                dve.wait_ge(s["kv"].sem, s["kv"].at(t))
                                dve.wait_ge(s["k_exp"].sem, s["k_exp"].at(t - 1))
                                nc.vector.tensor_scalar(kc[:, :, :], got[:, :, 0, :], -60.0, 30.0, ALU.max, ALU.min).then_inc(s["clipped"].sem, 1)
                            if 2 in stages:
                                dve.wait_ge(s["r_exp"].sem, s["r_exp"].at(t - 1))
                                dve.wait_ge(s["k_sum"].sem, s["k_sum"].at(t - 1))
                                nc.vector.scalar_tensor_tensor(out=dn[:, :], in0=er[:, :], scalar=1.0, in1=bank[SB][:, 0:T],
                                                               op0=ALU.add, op1=ALU.mult).then_inc(s["den"].sem, 1)
                                dve.wait_ge(s["den"].sem, s["den"].at(t - 1))
                                nc.vector.reciprocal(di[:, :], dn[:, :]).then_inc(s["inv"].sem, 1)
                                dve.wait_ge(s["inv"].sem, s["inv"].at(t - 1))
                                dve.wait_ge(s["wkv"].sem, s["wkv"].at(t - 1))
                                dve.wait_ge(s["out"].sem, s["out"].at(t - 3))
                                nc.vector.tensor_tensor(rw[:, 1 - u, :], bank[WB][:, 0:T], di[:, :], ALU.mult).then_inc(s["rwkv"].sem, 1)
                            if 3 in stages:
                                dve.wait_ge(s["out"].sem, s["out"].at(t - 2))
                                nc.vector.tensor_tensor(resid[:, cols(t - 2)], bank[OB][:, 0:T], resid[:, cols(t - 2)], ALU.add).then_inc(s["added"].sem, 1)
                        pipelined(dve, TILES, body, 3)

        def softmax_attention(y, xx):
            s = signals(fixed=1, proj=3, turned_q=1, part_k=2, k_summed=1, k_made=1, v=1, v_out=1, scores=HQ, maxed=HQ, less_max=HQ,
                        exped=HQ, att=HQ, att_out=HQ, y_half=1, y_out=1, den=1, den_log=1, den_inv=1, y_normed=1,
                        out=1, y_added=1)

            def cols(t):
                return bass.ds(t * T, T)

            with ExitStack() as ctx:
                xs = sbuf(ctx, "s_xs", [128, 2, 2, T], F32R)
                qz = sbuf(ctx, "s_qz", [128, 2, 2, T2])
                k1 = sbuf(ctx, "s_k1", [128, 2, T2])
                kr = sbuf(ctx, "s_kr", [128, T2])
                kz = late[:, 0:4 * T2].rearrange("p (u k t) -> p u k t", u=2, k=2)
                va = sbuf(ctx, "s_va", [HT, 2, 4, 2, 32])
                mx = sbuf(ctx, "s_mx", [HT, HQ, 4])
                pr = sbuf(ctx, "s_pr", [HT, HQ, SCORES])
                at = sbuf(ctx, "s_at", [HT, HQ, 2, T + HT])
                ysb = late[:, 4 * T2:5 * T2]
                di = late[:, 5 * T2:6 * T2]
                SC, ATB, YB, M0, M1, OB = (0, 1), (2, 3), 4, 5, 6, 7
                ones_set = plain("s_ones_set")

                def batches(rows):
                    return rows.rearrange("p (b t) -> p b t", b=2)

                def both(name):
                    return table(name).unsqueeze(1).broadcast_to([128, 2, T])

                def halves(rows):
                    return (rows[:, 0:T].rearrange("p (b s) -> p b s", b=2),
                            rows[:, T:SCORES].rearrange("p (b s) -> p b s", b=2))

                with nc.Block() as block:

                    @block.gpsimd
                    def _(pool):
                        nc.gpsimd.memset(va[:, :, :, :, :], 1.0).then_inc(ones_set, 1)

                        def body(t, u, stages):
                            if 0 in stages:
                                pool.wait_ge(s["v"].sem, s["v"].at(t - 1))
                                nc.gpsimd.tensor_copy(xs[:, 1 - u, :, :], xx[:, :, cols(t + 1)]).then_inc(s["fixed"].sem, 1)
                                pool.wait_ge(s["part_k"].sem, s["part_k"].at(t + 1, 1))
                                pool.wait_ge(s["k_made"].sem, s["k_made"].at(t))
                                nc.gpsimd.tensor_tensor(kr[:, :], k1[:, 0, :], k1[:, 1, :], ALU.add).then_inc(s["k_summed"].sem, 1)
                                pool.wait_ge(s["k_summed"].sem, s["k_summed"].at(t + 1))
                                pool.wait_ge(s["scores"].sem, s["scores"].at(t - 1, HQ - 1))
                                for half in range(2):
                                    last = nc.gpsimd.tensor_tensor(kz[:, 1 - u, half, :], kr[:, :],
                                                                   table("key_half")[:, half:half + 1].broadcast_to([128, T2]), ALU.mult)
                                last.then_inc(s["k_made"].sem, 1)
                        pipelined(pool, TILES, body)

                    @block.tensor
                    def _(pe):
                        def project(t, u, c, to):
                            for part in range(2):
                                mm = nc.tensor.matmul(bank[to][:, 0:T2], w_q[:, part, c, :], xs[:, u, :, :],
                                                      start=(part == 0), stop=(part == 1))
                            mm.then_inc(s["proj"].sem, 1)

                        def scores(t, u, h):
                            if h == 0:
                                pe.wait_ge(s["turned_q"].sem, s["turned_q"].at(t))
                                pe.wait_ge(s["k_made"].sem, s["k_made"].at(t))
                            pe.wait_ge(s["less_max"].sem, s["less_max"].at(t, h - 2))
                            to = bank[SC[h % 2]][0:HT, 0:SCORES]
                            nc.tensor.matmul(to, eye_b[:, :], banned[:, :], start=True, stop=False, skip_group_check=True)
                            for j in range(2):
                                for b in range(2):
                                    w = HT + HT * j
                                    c0 = j * T + b * w
                                    q0 = b * T + j * HT
                                    mm = nc.tensor.matmul(to[:, c0:c0 + w], qz[:, u, h % 2, q0:q0 + HT], kz[:, u, h // 2, b * T:b * T + w],
                                                          start=False, stop=True, skip_group_check=True)
                            mm.then_inc(s["scores"].sem, 1)

                        def turn(t, h):
                            pe.wait_ge(s["exped"].sem, s["exped"].at(t, h))
                            pe.wait_ge(s["att_out"].sem, s["att_out"].at(t, h - 2))
                            for b in range(2):
                                for n, c0 in enumerate((b * HT, T + b * T, T + b * T + HT)):
                                    d0 = b * (T + HT) + n * HT
                                    mm = nc.tensor.transpose(bank[ATB[h % 2]][0:HT, d0:d0 + HT], pr[:, h, c0:c0 + HT],
                                                             table("eye")[0:HT, 0:HT])
                            mm.then_inc(s["att"].sem, 1)

                        def values(t, u):
                            pe.wait_ge(s["att_out"].sem, s["att_out"].at(t, HQ - 1))
                            pe.wait_ge(s["v_out"].sem, s["v_out"].at(t))
                            pe.wait_ge(s["y_out"].sem, s["y_out"].at(t - 1))
                            for b in range(2):
                                for j in range(2):
                                    for h in range(HQ):
                                        mm = nc.tensor.matmul(bank[YB][32 * h:32 * h + 32, b * T + j * HT:b * T + T],
                                                              va[:, u, 2 * b + j, h // 2, :],
                                                              at[:, h, b, j * T:T + j * HT], start=(j == 0), stop=(j == 1))
                            mm.then_inc(s["y_half"].sem, 1)

                        def body(t, u, stages):
                            if 0 in stages:
                                pe.wait_ge(s["fixed"].sem, s["fixed"].at(t + 1))
                                pe.wait_ge(s["part_k"].sem, s["part_k"].at(t, 1))
                                project(t + 1, 1 - u, 0, M0)
                                pe.wait_ge(s["v_out"].sem, s["v_out"].at(t))
                                project(t + 1, 1 - u, 1, M1)
                            if 1 in stages:
                                scores(t, u, 0)
                            if 2 in stages:
                                turn(t - 1, HQ - 1)
                            if 1 in stages:
                                scores(t, u, 1)
                            if 0 in stages:
                                pe.wait_ge(s["turned_q"].sem, s["turned_q"].at(t + 1))
                                project(t + 1, 1 - u, 2, M0)
                            if 2 in stages:
                                values(t - 1, 1 - u)
                            if 0 in stages:
                                pe.wait_ge(s["part_k"].sem, s["part_k"].at(t + 1, 0))
                                for b in range(2):
                                    for j in range(2):
                                        for part in range(2):
                                            n = 2 * b + j
                                            mm = nc.tensor.matmul(bank[M1][0:HT, 32 * n:32 * n + 32], xs[:, 1 - u, b, HT * j:HT * j + HT],
                                                                  w_v[:, part, :], start=(part == 0), stop=(part == 1))
                                mm.then_inc(s["v"].sem, 1)
                            if 1 in stages:
                                scores(t, u, 2)
                                turn(t, 0)
                            if 2 in stages:
                                pe.wait_ge(s["y_out"].sem, s["y_out"].at(t - 1))
                                pe.wait_ge(s["y_added"].sem, s["y_added"].at(t - 2))
                                nc.tensor.matmul(bank[OB][:, 0:T2], table("den_of_head"), ysb, start=True, stop=True).then_inc(s["den"].sem, 1)
                            if 1 in stages:
                                scores(t, u, 3)
                                turn(t, 1)
                                turn(t, 2)
                            if 2 in stages:
                                pe.wait_ge(s["y_normed"].sem, s["y_normed"].at(t - 1))
                                for b in range(2):
                                    mm = nc.tensor.matmul(bank[OB][D * b:D * b + D, 0:T], w_ao[:, :], ysb[:, b * T:b * T + T],
                                                          start=True, stop=True)
                                mm.then_inc(s["out"].sem, 1)
                        pe.wait_ge(ones_set, 1)
                        pipelined(pe, TILES, body)

                    @block.scalar
                    def _(act):
                        nc.scalar.preload_act_table_set(EXP_LN)

                        def exp(t, h):
                            act.wait_ge(s["less_max"].sem, s["less_max"].at(t, h))
                            nc.scalar.activation(pr[:, h, :], pr[:, h, :], ACT.Exp).then_inc(s["exped"].sem, 1)

                        def att_out(t, h):
                            act.wait_ge(s["att"].sem, s["att"].at(t, h))
                            act.wait_ge(s["y_half"].sem, s["y_half"].at(t - 1))
                            nc.scalar.copy(at[:, h, :, :].rearrange("p b s -> p (b s)"), bank[ATB[h % 2]][0:HT, 0:SCORES]).then_inc(s["att_out"].sem, 1)

                        def body(t, u, stages):
                            if 2 in stages:
                                att_out(t - 1, HQ - 1)
                            if 1 in stages:
                                exp(t, 0)
                            if 2 in stages:
                                act.wait_ge(s["y_half"].sem, s["y_half"].at(t - 1))
                                act.wait_ge(s["out"].sem, s["out"].at(t - 2))
                                nc.scalar.copy(ysb, bank[YB][:, 0:T2]).then_inc(s["y_out"].sem, 1)
                            if 1 in stages:
                                exp(t, 1)
                                att_out(t, 0)
                            if 2 in stages:
                                act.wait_ge(s["den"].sem, s["den"].at(t - 1))
                                act.wait_ge(s["y_normed"].sem, s["y_normed"].at(t - 2))
                                nc.scalar.activation(di, bank[OB][:, 0:T2], ACT.Ln).then_inc(s["den_log"].sem, 1)
                                act.wait_ge(s["den_log"].sem, s["den_log"].at(t - 1))
                                nc.scalar.activation(di, di, ACT.Exp, scale=-1.0).then_inc(s["den_inv"].sem, 1)
                            if 1 in stages:
                                exp(t, 2)
                                att_out(t, 1)
                                exp(t, 3)
                                att_out(t, 2)
                        pipelined(act, TILES, body)

                    @block.vector
                    def _(dve):
                        dve.wait_ge(ones_set, 1)

                        def soften(t, h):
                            dve.wait_ge(s["scores"].sem, s["scores"].at(t, h))
                            dve.wait_ge(s["less_max"].sem, s["less_max"].at(t - 1, h))
                            dve.wait_ge(s["att"].sem, s["att"].at(t - 1, h))
                            got = halves(bank[SC[h % 2]][0:HT, 0:SCORES])
                            for j in range(2):
                                last = nc.vector.tensor_reduce(mx[:, h, 2 * j:2 * j + 2], got[j], AX.X, ALU.max)
                            last.then_inc(s["maxed"].sem, 1)
                            dve.wait_ge(s["maxed"].sem, s["maxed"].at(t, h))
                            for j in range(2):
                                w = HT + HT * j
                                last = nc.vector.tensor_tensor(halves(pr[:, h, :])[j], got[j],
                                                               mx[:, h, 2 * j:2 * j + 2].unsqueeze(2).broadcast_to([HT, 2, w]),
                                                               ALU.subtract)
                            last.then_inc(s["less_max"].sem, 1)

                        def body(t, u, stages):
                            if 0 in stages:
                                dve.wait_ge(s["proj"].sem, s["proj"].at(t + 1, 0))
                                dve.wait_ge(s["scores"].sem, s["scores"].at(t - 1, HQ - 1))
                                for n in range(2):
                                    last = nc.vector.tensor_tensor(batches(qz[:, 1 - u, n, :]), batches(bank[M0][:, 0:T2]), both(f"rope_q{n}"), ALU.mult)
                                last.then_inc(s["turned_q"].sem, 1)
                                dve.wait_ge(s["proj"].sem, s["proj"].at(t + 1, 1))
                                dve.wait_ge(s["k_summed"].sem, s["k_summed"].at(t))
                                nc.vector.tensor_tensor(batches(k1[:, 0, :]), batches(bank[M1][:, 0:T2]), both("rope_kc"), ALU.mult).then_inc(s["part_k"].sem, 1)
                            if 1 in stages:
                                soften(t, 0)
                                soften(t, 1)
                            if 0 in stages:
                                dve.wait_ge(s["proj"].sem, s["proj"].at(t + 1, 2))
                                nc.vector.tensor_tensor(batches(k1[:, 1, :]), batches(bank[M0][:, 0:T2]), both("rope_ks"), ALU.mult).then_inc(s["part_k"].sem, 1)
                                dve.wait_ge(s["v"].sem, s["v"].at(t + 1))
                                dve.wait_ge(s["y_half"].sem, s["y_half"].at(t - 1))
                                got = bank[M1][0:HT, 0:128].rearrange("p (n g d) -> p n g d", n=4, g=2)
                                nc.vector.tensor_copy(va[:, 1 - u, :, :, 0:HD], got).then_inc(s["v_out"].sem, 1)
                            if 1 in stages:
                                soften(t, 2)
                            if 2 in stages:
                                dve.wait_ge(s["den_inv"].sem, s["den_inv"].at(t - 1))
                                nc.vector.tensor_tensor(ysb, ysb, di, ALU.mult).then_inc(s["y_normed"].sem, 1)
                            if 1 in stages:
                                soften(t, 3)
                            if 2 in stages:
                                dve.wait_ge(s["out"].sem, s["out"].at(t - 1))
                                nc.vector.tensor_tensor(y[:, cols(t - 1)], bank[OB][:, 0:T], y[:, cols(t - 1)], ALU.add).then_inc(s["y_added"].sem, 1)
                        pipelined(dve, TILES, body)

        PIECES = 8
        parts = sbuf(stack, "parts", [128, 2, COLS], F32R)
        stored = plain("stored")
        if stop >= 1:
            norm_pass("n1", resid, xx=parts)
            linear_attention(parts)
        if stop >= 2:
            with ExitStack() as ctx:
                logits0 = sbuf(ctx, "logits0", [HT, P * 4, E0])
                gates0 = sbuf(ctx, "gates0", [HT, P * 4, 2 * E0], F32R)
                norm_pass("n2", resid, xx=parts, router=1, logits=logits0)
                choose_experts("c0", logits0, E0, gates0)
                experts0(parts, gates0)
        if stop >= 3:
            with ExitStack() as ctx:
                normed2 = sbuf(ctx, "normed2", [128, COLS])
                norm_pass("n3", resid, keep=normed2)
                time_mixing(normed2)
        if stop >= 4:
            with ExitStack() as ctx:
                y = sbuf(ctx, "y", [128, COLS])
                norm_pass("n4", resid, twice=True, keep=y, xx=parts)
                softmax_attention(y, parts)
                norm_pass("n5", y, layer_norm=False, xx=parts, router=2, logits=logits1)
            if stop >= 5:
                with ExitStack() as ctx:
                    gates1 = sbuf(ctx, "gates1", [HT, P * 4, 2 * E1], F32R)
                    weights = (
                        sbuf(ctx, "e_w1", [128, 2, CH1 * 128], F32R),
                        sbuf(ctx, "e_w3", [128, 2, CH1 * 128], F32R),
                        sbuf(ctx, "e_w2", [128, CH1, D]),
                    )
                    choose_experts("c1", logits1, E1, gates1, weights)
                    experts1(parts, gates1, weights)


def layouts(v):
    import numpy as np

    c = np.ascontiguousarray
    x, txt = v["x"], v["txt"]
    B = x.shape[0]
    out = {
        "x": c(x[:, 0].transpose(1, 0, 2)),
        "txt": c(txt.reshape(B // 2, 2, TXT, D).transpose(1, 3, 0, 2).reshape(128, B // 2, TXT)),
        "const": CONSTS,
        "wtok": c(v["L0_tok_weight"].reshape(PH, PW, D)),
        "btok": v["L0_tok_bias"].reshape(D, 1),
    }
    keys = v["L0_attn_Wks"].transpose(1, 0, 2).reshape(D, H0 * K0)
    queries = v["L0_attn_Wqs"].transpose(1, 0, 2).reshape(D, H0 * K0)
    out["wkq"] = c(np.concatenate([keys, queries], 1))
    out["wvt"] = c(v["L0_attn_Wvs"].transpose(2, 0, 1))
    out["wo0"] = c(v["L0_attn_Wo"].transpose(1, 0, 2))
    out["rw1"] = v["L0_ffn_router_w1"]
    out["rb1"] = v["L0_ffn_router_b1"].reshape(RH0, 1)
    out["rw2"] = v["L0_ffn_router_w2"]
    out["rb2"] = v["L0_ffn_router_b2"].reshape(1, E0)
    out["ew1"] = c(v["L0_ffn_expert_w1"].transpose(1, 0, 2).reshape(D, E0 * EH0))
    out["eb1"] = c(v["L0_ffn_expert_b1"].reshape(3, 128).T)
    out["ew2"] = v["L0_ffn_expert_w2"]
    out["eb2"] = c(v["L0_ffn_expert_b2"].reshape(3, 128).T)
    out["ew3"] = c(v["L0_ffn_expert_w3"].reshape(3, 128, D).transpose(1, 0, 2))
    out["eb3"] = v["L0_ffn_expert_b3"]
    out["wkvr"] = c(np.stack([v["L1_attn_Wk"], v["L1_attn_Wv"], v["L1_attn_Wr"]], 1))
    out["mix"] = c(np.stack([v[f"L1_attn_time_mix_{n}"].reshape(D) for n in "kvr"], 1))
    out["wo1"] = v["L1_attn_Wo"]
    time_w = v["L1_attn_time_w"]
    u, t = np.arange(HT)[:, None], np.arange(T)[None, :]
    out["decay"] = c(time_w[np.clip(time_w.shape[0] - 1 - (t - u), 0, time_w.shape[0] - 1)])
    out["ln1"] = v["L1_ffn_ln1_w"].reshape(D, 1)
    out["ln2"] = v["L1_ffn_ln2_w"].reshape(D, 1)
    swap = (np.arange(HD) + HD // 2) % HD
    q = v["L1_ffn_wq"].reshape(HQ, HD, D)
    k = v["L1_ffn_wk"].reshape(2, HD, D)[np.arange(HQ) // 2]
    q = np.concatenate([q, q[:, swap]], 1)
    k1, k2 = np.concatenate([k, k], 1), np.concatenate([k[:, swap], k[:, swap]], 1)
    out["wq"] = c(np.stack([a.reshape(128, D).T for a in (q, k1, k2)], 1))
    out["wv"] = c(v["L1_ffn_wv"].T)
    out["wao"] = c(v["L1_ffn_wo"].T)
    out["rt"] = c(v["L1_ffn_router_w"].T)
    out["w1"] = c(v["L1_ffn_w1"].reshape(E1 * HID, D).T)
    out["w3"] = c(v["L1_ffn_w3"].reshape(E1 * HID, D).T)
    out["w2"] = c(v["L1_ffn_w2"].transpose(0, 2, 1).reshape(E1 * HID, D))
    return out


def kernel(**inputs):
    import numpy as np
    import concourse.bacc as bacc
    from concourse.bass_utils import run_bass_kernel_spmd

    arrays = layouts({k: np.asarray(a) for k, a in inputs.items()})
    B = inputs["x"].shape[0]
    nc = bacc.Bacc("TRN2", target_bir_lowering=False, num_devices=1)
    ap = {k: nc.dram_tensor(f"in_{k}", a.shape, mybir.dt.from_np(a.dtype), kind="ExternalInput").ap()
          for k, a in arrays.items()}
    out = nc.dram_tensor("out_h", [128, B // 2 * T], F32, kind="ExternalOutput").ap()
    build(nc, ap, out)
    run = run_bass_kernel_spmd(nc, [{f"in_{k}": a for k, a in arrays.items()}], core_ids=[0])
    got = run.results[0]["out_h"]
    return np.ascontiguousarray(got.reshape(2, D, B // 2, T).transpose(2, 0, 3, 1).reshape(B, T, D))
```
